# Optimizing a Trainium2 kernel written in Bass

```python
import numpy as np
import jax
import jax.numpy as jnp

def _softmax(x, axis=-1):
    return jax.nn.softmax(x, axis=axis)

def _gelu(x):
    return jax.nn.gelu(x, approximate=True)

def _silu(x):
    return jax.nn.silu(x)

def _sigmoid(x):
    return jax.nn.sigmoid(x)

def _layernorm(x, axis=-1, eps=1e-05):
    m = jnp.mean(x, axis=axis, keepdims=True)
    v = jnp.var(x, axis=axis, keepdims=True)
    return (x - m) / jnp.sqrt(v + eps)

def _scatter_add(tgt, idx, src, axis=0):
    return tgt.at[idx].add(src)

def _segment_sum(src, seg, n):
    return jax.ops.segment_sum(src, seg, n)
kernel_name = 'mk_decoder_preln_d2_seqx_r8_81a32a'

def setup_inputs(seed: int=0):
    np.random.seed(seed)
    _w = jnp.asarray

    def _rec_inputs():
        import jax
        import jax.numpy as jnp
        _rk = jax.random.key(seed)
        x = 7.22e-05 + 1 * jax.random.normal(jax.random.fold_in(_rk, 1), (4, 512, 128), jnp.float32)
        _lenS = 512 - jax.random.randint(jax.random.fold_in(_rk, 7), (4,), 0, max(1, 512 // 4) + 1, jnp.int32)
        _lenS2 = 77 - jax.random.randint(jax.random.fold_in(_rk, 8), (4,), 0, max(1, 77 // 4) + 1, jnp.int32)
        _ctx_1024P = jax.random.normal(jax.random.fold_in(_rk, 11), (4, 16, 128), jnp.float32)
        _ctx_1024c = jax.random.dirichlet(jax.random.fold_in(_rk, 511), 0.3 * jnp.ones((16,), jnp.float32), (4, 77))
        _ctx_1024t = jnp.einsum('bsk,bkd->bsd', _ctx_1024c, _ctx_1024P)
        _ctx_1024t = _ctx_1024t * jax.lax.rsqrt(jnp.mean(jnp.square(_ctx_1024t)) + 1e-12) * 0.953939
        ctx_1024 = 4.13588e-05 + 0.999923 * (_ctx_1024t + 0.3 * jax.random.normal(jax.random.fold_in(_rk, 611), (4, 77, 128), jnp.float32))
        return (x, ctx_1024)
    x, ctx_1024 = _rec_inputs()

    def _L0_attn_setup():
        import jax, jax.numpy as jnp
        import numpy as np
        B, S, D, H, DH, FF = (2, 512, 128, 16, 64, 512)

        def _ln(x, g, b):
            m = x.mean(-1, keepdims=True)
            v = ((x - m) ** 2).mean(-1, keepdims=True)
            return (x - m) * jax.lax.rsqrt(v + 1e-05) * g + b

        def _phi(x, proj):
            return jax.nn.elu(x @ proj) + 1.0
        key = jax.random.key(seed)
        ks = jax.random.split(key, 10)
        s = 0.02
        return {'x': jax.random.normal(ks[0], (B, S, D), jnp.float32), 'wq': jax.random.normal(ks[1], (D, H * DH), jnp.float32) * s, 'wk': jax.random.normal(ks[2], (D, H * DH), jnp.float32) * s, 'wv': jax.random.normal(ks[3], (D, H * DH), jnp.float32) * s, 'wo': jax.random.normal(ks[4], (H * DH, D), jnp.float32) * s, 'proj': jax.random.normal(ks[5], (DH, DH), jnp.float32) / np.sqrt(DH).astype(np.float32), 'w1': jax.random.normal(ks[6], (D, FF), jnp.float32) * s, 'b1': jnp.zeros((FF,), jnp.float32), 'w2': jax.random.normal(ks[7], (FF, D), jnp.float32) * s, 'b2': jnp.zeros((D,), jnp.float32), 'g1': jnp.ones((D,), jnp.float32), 'beta1': jnp.zeros((D,), jnp.float32), 'g2': jnp.ones((D,), jnp.float32), 'beta2': jnp.zeros((D,), jnp.float32)}
    _L0_attn_all = _L0_attn_setup()
    _L0_attn_in = {k: v for k, v in _L0_attn_all.items() if k in ('wq', 'wk', 'wv', 'wo', 'proj', 'w1', 'b1', 'w2', 'b2', 'g1', 'beta1', 'g2', 'beta2')}
    del _L0_attn_all

    def _L0_xattn_setup():
        import jax, jax.numpy as jnp
        import numpy as np
        B, S, D = (4, 256, 128)
        D_K, D_V = (128, 128)
        key = jax.random.key(seed)
        ks = jax.random.split(key, 9)
        s = 1.0 / np.sqrt(D)
        return {'q_in': jax.random.normal(ks[0], (B, S, D), jnp.float32), 'k_in': jax.random.normal(ks[1], (B, S, D), jnp.float32), 'v_in': jax.random.normal(ks[2], (B, S, D), jnp.float32), 'Wq': jax.random.normal(ks[3], (D, D_K), jnp.float32) * s, 'bq': jnp.zeros((D_K,), jnp.float32), 'Wk': jax.random.normal(ks[4], (D, D_K), jnp.float32) * s, 'bk': jnp.zeros((D_K,), jnp.float32), 'Wv': jax.random.normal(ks[5], (D, D_V), jnp.float32) * s, 'bv': jnp.zeros((D_V,), jnp.float32)}
    _L0_xattn_all = _L0_xattn_setup()
    _L0_xattn_in = {k: v for k, v in _L0_xattn_all.items() if k in ('Wq', 'bq', 'Wk', 'bk', 'Wv', 'bv')}
    del _L0_xattn_all

    def _L0_ffn_setup():
        import jax, jax.numpy as jnp
        import numpy as np
        D_MODEL, D_FF, N_EXPERTS, TOP_K = (128, 512, 8, 2)
        B, S = (4, 256)

        def _moe_forward(x, W1, b1, W2, b2, Wg, bg):
            b, s, d = x.shape
            xt = x.reshape(-1, d)
            T = xt.shape[0]
            router_logits = xt @ Wg + bg
            routing_weights = jax.nn.softmax(router_logits, axis=1)
            topk_w, topk_idx = jax.lax.top_k(routing_weights, TOP_K)
            topk_w = topk_w / jnp.sum(topk_w, axis=1, keepdims=True)
            combine = jnp.zeros((T, N_EXPERTS), dtype=xt.dtype)
            combine = combine.at[jnp.arange(T)[:, None], topk_idx].add(topk_w)
            out = jnp.zeros_like(xt)
            for e in range(N_EXPERTS):
                h = jax.nn.relu(xt @ W1[e] + b1[e])
                y = h @ W2[e] + b2[e]
                out = out + combine[:, e:e + 1] * y
            return out.reshape(b, s, d)
        key = jax.random.key(seed)
        ks = jax.random.split(key, 7)
        scale = 0.02
        x = jax.random.normal(ks[0], (B, S, D_MODEL), dtype=jnp.float32)
        W1 = jax.random.normal(ks[1], (N_EXPERTS, D_MODEL, D_FF), dtype=jnp.float32) * scale
        b1 = jnp.zeros((N_EXPERTS, D_FF), dtype=jnp.float32)
        W2 = jax.random.normal(ks[2], (N_EXPERTS, D_FF, D_MODEL), dtype=jnp.float32) * scale
        b2 = jnp.zeros((N_EXPERTS, D_MODEL), dtype=jnp.float32)
        Wg = jax.random.normal(ks[3], (D_MODEL, N_EXPERTS), dtype=jnp.float32) * scale
        bg = jnp.zeros((N_EXPERTS,), dtype=jnp.float32)
        return {'x': x, 'W1': W1, 'b1': b1, 'W2': W2, 'b2': b2, 'Wg': Wg, 'bg': bg}
    _L0_ffn_all = _L0_ffn_setup()
    _L0_ffn_in = {k: v for k, v in _L0_ffn_all.items() if k in ('W1', 'b1', 'W2', 'b2', 'Wg', 'bg')}
    del _L0_ffn_all

    def _L1_attn_setup():
        import jax, jax.numpy as jnp
        import numpy as np
        D_MODEL, D_STATE, D_CONV, D_INNER = (128, 16, 4, 256)
        BATCH, SEQ = (4, 256)

        def silu(v):
            return v * jax.nn.sigmoid(v)
        key = jax.random.key(seed)
        ks = jax.random.split(key, 7)
        x = jax.random.normal(ks[0], (BATCH, SEQ, D_MODEL), dtype=jnp.float32)
        s = 0.02
        W_in = jax.random.normal(ks[1], (D_MODEL, 2 * D_INNER), dtype=jnp.float32) * s
        conv_w = jax.random.normal(ks[2], (D_INNER, 1, D_CONV), dtype=jnp.float32) * s
        conv_b = jax.random.normal(ks[3], (D_INNER,), dtype=jnp.float32) * s
        W_xproj = jax.random.normal(ks[4], (D_INNER, 2 * D_STATE + 1), dtype=jnp.float32) * s
        A_log = jnp.log(jnp.tile(jnp.arange(1, D_STATE + 1, dtype=jnp.float32), (D_INNER, 1)))
        D = jnp.ones((D_INNER,), dtype=jnp.float32)
        W_out = jax.random.normal(ks[5], (D_INNER, D_MODEL), dtype=jnp.float32) * s
        return {'x': x, 'W_in': W_in, 'conv_w': conv_w, 'conv_b': conv_b, 'W_xproj': W_xproj, 'A_log': A_log, 'D': D, 'W_out': W_out}
    _L1_attn_all = _L1_attn_setup()
    _L1_attn_in = {k: v for k, v in _L1_attn_all.items() if k in ('W_in', 'conv_w', 'conv_b', 'W_xproj', 'A_log', 'D', 'W_out')}
    del _L1_attn_all

    def _L1_xattn_setup():
        import jax, jax.numpy as jnp
        import numpy as np
        DIM = 128
        key = jax.random.key(seed)
        k1, k2, k3, k4, k5 = jax.random.split(key, 5)
        B, Sq, Skv = (8, 256, 256)
        x = jax.random.normal(k1, (B, Sq, DIM), dtype=jnp.float32)
        context = jax.random.normal(k2, (B, Skv, DIM), dtype=jnp.float32)
        s = DIM ** (-0.5)
        Wq = jax.random.normal(k3, (DIM, DIM), dtype=jnp.float32) * s
        Wk = jax.random.normal(k4, (DIM, DIM), dtype=jnp.float32) * s
        Wv = jax.random.normal(k5, (DIM, DIM), dtype=jnp.float32) * s
        return {'x': x, 'context': context, 'Wq': Wq, 'Wk': Wk, 'Wv': Wv}
    _L1_xattn_all = _L1_xattn_setup()
    _L1_xattn_in = {k: v for k, v in _L1_xattn_all.items() if k in ('Wq', 'Wk', 'Wv')}
    del _L1_xattn_all

    def _L1_ffn_setup():
        import math
        import jax, jax.numpy as jnp
        import numpy as np
        E = 24

        def layer_norm(x, w, b, eps=1e-06):
            m = x.mean(-1, keepdims=True)
            v = x.var(-1, keepdims=True)
            return (x - m) / jnp.sqrt(v + eps) * w + b

        def top2_dispatch(x, Wg, C):
            logits = x @ Wg
            gates = jax.nn.softmax(logits, axis=-1)
            idx1 = jnp.argmax(gates, axis=-1)
            m1 = jax.nn.one_hot(idx1, E, dtype=x.dtype)
            masked = jnp.where(m1 > 0, -jnp.inf, logits)
            idx2 = jnp.argmax(masked, axis=-1)
            m2 = jax.nn.one_hot(idx2, E, dtype=x.dtype)
            loc1 = jnp.cumsum(m1, axis=0) - m1
            loc2 = jnp.cumsum(m2, axis=0) - m2 + jnp.sum(m1, axis=0, keepdims=True)
            m1 = m1 * (loc1 < C)
            m2 = m2 * (loc2 < C)
            g1 = jnp.sum(gates * m1, axis=-1)
            g2 = jnp.sum(gates * m2, axis=-1)
            denom = jnp.maximum(g1 + g2, 1e-09)
            g1, g2 = (g1 / denom, g2 / denom)
            p1 = jnp.sum(loc1 * m1, axis=-1).astype(jnp.int32)
            p2 = jnp.sum(loc2 * m2, axis=-1).astype(jnp.int32)
            c1 = g1[:, None, None] * m1[:, :, None] * jax.nn.one_hot(p1, C, dtype=x.dtype)[:, None, :]
            c2 = g2[:, None, None] * m2[:, :, None] * jax.nn.one_hot(p2, C, dtype=x.dtype)[:, None, :]
            combine = c1 + c2
            dispatch = (combine > 0).astype(x.dtype)
            return (combine, dispatch)

        def moe_apply(x, combine, dispatch, W, b):
            disp = jnp.einsum('sec,sd->ecd', dispatch, x)
            h = jnp.einsum('ecd,edf->ecf', disp, W) + b[:, None, :]
            return jnp.einsum('sec,ecf->sf', combine, h)
        b, seq, d_in, d_hid = (4, 256, 128, 512)
        ks = jax.random.split(jax.random.key(seed), 6)
        s = 0.02
        return {'x': jax.random.normal(ks[0], (b, seq, d_in), dtype=jnp.float32), 'Wg': jax.random.normal(ks[1], (d_in, E), dtype=jnp.float32) * s, 'W1': jax.random.normal(ks[2], (E, d_in, d_hid), dtype=jnp.float32) * s, 'b1': jnp.zeros((E, d_hid), dtype=jnp.float32), 'W2': jax.random.normal(ks[3], (E, d_hid, d_in), dtype=jnp.float32) * s, 'b2': jnp.zeros((E, d_in), dtype=jnp.float32), 'ln_hid_w': jnp.ones((4, d_hid), dtype=jnp.float32), 'ln_hid_b': jnp.zeros((4, d_hid), dtype=jnp.float32), 'ln_out_w': jnp.ones((d_in,), dtype=jnp.float32), 'ln_out_b': jnp.zeros((d_in,), dtype=jnp.float32)}
    _L1_ffn_all = _L1_ffn_setup()
    _L1_ffn_in = {k: v for k, v in _L1_ffn_all.items() if k in ('Wg', 'W1', 'b1', 'W2', 'b2', 'ln_hid_w', 'ln_hid_b', 'ln_out_w', 'ln_out_b')}
    del _L1_ffn_all
    return {'x': x, 'ctx_1024': ctx_1024, 'L0_attn_wq': _L0_attn_in['wq'], 'L0_attn_wk': _L0_attn_in['wk'], 'L0_attn_wv': _L0_attn_in['wv'], 'L0_attn_wo': _L0_attn_in['wo'], 'L0_attn_proj': _L0_attn_in['proj'], 'L0_attn_w1': _L0_attn_in['w1'], 'L0_attn_b1': _L0_attn_in['b1'], 'L0_attn_w2': _L0_attn_in['w2'], 'L0_attn_b2': _L0_attn_in['b2'], 'L0_attn_g1': _L0_attn_in['g1'], 'L0_attn_beta1': _L0_attn_in['beta1'], 'L0_attn_g2': _L0_attn_in['g2'], 'L0_attn_beta2': _L0_attn_in['beta2'], 'L0_xattn_Wq': _L0_xattn_in['Wq'], 'L0_xattn_bq': _L0_xattn_in['bq'], 'L0_xattn_Wk': _L0_xattn_in['Wk'], 'L0_xattn_bk': _L0_xattn_in['bk'], 'L0_xattn_Wv': _L0_xattn_in['Wv'], 'L0_xattn_bv': _L0_xattn_in['bv'], 'L0_ffn_W1': _L0_ffn_in['W1'], 'L0_ffn_b1': _L0_ffn_in['b1'], 'L0_ffn_W2': _L0_ffn_in['W2'], 'L0_ffn_b2': _L0_ffn_in['b2'], 'L0_ffn_Wg': _L0_ffn_in['Wg'], 'L0_ffn_bg': _L0_ffn_in['bg'], 'L1_attn_W_in': _L1_attn_in['W_in'], 'L1_attn_conv_w': _L1_attn_in['conv_w'], 'L1_attn_conv_b': _L1_attn_in['conv_b'], 'L1_attn_W_xproj': _L1_attn_in['W_xproj'], 'L1_attn_A_log': _L1_attn_in['A_log'], 'L1_attn_D': _L1_attn_in['D'], 'L1_attn_W_out': _L1_attn_in['W_out'], 'L1_xattn_Wq': _L1_xattn_in['Wq'], 'L1_xattn_Wk': _L1_xattn_in['Wk'], 'L1_xattn_Wv': _L1_xattn_in['Wv'], 'L1_ffn_Wg': _L1_ffn_in['Wg'], 'L1_ffn_W1': _L1_ffn_in['W1'], 'L1_ffn_b1': _L1_ffn_in['b1'], 'L1_ffn_W2': _L1_ffn_in['W2'], 'L1_ffn_b2': _L1_ffn_in['b2'], 'L1_ffn_ln_hid_w': _L1_ffn_in['ln_hid_w'], 'L1_ffn_ln_hid_b': _L1_ffn_in['ln_hid_b'], 'L1_ffn_ln_out_w': _L1_ffn_in['ln_out_w'], 'L1_ffn_ln_out_b': _L1_ffn_in['ln_out_b']}

def reference(x, ctx_1024, L0_attn_wq, L0_attn_wk, L0_attn_wv, L0_attn_wo, L0_attn_proj, L0_attn_w1, L0_attn_b1, L0_attn_w2, L0_attn_b2, L0_attn_g1, L0_attn_beta1, L0_attn_g2, L0_attn_beta2, L0_xattn_Wq, L0_xattn_bq, L0_xattn_Wk, L0_xattn_bk, L0_xattn_Wv, L0_xattn_bv, L0_ffn_W1, L0_ffn_b1, L0_ffn_W2, L0_ffn_b2, L0_ffn_Wg, L0_ffn_bg, L1_attn_W_in, L1_attn_conv_w, L1_attn_conv_b, L1_attn_W_xproj, L1_attn_A_log, L1_attn_D, L1_attn_W_out, L1_xattn_Wq, L1_xattn_Wk, L1_xattn_Wv, L1_ffn_Wg, L1_ffn_W1, L1_ffn_b1, L1_ffn_W2, L1_ffn_b2, L1_ffn_ln_hid_w, L1_ffn_ln_hid_b, L1_ffn_ln_out_w, L1_ffn_ln_out_b):
    import jax
    import jax.numpy as jnp

    def _L0_attn_ref(x, wq, wk, wv, wo, proj, w1, b1, w2, b2, g1, beta1, g2, beta2):
        import jax, jax.numpy as jnp
        import numpy as np
        B, S, D, H, DH, FF = (2, 512, 128, 16, 64, 512)

        def _ln(x, g, b):
            m = x.mean(-1, keepdims=True)
            v = ((x - m) ** 2).mean(-1, keepdims=True)
            return (x - m) * jax.lax.rsqrt(v + 1e-05) * g + b

        def _phi(x, proj):
            return jax.nn.elu(x @ proj) + 1.0
        b, s, d = x.shape
        h = _ln(x, g1, beta1)
        q = _phi((h @ wq).reshape(b, s, H, DH), proj)
        k = _phi((h @ wk).reshape(b, s, H, DH), proj)
        v = (h @ wv).reshape(b, s, H, DH)
        qs = jnp.moveaxis(q, 1, 0)
        ks_ = jnp.moveaxis(k, 1, 0)
        vs = jnp.moveaxis(v, 1, 0)

        def step(carry, qkv_t):
            kv, ksum = carry
            q_t, k_t, v_t = qkv_t
            kv = kv + k_t[..., :, None] * v_t[..., None, :]
            ksum = ksum + k_t
            num = jnp.einsum('bhd,bhde->bhe', q_t, kv)
            den = jnp.einsum('bhd,bhd->bh', q_t, ksum) + 1e-06
            return ((kv, ksum), num / den[..., None])
        kv0 = jnp.zeros((b, H, DH, DH), x.dtype)
        ks0 = jnp.zeros((b, H, DH), x.dtype)
        _, outs = jax.lax.scan(step, (kv0, ks0), (qs, ks_, vs))
        attn = jnp.moveaxis(outs, 0, 1).reshape(b, s, H * DH) @ wo
        x = x + attn
        h2 = _ln(x, g2, beta2)
        x = x + (jax.nn.gelu(h2 @ w1 + b1, approximate=False) @ w2 + b2)
        return x

    def _L0_xattn_ref(q_in, k_in, v_in, Wq, bq, Wk, bk, Wv, bv):
        import jax, jax.numpy as jnp
        import numpy as np
        B, S, D = (4, 256, 128)
        D_K, D_V = (128, 128)
        q = jnp.einsum('bsd,dk->bsk', q_in, Wq) + bq
        k = jnp.einsum('bsd,dk->bsk', k_in, Wk) + bk
        v = jnp.einsum('bsd,dv->bsv', v_in, Wv) + bv
        scores = jnp.einsum('bqk,bsk->bqs', q, k) / jnp.sqrt(jnp.float32(D_K))
        attn = jax.nn.softmax(scores, axis=-1)
        return jnp.einsum('bqs,bsv->bqv', attn, v)

    def _L0_ffn_ref(x, W1, b1, W2, b2, Wg, bg):
        import jax, jax.numpy as jnp
        import numpy as np
        D_MODEL, D_FF, N_EXPERTS, TOP_K = (128, 512, 8, 2)
        B, S = (4, 256)

        def _moe_forward(x, W1, b1, W2, b2, Wg, bg):
            b, s, d = x.shape
            xt = x.reshape(-1, d)
            T = xt.shape[0]
            router_logits = xt @ Wg + bg
            routing_weights = jax.nn.softmax(router_logits, axis=1)
            topk_w, topk_idx = jax.lax.top_k(routing_weights, TOP_K)
            topk_w = topk_w / jnp.sum(topk_w, axis=1, keepdims=True)
            combine = jnp.zeros((T, N_EXPERTS), dtype=xt.dtype)
            combine = combine.at[jnp.arange(T)[:, None], topk_idx].add(topk_w)
            out = jnp.zeros_like(xt)
            for e in range(N_EXPERTS):
                h = jax.nn.relu(xt @ W1[e] + b1[e])
                y = h @ W2[e] + b2[e]
                out = out + combine[:, e:e + 1] * y
            return out.reshape(b, s, d)
        return _moe_forward(x, W1, b1, W2, b2, Wg, bg)

    def _L1_attn_ref(x, W_in, conv_w, conv_b, W_xproj, A_log, D, W_out):
        import jax, jax.numpy as jnp
        import numpy as np
        D_MODEL, D_STATE, D_CONV, D_INNER = (128, 16, 4, 256)
        BATCH, SEQ = (4, 256)

        def silu(v):
            return v * jax.nn.sigmoid(v)
        B, L, _ = x.shape
        xz = x @ W_in
        x_proj, z = jnp.split(xz, 2, axis=-1)
        xc = jax.lax.conv_general_dilated(x_proj.transpose(0, 2, 1), conv_w, window_strides=(1,), padding=[(D_CONV - 1, 0)], feature_group_count=D_INNER, dimension_numbers=('NCH', 'OIH', 'NCH'))
        x_conv = silu((xc + conv_b[None, :, None]).transpose(0, 2, 1))
        ssm = x_conv @ W_xproj
        delta = jax.nn.softplus(ssm[..., 0])
        Bm = ssm[..., 1:1 + D_STATE]
        Cm = ssm[..., 1 + D_STATE:]
        deltaB = delta[..., None] * Bm
        h_mean = jnp.einsum('bld,bln->bdn', x_conv, deltaB) / L
        y = jnp.einsum('bdn,bln->bld', h_mean, Cm)
        y = y + D[None, None, :] * x_conv
        y = y * silu(z)
        return y @ W_out

    def _L1_xattn_ref(x, context, Wq, Wk, Wv):
        import jax, jax.numpy as jnp
        import numpy as np
        DIM = 128
        q = jnp.einsum('bsd,ed->bse', x, Wq)
        k = jnp.einsum('btd,ed->bte', context, Wk)
        v = jnp.einsum('btd,ed->bte', context, Wv)
        scale = Wq.shape[0] ** (-0.5)
        dots = jnp.einsum('bse,bte->bst', q, k) * scale
        attn = jax.nn.softmax(dots, axis=-1)
        out = jnp.einsum('bst,bte->bse', attn, v)
        return out

    def _L1_ffn_ref(x, Wg, W1, b1, W2, b2, ln_hid_w, ln_hid_b, ln_out_w, ln_out_b):
        import math
        import jax, jax.numpy as jnp
        import numpy as np
        E = 24

        def layer_norm(x, w, b, eps=1e-06):
            m = x.mean(-1, keepdims=True)
            v = x.var(-1, keepdims=True)
            return (x - m) / jnp.sqrt(v + eps) * w + b

        def top2_dispatch(x, Wg, C):
            logits = x @ Wg
            gates = jax.nn.softmax(logits, axis=-1)
            idx1 = jnp.argmax(gates, axis=-1)
            m1 = jax.nn.one_hot(idx1, E, dtype=x.dtype)
            masked = jnp.where(m1 > 0, -jnp.inf, logits)
            idx2 = jnp.argmax(masked, axis=-1)
            m2 = jax.nn.one_hot(idx2, E, dtype=x.dtype)
            loc1 = jnp.cumsum(m1, axis=0) - m1
            loc2 = jnp.cumsum(m2, axis=0) - m2 + jnp.sum(m1, axis=0, keepdims=True)
            m1 = m1 * (loc1 < C)
            m2 = m2 * (loc2 < C)
            g1 = jnp.sum(gates * m1, axis=-1)
            g2 = jnp.sum(gates * m2, axis=-1)
            denom = jnp.maximum(g1 + g2, 1e-09)
            g1, g2 = (g1 / denom, g2 / denom)
            p1 = jnp.sum(loc1 * m1, axis=-1).astype(jnp.int32)
            p2 = jnp.sum(loc2 * m2, axis=-1).astype(jnp.int32)
            c1 = g1[:, None, None] * m1[:, :, None] * jax.nn.one_hot(p1, C, dtype=x.dtype)[:, None, :]
            c2 = g2[:, None, None] * m2[:, :, None] * jax.nn.one_hot(p2, C, dtype=x.dtype)[:, None, :]
            combine = c1 + c2
            dispatch = (combine > 0).astype(x.dtype)
            return (combine, dispatch)

        def moe_apply(x, combine, dispatch, W, b):
            disp = jnp.einsum('sec,sd->ecd', dispatch, x)
            h = jnp.einsum('ecd,edf->ecf', disp, W) + b[:, None, :]
            return jnp.einsum('sec,ecf->sf', combine, h)
        bsz, seq, d = x.shape
        H = 4
        n = seq // H
        S = bsz * n
        C = math.ceil(2 * S / E)
        xg = x.reshape(bsz, H, n, d).transpose(1, 0, 2, 3).reshape(H, S, d)

        def per_group(xf, lw, lb):
            combine, dispatch = top2_dispatch(xf, Wg, C)
            h = moe_apply(xf, combine, dispatch, W1, b1)
            h = layer_norm(h, lw, lb)
            h = jax.nn.relu(h)
            return moe_apply(h, combine, dispatch, W2, b2)
        out = jax.vmap(per_group)(xg, ln_hid_w, ln_hid_b)
        out = out.reshape(H, bsz, n, d).transpose(1, 0, 2, 3).reshape(bsz, seq, d)
        return layer_norm(out + x, ln_out_w, ln_out_b)
    x = x + _L0_attn_ref(_layernorm(x, axis=-1), L0_attn_wq, L0_attn_wk, L0_attn_wv, L0_attn_wo, L0_attn_proj, L0_attn_w1, L0_attn_b1, L0_attn_w2, L0_attn_b2, L0_attn_g1, L0_attn_beta1, L0_attn_g2, L0_attn_beta2)
    x = x + _L0_xattn_ref(_layernorm(x, axis=-1), ctx_1024, ctx_1024, L0_xattn_Wq, L0_xattn_bq, L0_xattn_Wk, L0_xattn_bk, L0_xattn_Wv, L0_xattn_bv)
    x = x + _L0_ffn_ref(_layernorm(x, axis=-1), L0_ffn_W1, L0_ffn_b1, L0_ffn_W2, L0_ffn_b2, L0_ffn_Wg, L0_ffn_bg)
    x = x + _L1_attn_ref(_layernorm(x, axis=-1), L1_attn_W_in, L1_attn_conv_w, L1_attn_conv_b, L1_attn_W_xproj, L1_attn_A_log, L1_attn_D, L1_attn_W_out)
    x = x + _L1_xattn_ref(_layernorm(x, axis=-1), ctx_1024, L1_xattn_Wq, L1_xattn_Wk, L1_xattn_Wv)
    x = x + _L1_ffn_ref(_layernorm(x, axis=-1), L1_ffn_Wg, L1_ffn_W1, L1_ffn_b1, L1_ffn_W2, L1_ffn_b2, L1_ffn_ln_hid_w, L1_ffn_ln_hid_b, L1_ffn_ln_out_w, L1_ffn_ln_out_b)
    return x

_drawn_inputs = setup_inputs


def setup_inputs(seed=0):
    import zlib

    import numpy as np

    out = dict(_drawn_inputs(seed))
    spreads = {'L0_attn_b1': (0.0, 0.341),
     'L0_attn_b2': (0.0, 0.1),
     'L0_attn_g1': (1.0, 0.6),
     'L0_attn_beta1': (0.0, 0.465),
     'L0_attn_g2': (1.0, 0.6),
     'L0_attn_beta2': (0.0, 0.712),
     'L0_xattn_bq': (0.0, 0.316),
     'L0_xattn_bk': (0.0, 2.0),
     'L0_xattn_bv': (0.0, 0.1),
     'L0_ffn_b1': (0.0, 0.38),
     'L0_ffn_b2': (0.0, 0.1),
     'L0_ffn_bg': (0.0, 0.1),
     'L1_attn_D': (1.0, 0.6),
     'L1_ffn_b1': (0.0, 0.1),
     'L1_ffn_b2': (0.0, 0.325),
     'L1_ffn_ln_hid_w': (1.0, 0.6),
     'L1_ffn_ln_hid_b': (0.0, 0.8),
     'L1_ffn_ln_out_w': (1.0, 0.2),
     'L1_ffn_ln_out_b': (0.0, 0.278)}
    factors = {'L0_attn_wq': 8.0,
     'L0_attn_wk': 8.0,
     'L0_attn_wv': 3.004,
     'L0_attn_wo': 3.139,
     'L0_attn_proj': 8.0,
     'L1_attn_W_in': 8.0,
     'L1_attn_conv_w': 8.0,
     'L1_attn_conv_b': 8.0,
     'L1_attn_W_xproj': 8.0,
     'L1_attn_W_out': 8.0}
    for name, (base, spread) in spreads.items():
        noise = np.random.default_rng([zlib.crc32(name.encode()), seed]).standard_normal(out[name].shape)
        drawn = base * np.exp(spread * noise) if base else spread * noise
        out[name] = jnp.asarray(drawn.astype(out[name].dtype))
    for name, factor in factors.items():
        out[name] = (out[name] * factor).astype(out[name].dtype)
    return out
```

```python
from contextlib import ExitStack

import concourse.bass as bass
from concourse import mybir

F32 = mybir.dt.float32
BF16 = mybir.dt.bfloat16
I32 = mybir.dt.int32
ALU = mybir.AluOpType
ACT = mybir.ActivationFunctionType
AX = mybir.AxisListType

P = 128


def decoder(nc, a, out, stop=None):
    B, S, D = a["x"].shape
    T = S // P
    H, DH = 16, 64
    NPAIR = H * DH // P
    FF = a["L0_attn_w1"].shape[1]
    FC = FF // P
    SK = a["ctx_1024"].shape[1]
    E0 = a["L0_ffn_W1"].shape[0]
    DI = a["L1_attn_conv_w"].shape[0]
    IC = DI // P
    KC = a["L1_attn_conv_w"].shape[2]
    NS = a["L1_attn_A_log"].shape[1]
    NX = 2 * NS + 1
    E1 = a["L1_ffn_W1"].shape[0]
    V1 = DH + 1
    SCALE0 = float(D) ** -0.5
    BIG = 3.0e38
    assert D == P and T == 4 and FC == 4 and NPAIR == 8 and S == 512

    with ExitStack() as ctx:
        def sb(name, shape, dt=F32, at=ctx):
            return at.enter_context(nc.sbuf_tensor(name, shape, dt))

        def sem(name):
            return ctx.enter_context(nc.semaphore(name))

        bank = [ctx.enter_context(nc.psum_tensor(f"bank{i}", [P, 512], F32)) for i in range(8)]

        x_all = sb("x_all", [P, B * T, D])
        u_all = sb("u_all", [P, B * T, D])
        ident = sb("ident", [P, P])
        NROWS = 78
        rows = sb("rows", [NROWS, P])
        cols = sb("cols", [P, NROWS])
        tick = sb("tick", [P, 2])
        half = sb("half", [P, T])
        R_AB1, R_EB1, R_G1, R_BE1, R_G2, R_BE2, R_BQ, R_BK, R_CB, R_DS, R_LW, R_LB = (
            0, 4, 36, 37, 38, 39, 40, 41, 42, 44, 46, 62)

        NR = 8
        ring = sb("ring", [P, NR, FF])
        slot_in = [sem(f"slot_in{k}") for k in range(NR)]

        ph = ctx.enter_context(ExitStack())

        def s1(name, shape, dt=F32):
            return sb(name, shape, dt, ph)

        wqk = s1("wqk", [P, 2, H * DH])
        wv = s1("wv", [P, H * DH])
        wo = s1("wo", [P, NPAIR, D])
        w1 = s1("w1", [P, FF])
        w2 = s1("w2", [P, FC, D])
        projd = s1("projd", [P, P])
        b2bc = s1("b2bc", [P, D])
        wx = s1("wx", [P, 6, D])
        bvbc = s1("bvbc", [SK, D])
        e0w1 = s1("e0w1", [P, E0, FF])
        e0w2 = s1("e0w2", [P, E0, FC, D])
        e0b2 = s1("e0b2", [E0, D])
        e0wg = s1("e0wg", [P, E0])
        e0bg = s1("e0bg", [P, E0])
        win = s1("win", [P, 2 * DI])
        wxp = s1("wxp", [P, IC, NX])
        wout = s1("wout", [P, IC, D])
        convw = s1("convw", [P, IC, KC])
        mask = s1("mask", [P, 3 * P])
        ones_row = s1("ones_row", [1, P])
        iota8i = s1("iota8i", [P, T, E0], I32)
        iota8 = s1("iota8", [P, T, E0])
        ctx_in = s1("ctx_in", [SK, B, D])
        ctxT = s1("ctxT", [P, B * SK])
        kxT = s1("kxT", [P, 2, B * SK])
        sxA = s1("sxA", [P, 2, B * SK])
        sx0 = s1("sx0", [1, B * SK])
        vx = s1("vx", [SK, 2, B, D])
        wxT = s1("wxT", [P, 3, D])
        x_in = s1("x_in", [P, T, D])
        st = s1("st", [P, T, 6])
        mv = s1("mv", [P, T, 2])
        ve = s1("ve", [P, T])
        rs = s1("rs", [P, T])
        r2 = s1("r2", [P, T])
        xn = s1("xn", [P, T, D])
        xh = s1("xh", [P, T, D])
        xs = s1("xs", [P, T, D])
        xr = s1("xr", [P, T, D])
        hT = s1("hT", [P, S])
        v_tm = s1("v_tm", [P, T, H, V1])
        eb = s1("eb", [P, 2, S])
        rb = s1("rb", [P, 2, S])
        qT = s1("qT", [P, 2, S])
        kT = s1("kT", [P, 2, S])
        ktm = s1("ktm", [P, 2, P])
        kv = s1("kv", [P, 2 * V1])
        stm = s1("stm", [P, 2, 2, 3 * P])
        dn = s1("dn", [P, T])
        rd = s1("rd", [P, T])
        atm = s1("atm", [P, 2, T, P])
        big = s1("big", [P, 8, S])
        pd = s1("pd", [P, T, SK])
        pp = s1("pp", [P, T, SK])
        mx = s1("mx", [P, T])
        sm = s1("sm", [P, T])
        ri = s1("ri", [P, T])
        pT = s1("pT", [SK, S])
        lg = s1("lg", [P, T, E0])
        oh1 = s1("oh1", [P, T, E0])
        oh2 = s1("oh2", [P, T, E0])
        key = s1("key", [P, T, E0])
        l2 = s1("l2", [P, T, E0])
        m1 = s1("m1", [P, T])
        m2 = s1("m2", [P, T])
        mn = s1("mn", [P, T])
        g1 = s1("g1", [P, T])
        g2 = s1("g2", [P, T])
        comb = s1("comb", [P, T, E0])
        combT = s1("combT", [E0, S])
        xpad = s1("xpad", [P, IC, S + KC - 1])
        cv = eb
        xc = rb
        sz = qT
        xcT = s1("xcT", [P, T, DI])
        ssm = s1("ssm", [P, T, NX])
        sp_x = s1("sp_x", [P, 8, T])
        dB = s1("dB", [P, T, NS])
        hmT = s1("hmT", [NS, DI])
        cT = s1("cT", [NS, S])
        yT = kT

        w_in = sem("w_in")
        x_loaded = sem("x_loaded")
        consts = sem("consts")
        pre_pe = sem("pre_pe")
        pre_act = sem("pre_act")
        vec = sem("vec")
        out_done = sem("out_done")
        names = ("var_ready rstd_ready ln_ready lnT_done hT_ready v_done v_act v_dve qk_done phi_parts phi_ready "
                 "kt_done ktm_ready state_done state_ready scores_done st_ready apply_done attn_evac atT_done atT_evac "
                 "y_done ff_done ff_ready sc_done sd_ready p_ready pT_done pT_ready lg_done comb_ready combT_done "
                 "combT_ready up_done up_act up_dve acc_done xz_done xp_ready cv_ready xc_ready sz_ready ssm_done ct_done "
                 "xcT_done xcT_ready ct_ready ssm_ready abs_ready u_ready w_ready l_ready db_ready hm_done hm_ready yt_done "
                 "yt_ready xs_ready xa_ready x_free md_ready me_ready x_kept neg_ready").split()
        s = {n: sem(n) for n in names}
        (var_ready, rstd_ready, ln_ready, lnT_done, hT_ready, v_done, v_act, v_dve, qk_done, phi_parts, phi_ready,
         kt_done, ktm_ready, state_done, state_ready, scores_done, st_ready, apply_done, attn_evac, atT_done, atT_evac,
         y_done, ff_done, ff_ready, sc_done, sd_ready, p_ready, pT_done, pT_ready, lg_done, comb_ready, combT_done,
         combT_ready, up_done, up_act, up_dve, acc_done, xz_done, xp_ready, cv_ready, xc_ready, sz_ready, ssm_done,
         ct_done, xcT_done, xcT_ready, ct_ready, ssm_ready, abs_ready, u_ready, w_ready, l_ready, db_ready, hm_done,
         hm_ready, yt_done, yt_ready, xs_ready, xa_ready, x_free, md_ready, me_ready, x_kept, neg_ready) = [s[n] for n in names]

        VEC_PRE, VEC_STEPS = 2, 95
        N_LN, N_LN_ALL, N_POW, N_Y = 6, 7, 8, 14
        LN_ATT, LN_FFN, LN_X0, LN_MOE, LN_SSM, LN_X1 = range(6)

        Y_WO, Y_FFN, Y_X0, Y_BIAS, Y_E, Y_SSM, Y_X1 = 0, 1, 2, 3, 4, 4 + E0, 5 + E0
        W_DMAS = 38

        block = ph.enter_context(nc.Block())

        @block.sync
        def _(sp):
            n = [0]

            def load(dst, src):
                sp.dma_start(dst, src).then_inc(w_in, 16)
                n[0] += 1

            def vec_rows(r, v):
                k = v.shape[0] // P
                load(rows[r:r + k, :], v.rearrange("(c p) -> c p", p=P))

            sp.dma_start(x_in[:], a["x"][0].rearrange("(t p) d -> p t d", p=P)).then_inc(x_loaded, 16)
            load(wqk[:, 0, :], a["L0_attn_wq"])
            load(wqk[:, 1, :], a["L0_attn_wk"])
            load(wv[:], a["L0_attn_wv"])
            sp.wait_ge(consts, 3)
            load(projd[0:DH, 0:DH], a["L0_attn_proj"])
            load(projd[DH:P, DH:P], a["L0_attn_proj"])
            vec_rows(R_AB1, a["L0_attn_b1"])
            load(rows[R_EB1:R_EB1 + E0 * FC, :], a["L0_ffn_b1"].rearrange("e (c p) -> (e c) p", p=P))
            vec_rows(R_G1, a["L0_attn_g1"])
            vec_rows(R_BE1, a["L0_attn_beta1"])
            vec_rows(R_G2, a["L0_attn_g2"])
            vec_rows(R_BE2, a["L0_attn_beta2"])
            vec_rows(R_BQ, a["L0_xattn_bq"])
            vec_rows(R_BK, a["L0_xattn_bk"])
            vec_rows(R_CB, a["L1_attn_conv_b"])
            vec_rows(R_DS, a["L1_attn_D"])
            load(rows[R_LW:R_LW + 16, :], a["L1_ffn_ln_hid_w"].rearrange("g (c p) -> (g c) p", p=P))
            load(rows[R_LB:R_LB + 16, :], a["L1_ffn_ln_hid_b"].rearrange("g (c p) -> (g c) p", p=P))
            load(ctx_in[:], a["ctx_1024"].rearrange("b k d -> k b d"))
            for i, name in enumerate(("L0_xattn_Wq", "L0_xattn_Wk", "L0_xattn_Wv",
                                      "L1_xattn_Wq", "L1_xattn_Wk", "L1_xattn_Wv")):
                load(wx[:, i, :], a[name])
            load(bvbc[:], a["L0_xattn_bv"].rearrange("(o d) -> o d", o=1).to_broadcast([SK, D]))
            load(b2bc[:], a["L0_attn_b2"].rearrange("(o d) -> o d", o=1).to_broadcast([P, D]))
            load(wo[:], a["L0_attn_wo"].rearrange("(j p) n -> p j n", p=P))
            load(w1[:], a["L0_attn_w1"])
            load(w2[:], a["L0_attn_w2"].rearrange("(c p) n -> p c n", p=P))
            load(e0w1[:], a["L0_ffn_W1"].rearrange("e d f -> d e f"))
            load(e0w2[:], a["L0_ffn_W2"].rearrange("e (c p) d -> p e c d", p=P))
            load(e0b2[:], a["L0_ffn_b2"])
            load(e0wg[:], a["L0_ffn_Wg"])
            load(e0bg[:], a["L0_ffn_bg"].rearrange("(o d) -> o d", o=1).to_broadcast([P, E0]))
            load(win[:], a["L1_attn_W_in"])
            load(wxp[:], a["L1_attn_W_xproj"].rearrange("(c p) n -> p c n", p=P))
            load(wout[:], a["L1_attn_W_out"].rearrange("(c p) n -> p c n", p=P))
            load(convw[:], a["L1_attn_conv_w"].rearrange("(c p) o k -> p c (o k)", p=P))
            assert n[0] == W_DMAS
            for k in range(NR):
                sp.dma_start(ring[:, k, :], a["L1_ffn_W1"][k]).then_inc(slot_in[k], 16)
            with sp.Fori(1, B) as b:
                sp.wait_ge(x_free, b)
                src = a["x"].rearrange("b (t p) d -> p b t d", p=P)[:, bass.ds(b, 1), :, :]
                sp.dma_start(x_in[:], src.rearrange("p b t d -> p (b t) d")).then_inc(x_loaded, 16)

        @block.gpsimd
        def _(pool):
            nc.gpsimd.memset(ident[:], 0.0).then_inc(consts, 1)
            nc.gpsimd.memset(mask[:], 1.0).then_inc(consts, 1)
            nc.gpsimd.memset(projd[:], 0.0).then_inc(consts, 1)
            pool.wait_ge(consts, 3)
            nc.gpsimd.affine_select(out=ident[:], in_=ident[:], compare_op=ALU.not_equal, fill=1.0, base=0,
                                    pattern=[[-1, P]], channel_multiplier=1)
            for c in (0, 2):
                nc.gpsimd.affine_select(out=mask[:, c * P:(c + 1) * P], in_=mask[:, c * P:(c + 1) * P],
                                        compare_op=ALU.is_ge, fill=0.0, base=0, pattern=[[1, P]],
                                        channel_multiplier=-1)
            nc.gpsimd.iota(iota8i[:], pattern=[[0, T], [1, E0]], base=0, channel_multiplier=0)
            nc.gpsimd.memset(ones_row[:], 1.0)
            nc.gpsimd.memset(half[:], -0.5)
            nc.gpsimd.memset(v_tm[:, :, :, DH:V1], 1.0)
            nc.gpsimd.memset(xpad[:, :, 0:KC - 1], 0.0).then_inc(consts, 1)
            pool.wait_ge(consts, 4)
            pool.wait_ge(w_in, 16 * W_DMAS)
            with pool.Fori(0, B) as b:
                def inverse_root(k, dst):
                    pool.wait_ge(var_ready, b * N_POW + (k + 1))
                    nc.gpsimd.tensor_tensor(dst[:], ve[:], half[:], ALU.pow).then_inc(rstd_ready, 1)

                pool.wait_ge(x_loaded, b * 16 + 16)
                nc.gpsimd.tensor_tensor(xs[:], x_in[:], b2bc[:].unsqueeze(1).to_broadcast([P, T, D]),
                                        ALU.add).then_inc(xs_ready, 1)
                inverse_root(0, rs)
                inverse_root(1, r2)
                pool.wait_ge(xa_ready, b + 1)
                pool.wait_ge(xs_ready, b * 2 + 1)
                nc.gpsimd.tensor_tensor(xs[:], xs[:], xn[:], ALU.add).then_inc(xs_ready, 1)
                for k in range(2, N_POW):
                    inverse_root(k, rs)

        @block.tensor
        def _(pe):
            mm, tr = nc.tensor.matmul, nc.tensor.transpose
            pe.wait_ge(w_in, 16 * W_DMAS)
            pe.wait_ge(consts, 4)
            tr(bank[7][:, 0:NROWS], rows[:], ident[0:NROWS, 0:NROWS]).then_inc(pre_pe, 1)
            for g in range(4):
                w, j0 = g // 2, 4 * (g % 2)
                for j in range(4):
                    l = tr(bank[g][:, j * P:(j + 1) * P], wqk[:, w, (j0 + j) * P:(j0 + j + 1) * P], ident[:])
                l.then_inc(pre_pe, 1)
            for g in range(4):
                pe.wait_ge(pre_act, 2 + g if g < 2 else 4 + g)
                for j in range(4):
                    l = mm(bank[4 + g % 2][:, j * P:(j + 1) * P], big[:, g, j * P:(j + 1) * P], projd[:],
                           start=True, stop=True)
                l.then_inc(pre_pe, 1)
            for b in range(B):
                l = tr(bank[0][:, b * SK:(b + 1) * SK], ctx_in[:, b, :], ident[0:SK, 0:SK])
            l.then_inc(pre_pe, 1)
            for i, w in enumerate((0, 4, 5)):
                l = tr(bank[1][:, i * P:(i + 1) * P], wx[:, w, :], ident[:])
            l.then_inc(pre_pe, 1)
            pe.wait_ge(pre_act, 11)
            mm(bank[2][:, 0:B * SK], wx[:, 1, :], ctxT[:], start=True, stop=True)
            mm(bank[3][:, 0:B * SK], wxT[:, 1, :], ctxT[:], start=True, stop=True).then_inc(pre_pe, 1)
            for i, w in enumerate((wx[:, 2, :], wxT[:, 2, :])):
                for b in range(B):
                    l = mm(bank[6 + i][0:SK, b * P:(b + 1) * P], ctxT[:, b * SK:(b + 1) * SK], w,
                           start=True, stop=True)
            l.then_inc(pre_pe, 1)
            pe.wait_ge(pre_act, 13)
            mm(bank[0][:, 0:B * SK], wxT[:, 0, :], kxT[:, 0, :], start=True, stop=True)
            mm(bank[1][:, 0:B * SK], wx[:, 3, :], kxT[:, 1, :], start=True, stop=True)
            mm(bank[2][0:1, 0:B * SK], cols[:, R_BQ:R_BQ + 1], kxT[:, 0, :], start=True, stop=True).then_inc(pre_pe, 1)
            pe.wait_ge(pre_act, 17)
            pe.wait_ge(vec, VEC_PRE)

            with pe.Fori(0, B) as b:
                ps_q, ps_k, ps_s, ps_o, ps_x, ps_t = bank[0], bank[1], bank[2:4], bank[4:6], bank[6], bank[7]
                four = (*ps_s, *ps_o)

                def to_features(k):
                    pe.wait_ge(ln_ready, b * N_LN_ALL + (k + 1))
                    for t in range(T):
                        l = tr(ps_t[:, t * P:(t + 1) * P], xh[:, t, :], ident[:])
                    l.then_inc(lnT_done, 1)
                    pe.wait_ge(hT_ready, b * N_LN + (k + 1))

                to_features(LN_ATT)
                for n in range(2 * T):
                    t, h = n // 2, n % 2
                    if n >= 4:
                        pe.wait_ge((v_act, v_dve)[n % 2], b * T + (n - 4) // 2 + 1)
                    mm(four[n % 4][:], hT[:, t * P:(t + 1) * P], wv[:, h * 512:(h + 1) * 512],
                       start=True, stop=True).then_inc(v_done, 1)

                def project(w, j):
                    if j:
                        pe.wait_ge(phi_ready, b * 2 * NPAIR + (2 * j - 1 + w))
                    mm((ps_q, ps_k)[w][:], wqk[:, w, j * P:(j + 1) * P], hT[:], start=True, stop=True)\
                        .then_inc(qk_done, 1)

                def scores(j, hh):
                    i, h0 = 2 * j + hh, hh * DH
                    r = slice(h0, h0 + DH)
                    if i == 0:
                        pe.wait_ge(v_act, b * T + T)
                        pe.wait_ge(v_dve, b * T + T)
                    else:
                        pe.wait_ge(st_ready, b * 2 * H + 2 * i)
                    pe.wait_ge(phi_ready, b * 2 * NPAIR + 2 * j + 2)
                    for c in range(2):
                        t0 = 2 * c * P
                        mm(ps_s[c][:, 0:2 * P], kT[r, j % 2, t0:t0 + P], qT[r, j % 2, t0:t0 + 2 * P],
                           start=True, stop=True)
                        mm(ps_s[c][:, 2 * P:3 * P], kT[r, j % 2, t0 + P:t0 + 2 * P],
                           qT[r, j % 2, t0 + P:t0 + 2 * P], start=True, stop=True).then_inc(scores_done, 1)

                def keys_to_tokens(j):
                    if j:
                        pe.wait_ge(state_ready, b * NPAIR + j)
                    for t in range(2):
                        l = tr(ps_x[:, t * P:(t + 1) * P], kT[:, j % 2, t * P:(t + 1) * P], ident[:])
                    l.then_inc(kt_done, 1)

                def state(j):
                    pe.wait_ge(ktm_ready, b * NPAIR + j + 1)
                    for t in range(2):
                        l = mm(ps_x[:, 2 * P:2 * P + 2 * V1], ktm[:, t, :],
                               v_tm[:, t, 2 * j:2 * j + 2, :].rearrange("p h v -> p (h v)"),
                               start=(t == 0), stop=(t == 1))
                    l.then_inc(state_done, 1)

                def apply(j, hh):
                    i, h = 2 * j + hh, 2 * j + hh
                    r = slice(hh * DH, hh * DH + DH)
                    pe.wait_ge(st_ready, b * 2 * H + 2 * i + 2)
                    if hh == 0:
                        pe.wait_ge(state_ready, b * NPAIR + j + 1)
                    if j:
                        pe.wait_ge(attn_evac, b * H + i - 1)
                    for c in range(2):
                        for tt in range(2):
                            o = ps_o[hh][:, (2 * c + tt) * V1:(2 * c + tt + 1) * V1]
                            w = stm[:, i % 2, c, :]
                            l = mm(o, w[:, tt * P:(tt + 1) * P], v_tm[:, 2 * c, h, :],
                                   start=True, stop=(c == 0 and tt == 0))
                            if tt:
                                l = mm(o, w[:, 2 * P:3 * P], v_tm[:, 2 * c + 1, h, :], start=False, stop=(c == 0))
                            if c:
                                q0 = (2 * c + tt) * P
                                l = mm(o, qT[r, j % 2, q0:q0 + P], kv[r, hh * V1:(hh + 1) * V1],
                                       start=False, stop=True)
                    l.then_inc(apply_done, 1)

                def attn_to_features(j):
                    pe.wait_ge(attn_evac, b * 2 * NPAIR + 2 * j + 2)
                    if j:
                        pe.wait_ge(atT_evac, b * NPAIR + j)
                    for t in range(T):
                        l = tr(ps_t[:, t * P:(t + 1) * P], atm[:, j % 2, t, :], ident[:])
                    l.then_inc(atT_done, 1)

                project(0, 0)
                project(1, 0)
                for j in range(NPAIR):
                    scores(j, 0)
                    keys_to_tokens(j)
                    if j + 1 < NPAIR:
                        project(0, j + 1)
                    scores(j, 1)
                    if j:
                        attn_to_features(j - 1)
                    state(j)
                    if j + 1 < NPAIR:
                        project(1, j + 1)
                    apply(j, 0)
                    apply(j, 1)
                attn_to_features(NPAIR - 1)

                def down(dst, hid, w, n):
                    for t in range(T):
                        for c in range(n):
                            l = mm(dst[:, t * P:(t + 1) * P], hid[:, c, t * P:(t + 1) * P], w[:, c, :],
                                   start=(c == 0), stop=(c == n - 1))
                    l.then_inc(y_done, 1)

                pe.wait_ge(atT_evac, b * NPAIR + NPAIR)
                down(ps_q, big, wo, NPAIR)

                to_features(LN_FFN)
                for c in range(FC):
                    mm(four[c][:], w1[:, c * P:(c + 1) * P], hT[:], start=True, stop=True).then_inc(ff_done, 1)
                pe.wait_ge(ff_ready, b * FC + FC)
                down(ps_k, big, w2, FC)

                def cross(i):
                    to_features((LN_X0, LN_X1)[i])
                    keys = sxA[:, i, :].rearrange("p (b k) -> p b k", b=B)[:, bass.ds(b, 1), :]\
                        .rearrange("p b k -> p (b k)")
                    for t in range(T):
                        o = ps_s[0][:, t * SK:(t + 1) * SK]
                        l = mm(o, hT[:, t * P:(t + 1) * P], keys, start=True, stop=(i == 1))
                        if i == 0:
                            l = mm(o, ones_row[:], sx0[:].rearrange("p (b k) -> p b k", b=B)[:, bass.ds(b, 1), :]
                                   .rearrange("p b k -> p (b k)"), start=False, stop=True)
                    l.then_inc(sc_done, 1)
                    pe.wait_ge(p_ready, b * 2 + (i + 1))
                    for t in range(T):
                        l = tr(ps_t[0:SK, t * P:(t + 1) * P], pp[:, t, :], ident[:])
                    l.then_inc(pT_done, 1)
                    pe.wait_ge(pT_ready, b * 2 + (i + 1))
                    vals = vx[:, i, bass.ds(b, 1), :].rearrange("p b k -> p (b k)")
                    for t in range(T):
                        l = mm(ps_q[:, t * P:(t + 1) * P], pT[:, t * P:(t + 1) * P], vals, start=True, stop=True)
                    l.then_inc(y_done, 1)

                cross(0)

                to_features(LN_MOE)
                for t in range(T):
                    l = mm(ps_s[1][:, t * E0:(t + 1) * E0], hT[:, t * P:(t + 1) * P], e0wg[:], start=True, stop=True)
                l.then_inc(lg_done, 1)

                def up(e):
                    for c in range(FC):
                        if e:
                            pe.wait_ge((up_act, up_dve)[c % 2], b * 2 * E0 + 2 * (e - 1) + c // 2 + 1)
                        mm(four[(c + 2) % 4][:], e0w1[:, e, c * P:(c + 1) * P], hT[:], start=True, stop=True)\
                            .then_inc(up_done, 1)

                pe.wait_ge(comb_ready, b + 1)
                for t in range(T):
                    l = tr(ps_t[0:E0, t * P:(t + 1) * P], comb[:, t, :], ident[:])
                l.then_inc(combT_done, 1)
                up(0)
                pe.wait_ge(combT_ready, b + 1)
                for t in range(T):
                    l = mm(ps_q[:, t * P:(t + 1) * P], combT[:, t * P:(t + 1) * P], e0b2[:], start=True, stop=True)
                l.then_inc(y_done, 1)
                for e in range(E0):
                    if e + 1 < E0:
                        up(e + 1)
                    pe.wait_ge(up_act, b * 2 * E0 + 2 * e + 2)
                    pe.wait_ge(up_dve, b * 2 * E0 + 2 * e + 2)
                    if e:
                        pe.wait_ge(acc_done, b * E0 + e)
                    down((ps_k, ps_q)[e % 2], big[:, 4 * (e % 2):4 * (e % 2) + 4, :], e0w2[:, e], FC)

                to_features(LN_SSM)
                for c in range(4):
                    mm(four[c][:], win[:, c * P:(c + 1) * P], hT[:], start=True, stop=True).then_inc(xz_done, 1)
                pe.wait_ge(xc_ready, b * IC + IC)
                for t in range(T):
                    for c in range(IC):
                        l = mm(ps_x[:, t * NX:(t + 1) * NX], xc[:, c, t * P:(t + 1) * P], wxp[:, c, :],
                               start=(c == 0), stop=(c == IC - 1))
                l.then_inc(ssm_done, 1)
                for c in range(IC):
                    for t in range(T):
                        l = tr((ps_t, ps_q)[c][:, t * P:(t + 1) * P], xc[:, c, t * P:(t + 1) * P], ident[:])
                l.then_inc(xcT_done, 1)
                for c in range(IC):
                    l = mm(ps_k[0:NS, :], wxp[:, c, 1 + NS:NX], xc[:, c, :], start=(c == 0), stop=(c == IC - 1))
                l.then_inc(ct_done, 1)
                pe.wait_ge(db_ready, b + 1)
                pe.wait_ge(xcT_ready, b * IC + IC)
                for t in range(T):
                    l = mm(ps_s[0][0:NS, 0:DI], dB[:, t, :], xcT[:, t, :], start=(t == 0), stop=(t == T - 1))
                l.then_inc(hm_done, 1)
                pe.wait_ge(ct_ready, b + 1)
                pe.wait_ge(hm_ready, b + 1)
                pe.wait_ge(sz_ready, b * IC + IC)
                for c in range(IC):
                    mm(ps_o[c][:], hmT[:, c * P:(c + 1) * P], cT[:], start=True, stop=True).then_inc(yt_done, 1)
                pe.wait_ge(yt_ready, b * IC + IC)
                down(ps_q, yT, wout, IC)

                cross(1)

        @block.scalar
        def _(act):
            af = nc.scalar.activation
            n = [0]

            def pre(ins):
                n[0] += 1
                ins.then_inc(pre_act, 1)

            act.wait_ge(pre_pe, 1)
            pre(af(cols[:], bank[7][:, 0:NROWS], ACT.Copy))
            for g in range(4):
                act.wait_ge(pre_pe, 2 + g)
                pre(af(big[:, g, :], bank[g][:], ACT.Copy))
            for g in range(4):
                act.wait_ge(pre_pe, 6 + g)
                pre(af(wqk[:, g // 2, (g % 2) * 512:(g % 2) * 512 + 512], bank[4 + g % 2][:], ACT.Copy))
            act.wait_ge(pre_pe, 10)
            pre(af(ctxT[:], bank[0][:, 0:B * SK], ACT.Copy))
            act.wait_ge(pre_pe, 11)
            pre(af(wxT[:].rearrange("p a d -> p (a d)"), bank[1][:, 0:3 * D], ACT.Copy))
            act.wait_ge(pre_pe, 12)
            act.wait_ge(pre_act, 1)
            pre(af(kxT[:, 0, :], bank[2][:, 0:B * SK], ACT.Identity, bias=cols[:, R_BK:R_BK + 1]))
            pre(af(kxT[:, 1, :], bank[3][:, 0:B * SK], ACT.Copy))
            act.wait_ge(pre_pe, 13)
            pre(af(vx[:, 1, :, :].rearrange("p b d -> p (b d)"), bank[7][0:SK, :], ACT.Copy))
            act.wait_ge(pre_pe, 14)
            pre(af(sxA[:, 0, :], bank[0][:, 0:B * SK], ACT.Copy))
            pre(af(sxA[:, 1, :], bank[1][:, 0:B * SK], ACT.Copy))
            pre(af(sx0[:], bank[2][0:1, 0:B * SK], ACT.Copy))
            assert n[0] == 17

            with act.Fori(0, B) as b:
                ps_q, ps_k, ps_s, ps_o, ps_x, ps_t = bank[0], bank[1], bank[2:4], bank[4:6], bank[6], bank[7]
                four = (*ps_s, *ps_o)

                def features(k, g=None, be=None):
                    act.wait_ge(lnT_done, b * N_LN + (k + 1))
                    if g is None:
                        af(hT[:], ps_t[:], ACT.Copy).then_inc(hT_ready, 1)
                    else:
                        af(hT[:], ps_t[:], ACT.Identity, scale=cols[:, g:g + 1], bias=cols[:, be:be + 1])\
                            .then_inc(hT_ready, 1)

                features(LN_ATT, R_G1, R_BE1)
                for t in range(T):
                    act.wait_ge(v_done, b * 2 * T + 2 * t + 1)
                    af(v_tm[:, t, 0:H // 2, 0:DH], four[2 * t % 4][:].rearrange("p (h d) -> p h d", d=DH),
                       ACT.Copy).then_inc(v_act, 1)

                def parts(w, j):
                    m = 2 * j + w
                    act.wait_ge(qk_done, b * 2 * NPAIR + m + 1)
                    if m >= 2:
                        act.wait_ge(phi_ready, b * 2 * NPAIR + m - 1)
                    af(rb[:, m % 2, :], (ps_q, ps_k)[w][:], ACT.Relu, scale=-1.0).then_inc(neg_ready, 1)
                    act.wait_ge(neg_ready, b * 2 * NPAIR + m + 1)
                    af(eb[:, m % 2, :], rb[:, m % 2, :], ACT.Exp, scale=-1.0).then_inc(phi_parts, 1)

                parts(0, 0)
                parts(1, 0)
                for j in range(NPAIR):
                    act.wait_ge(kt_done, b * NPAIR + j + 1)
                    af(ktm[:], ps_x[:, 0:2 * P].rearrange("p (t d) -> p t d", t=2), ACT.Copy).then_inc(ktm_ready, 1)
                    if j + 1 < NPAIR:
                        parts(0, j + 1)
                    if j:
                        act.wait_ge(atT_done, b * NPAIR + j)
                        af(big[:, j - 1, :], ps_t[:], ACT.Copy).then_inc(atT_evac, 1)
                    act.wait_ge(state_done, b * NPAIR + j + 1)
                    if j:
                        act.wait_ge(apply_done, b * H + 2 * j)
                    af(kv[:], ps_x[:, 2 * P:2 * P + 2 * V1], ACT.Copy).then_inc(state_ready, 1)
                    if j + 1 < NPAIR:
                        parts(1, j + 1)
                act.wait_ge(atT_done, b * NPAIR + NPAIR)
                af(big[:, NPAIR - 1, :], ps_t[:], ACT.Copy).then_inc(atT_evac, 1)

                features(LN_FFN, R_G2, R_BE2)
                for c in range(FC):
                    act.wait_ge(ff_done, b * FC + c + 1)
                    af(big[:, c, :], four[c][:], ACT.Gelu, bias=cols[:, R_AB1 + c:R_AB1 + c + 1]).then_inc(ff_ready, 1)

                def cross(i):
                    features((LN_X0, LN_X1)[i])
                    act.wait_ge(sd_ready, b * 2 + (i + 1))
                    af(pp[:], pd[:], ACT.Exp, scale=SCALE0).then_inc(p_ready, 1)
                    act.wait_ge(pT_done, b * 2 + (i + 1))
                    af(pT[:], ps_t[0:SK, :], ACT.Copy).then_inc(pT_ready, 1)

                cross(0)
                features(LN_MOE)
                act.wait_ge(md_ready, b + 1)
                af(g2[:], mn[:], ACT.Exp).then_inc(me_ready, 1)
                act.wait_ge(combT_done, b + 1)
                af(combT[:], ps_t[0:E0, :], ACT.Copy).then_inc(combT_ready, 1)
                for e in range(E0):
                    for c in (0, 2):
                        act.wait_ge(up_done, b * FC * E0 + FC * e + c + 1)
                        if e >= 2:
                            act.wait_ge(y_done, b * N_Y + Y_E + e - 1)
                        r = R_EB1 + FC * e + c
                        af(big[:, 4 * (e % 2) + c, :], four[(c + 2) % 4][:], ACT.Relu, bias=cols[:, r:r + 1])\
                            .then_inc(up_act, 1)

                features(LN_SSM)
                for c in range(IC):
                    act.wait_ge(xz_done, b * 4 + c + 1)
                    af(xpad[:, c, KC - 1:], four[c][:], ACT.Copy).then_inc(xp_ready, 1)
                for c in range(IC):
                    act.wait_ge(xz_done, b * 4 + IC + c + 1)
                    af(sz[:, c, :], four[IC + c][:], ACT.Silu).then_inc(sz_ready, 1)
                for c in range(IC):
                    act.wait_ge(cv_ready, b * IC + c + 1)
                    af(xc[:, c, :], cv[:, c, :], ACT.Silu).then_inc(xc_ready, 1)
                act.wait_ge(xcT_done, b + 1)
                for c in range(IC):
                    af(xcT[:, :, c * P:(c + 1) * P], (ps_t, ps_q)[c][:].rearrange("p (t d) -> p t d", t=T),
                       ACT.Copy).then_inc(xcT_ready, 1)
                act.wait_ge(ct_done, b + 1)
                af(cT[:], ps_k[0:NS, :], ACT.Copy).then_inc(ct_ready, 1)
                act.wait_ge(abs_ready, b + 1)
                af(sp_x[:, 2, :], sp_x[:, 1, :], ACT.Exp).then_inc(u_ready, 1)
                act.wait_ge(w_ready, b + 1)
                af(sp_x[:, 4, :], sp_x[:, 3, :], ACT.Ln).then_inc(l_ready, 1)
                act.wait_ge(hm_done, b + 1)
                af(hmT[:], ps_s[0][0:NS, 0:DI], ACT.Copy).then_inc(hm_ready, 1)

                cross(1)
                act.wait_ge(ln_ready, b * N_LN_ALL + N_LN_ALL)
                af(x_all[:, bass.ds(b * T, T), :], xr[:], ACT.Copy)
                af(u_all[:, bass.ds(b * T, T), :], xh[:], ACT.Copy).then_inc(x_kept, 1)

        @block.vector
        def _(dve):
            v = nc.vector
            n = [0]

            dve.wait_ge(consts, 4)
            v.tensor_copy(iota8[:], iota8i[:]).then_inc(vec, 1)
            dve.wait_ge(pre_pe, 13)
            v.tensor_tensor(vx[:, 0, :, :], bank[6][0:SK, :].rearrange("p (b d) -> p b d", b=B),
                            bvbc[:].unsqueeze(1).to_broadcast([SK, B, D]), ALU.add).then_inc(vec, 1)
            dve.wait_ge(vec, VEC_PRE)

            with dve.Fori(0, B) as b:
                ps_q, ps_k, ps_s, ps_o, ps_x, ps_t = bank[0], bank[1], bank[2:4], bank[4:6], bank[6], bank[7]
                four = (*ps_s, *ps_o)

                def link(ins):
                    n[0] += 1
                    ins.then_inc(vec, 1)
                    dve.wait_ge(vec, b * VEC_STEPS + VEC_PRE + n[0])

                def tiles(ps):
                    return ps[:].rearrange("p (t d) -> p t d", t=T)

                def over(col, w):
                    return col.unsqueeze(2).to_broadcast([P, T, w])

                def moments(src, eps=1e-5):
                    for t in range(T):
                        l = v.bn_stats(st[:, t, :], src[:, t, :])
                    link(l)
                    v.tensor_copy(tick[:, 0:1], half[:, 0:1])
                    for t in range(T):
                        l = v.bn_aggr(mv[:, t, :], st[:, t, :])
                    link(l)
                    v.tensor_scalar(ve[:], mv[:, :, 1], eps, None, ALU.add).then_inc(var_ready, 1)

                def normalize(dst, src, k):
                    dve.wait_ge(rstd_ready, b * N_POW + (k + 1))
                    for t in range(T):
                        l = v.tensor_scalar(dst[:, t, :], src[:, t, :], mv[:, t, 0:1], rs[:, t:t + 1],
                                            ALU.subtract, ALU.mult)
                    return l

                dve.wait_ge(x_loaded, b * 16 + 16)
                moments(x_in)
                link(normalize(xn, x_in, 0))
                dve.wait_ge(xs_ready, b * 2 + 1)
                v.tensor_tensor(r2[:], mv[:, :, 1], rs[:], ALU.mult).then_inc(x_free, 1)
                dve.wait_ge(x_free, b + 1)
                link(v.tensor_tensor(r2[:], r2[:], rs[:], ALU.mult))
                v.tensor_scalar(ve[:], r2[:], 1e-5, None, ALU.add).then_inc(var_ready, 1)
                dve.wait_ge(rstd_ready, b * N_POW + 2)
                for t in range(T):
                    l = v.tensor_scalar(xh[:, t, :], xn[:, t, :], r2[:, t:t + 1], None, ALU.mult)
                l.then_inc(ln_ready, 1)

                for t in range(T):
                    dve.wait_ge(v_done, b * 2 * T + 2 * t + 2)
                    v.tensor_copy(v_tm[:, t, H // 2:H, 0:DH], four[(2 * t + 1) % 4][:]
                                  .rearrange("p (h d) -> p h d", d=DH)).then_inc(v_dve, 1)

                def phi(w, j):
                    m = 2 * j + w
                    dve.wait_ge(phi_parts, b * 2 * NPAIR + m + 1)
                    if j >= 2:
                        dve.wait_ge(apply_done, b * H + 2 * (j - 1))
                    v.scalar_tensor_tensor((qT, kT)[w][:, j % 2, :], (ps_q, ps_k)[w][:], 0.0, eb[:, m % 2, :],
                                           ALU.max, ALU.add).then_inc(phi_ready, 1)

                def causal(i):
                    if i >= 2:
                        dve.wait_ge(apply_done, b * H + i - 1)
                    for c in range(2):
                        dve.wait_ge(scores_done, b * 2 * H + 2 * i + c + 1)
                        v.tensor_tensor(stm[:, i % 2, c, :], ps_s[c][:, 0:3 * P], mask[:], ALU.mult)\
                            .then_inc(st_ready, 1)

                def attn_out(i):
                    j, hh = i // 2, i % 2
                    dve.wait_ge(apply_done, b * H + i + 1)
                    if j >= 2:
                        dve.wait_ge(atT_done, b * NPAIR + j - 1)
                    o = ps_o[hh][:, 0:T * V1].rearrange("p (t e) -> p t e", e=V1)
                    link(v.tensor_scalar(dn[:], o[:, :, DH], 1e-6, None, ALU.add))
                    link(v.reciprocal(rd[:], dn[:]))
                    v.tensor_tensor(atm[:, j % 2, :, hh * DH:(hh + 1) * DH], o[:, :, 0:DH], over(rd[:], DH),
                                    ALU.mult).then_inc(attn_evac, 1)

                phi(0, 0)
                phi(1, 0)
                for j in range(NPAIR):
                    causal(2 * j)
                    if j + 1 < NPAIR:
                        phi(0, j + 1)
                    causal(2 * j + 1)
                    if j + 1 < NPAIR:
                        phi(1, j + 1)
                    attn_out(2 * j)
                    attn_out(2 * j + 1)

                dve.wait_ge(y_done, b * N_Y + Y_WO + 1)
                v.tensor_tensor(xn[:], tiles(ps_q), xn[:], ALU.add).then_inc(xa_ready, 1)
                dve.wait_ge(xa_ready, b + 1)
                moments(xn)
                normalize(xh, xn, 2).then_inc(ln_ready, 1)
                dve.wait_ge(y_done, b * N_Y + Y_FFN + 1)
                dve.wait_ge(xs_ready, b * 2 + 2)
                link(v.tensor_tensor(xr[:], tiles(ps_k), xs[:], ALU.add))

                def cross(i):
                    moments(xr)
                    normalize(xh, xr, (3, 6)[i]).then_inc(ln_ready, 1)
                    dve.wait_ge(sc_done, b * 2 + (i + 1))
                    sc = ps_s[0][:, 0:T * SK].rearrange("p (t k) -> p t k", t=T)
                    link(v.tensor_reduce(mx[:], sc, AX.X, ALU.max))
                    v.tensor_tensor(pd[:], sc, over(mx[:], SK), ALU.subtract).then_inc(sd_ready, 1)
                    dve.wait_ge(p_ready, b * 2 + (i + 1))
                    link(v.tensor_reduce(sm[:], pp[:], AX.X, ALU.add))
                    link(v.reciprocal(ri[:], sm[:]))
                    dve.wait_ge(y_done, b * N_Y + (Y_X0, Y_X1)[i] + 1)
                    for t in range(T):
                        l = v.scalar_tensor_tensor(xr[:, t, :], ps_q[:, t * P:(t + 1) * P], ri[:, t:t + 1],
                                                   xr[:, t, :], ALU.mult, ALU.add)
                    link(l)

                cross(0)

                moments(xr)
                normalize(xh, xr, 4).then_inc(ln_ready, 1)
                dve.wait_ge(lg_done, b + 1)
                link(v.tensor_tensor(lg[:], ps_s[1][:, 0:T * E0].rearrange("p (t e) -> p t e", t=T),
                                     e0bg[:].unsqueeze(1).to_broadcast([P, T, E0]), ALU.add))

                def argmax(src, top, onehot):
                    link(v.tensor_reduce(top[:], src[:], AX.X, ALU.max))
                    link(v.tensor_tensor(key[:], src[:], over(top[:], E0), ALU.is_equal))
                    link(v.scalar_tensor_tensor(key[:], key[:], -64.0, iota8[:], ALU.mult, ALU.add))
                    link(v.tensor_reduce(mn[:], key[:], AX.X, ALU.min))
                    link(v.tensor_tensor(onehot[:], key[:], over(mn[:], E0), ALU.is_equal))

                argmax(lg, m1, oh1)
                link(v.scalar_tensor_tensor(l2[:], oh1[:], -BIG, lg[:], ALU.mult, ALU.add))
                argmax(l2, m2, oh2)
                v.tensor_tensor(mn[:], m2[:], m1[:], ALU.subtract).then_inc(md_ready, 1)
                dve.wait_ge(me_ready, b + 1)
                link(v.tensor_scalar(m1[:], g2[:], 1.0, None, ALU.add))
                link(v.reciprocal(g1[:], m1[:]))
                link(v.tensor_tensor(g2[:], g2[:], g1[:], ALU.mult))
                v.tensor_tensor(comb[:], oh1[:], over(g1[:], E0), ALU.mult)
                link(v.tensor_tensor(key[:], oh2[:], over(g2[:], E0), ALU.mult))
                v.tensor_tensor(comb[:], comb[:], key[:], ALU.add).then_inc(comb_ready, 1)
                dve.wait_ge(comb_ready, b + 1)

                def hidden(e):
                    for c in (1, 3):
                        dve.wait_ge(up_done, b * FC * E0 + FC * e + c + 1)
                        if e >= 2:
                            dve.wait_ge(y_done, b * N_Y + Y_E + e - 1)
                        r = R_EB1 + FC * e + c
                        v.tensor_scalar(big[:, 4 * (e % 2) + c, :], four[(c + 2) % 4][:], cols[:, r:r + 1], 0.0,
                                        ALU.add, ALU.max).then_inc(up_dve, 1)

                hidden(0)
                dve.wait_ge(y_done, b * N_Y + Y_BIAS + 1)
                link(v.tensor_tensor(xr[:], tiles(ps_q), xr[:], ALU.add))
                for e in range(E0):
                    if e + 1 < E0:
                        hidden(e + 1)
                    dve.wait_ge(y_done, b * N_Y + Y_E + e + 1)
                    for t in range(T):
                        l = v.scalar_tensor_tensor(xr[:, t, :], (ps_k, ps_q)[e % 2][:, t * P:(t + 1) * P],
                                                   comb[:, t, e:e + 1], xr[:, t, :], ALU.mult, ALU.add)
                    l.then_inc(acc_done, 1)
                    dve.wait_ge(acc_done, b * E0 + e + 1)

                moments(xr)
                normalize(xh, xr, 5).then_inc(ln_ready, 1)
                for c in range(IC):
                    dve.wait_ge(xp_ready, b * IC + c + 1)
                    r = R_CB + c
                    link(v.tensor_scalar(cv[:, c, :], xpad[:, c, KC - 1:KC - 1 + S], convw[:, c, KC - 1:KC],
                                         cols[:, r:r + 1], ALU.mult, ALU.add))
                    for k in range(KC - 1):
                        l = v.scalar_tensor_tensor(cv[:, c, :], xpad[:, c, k:k + S], convw[:, c, k:k + 1],
                                                   cv[:, c, :], ALU.mult, ALU.add)
                        if k < KC - 2:
                            link(l)
                    l.then_inc(cv_ready, 1)
                dve.wait_ge(ssm_done, b + 1)
                link(v.tensor_copy(ssm[:].rearrange("p t n -> p (t n)"), ps_x[:, 0:T * NX]))
                x0, neg, u, w, ln, d, z, dl = ssm[:, :, 0], *(sp_x[:, i, :] for i in (0, 2, 3, 4, 5, 6, 7))
                link(v.tensor_scalar(neg, x0, -1.0, None, ALU.mult))
                v.tensor_tensor(sp_x[:, 1, :], x0, neg, ALU.min).then_inc(abs_ready, 1)
                dve.wait_ge(u_ready, b + 1)
                v.tensor_scalar(w, u, 1.0, None, ALU.add).then_inc(w_ready, 1)
                dve.wait_ge(w_ready, b + 1)
                link(v.tensor_scalar(d, w, -1.0, None, ALU.add))
                link(v.tensor_scalar(z, d, 0.0, None, ALU.is_equal))
                link(v.tensor_tensor(d, d, z, ALU.add))
                link(v.reciprocal(neg, d))
                link(v.tensor_tensor(neg, neg, u, ALU.mult))
                link(v.tensor_tensor(z, z, u, ALU.mult))
                dve.wait_ge(l_ready, b + 1)
                link(v.tensor_tensor(ln, ln, neg, ALU.mult))
                link(v.tensor_tensor(ln, ln, z, ALU.add))
                link(v.scalar_tensor_tensor(dl, x0, 0.0, ln, ALU.max, ALU.add))
                link(v.tensor_scalar(dl, dl, 1.0 / S, None, ALU.mult))
                v.tensor_tensor(dB[:], ssm[:, :, 1:1 + NS], over(dl, NS), ALU.mult).then_inc(db_ready, 1)
                for c in range(IC):
                    dve.wait_ge(yt_done, b * IC + c + 1)
                    r = R_DS + c
                    link(v.scalar_tensor_tensor(yT[:, c, :], xc[:, c, :], cols[:, r:r + 1], ps_o[c][:],
                                                ALU.mult, ALU.add))
                    v.tensor_tensor(yT[:, c, :], yT[:, c, :], sz[:, c, :], ALU.mult).then_inc(yt_ready, 1)
                dve.wait_ge(y_done, b * N_Y + Y_SSM + 1)
                link(v.tensor_tensor(xr[:], tiles(ps_q), xr[:], ALU.add))

                cross(1)
                moments(xr)
                normalize(xh, xr, 7).then_inc(ln_ready, 1)
                dve.wait_ge(x_kept, b + 1)
                assert n[0] == VEC_STEPS, n

        ph.close()
        NG = T
        NT = B * T
        TG = B
        CAP = -(-2 * (B * S // NG) // E1)
        CS = CAP + CAP % 2
        RS = P // 2
        NK = E1 // 2
        EQ = 8
        NQ = E1 // EQ
        WS = E1 * CS
        NF = 7
        assert CS <= RS and EQ * CS <= 512 and NG % 2 == 0

        hd = sb("hd", [P, 2 * NK * FF])
        disp = sb("disp", [P, 2, TG, E1 * RS])
        dT = sb("dT", [P, NK, TG * P])
        xT = sb("xT", [P, E1, 2, RS])
        ht = sb("ht", [P, 2, TG, FF])
        ug = sb("ug", [P, TG, 2, D])
        iw = sb("iw", [P, WS])
        cT24 = sb("cT24", [E1, 2, TG * P])
        b124 = sb("b124", [E1, FF])
        b224 = sb("b224", [E1, D])
        lnw = sb("lnw", [P, D])
        lnb = sb("lnb", [P, D])
        wg24 = sb("wg24", [P, E1])
        comb24 = sb("comb24", [P, NT, E1])
        combp = sb("combp", [P, TG, 2, E1])
        sl = sb("sl", [P, NT, 2])
        slp = sb("slp", [P, TG, 2, 2])
        ft = sb("ft", [P, NT, NF], BF16)
        ftp = sb("ftp", [P, TG, 2, NF], BF16)
        lwp = sb("lwp", [P, 2 * FC])
        lbp = sb("lbp", [P, 2 * FC])
        ecol = sb("ecol", [P, NK])
        gf = sb("gf", [P, 2, NK, NF])
        gs = sb("gs", [P, 2, NK])
        gt = sb("gt", [P, 2, NK])
        gate = sb("gate", [P, 2, NK])
        tri = sb("tri", [P, P], BF16)
        one = sb("one", [P, P], BF16)
        st6 = sb("st6", [P, TG, 6])
        mv6 = sb("mv6", [P, TG, 2])
        ve6 = sb("ve6", [P, TG])
        rs6 = sb("rs6", [P, TG])
        ob = sb("ob", [P, 2, TG, D])
        sv = sb("sv", [P, 16, NT])

        hd2 = hd[:].rearrange("p (g k f) -> p g k f", g=2, k=NK)
        d2T = hd[:].rearrange("p (c e g s) -> p c e g s", c=FC, e=E1, g=2)
        yv = ht[:].rearrange("p g t f -> p (g t f)")[:, 0:2 * NK * D].rearrange("p (g k d) -> p g k d", g=2, k=NK)
        uT = hd[:, 0:NT * P]
        TW = NT * E1
        tmp = [hd[:, NT * P + i * TW:NT * P + (i + 1) * TW].rearrange("p (t e) -> p t e", e=E1) for i in range(6)]
        h0 = NT * P + 6 * TW
        i24 = hd[:, h0:h0 + TW].rearrange("p (t e) -> p t e", e=E1)
        i24i = hd[:, h0 + TW:h0 + 2 * TW].bitcast(I32).rearrange("p (t e) -> p t e", e=E1)
        eci = hd[:, h0 + 2 * TW:h0 + 2 * TW + NK].bitcast(I32)
        h1 = h0 + 3 * TW + WS
        oh1b, oh2b = (hd[:, h1 + i * TW:h1 + i * TW + TW // 2].bitcast(BF16).rearrange("p (t e) -> p t e", e=E1)
                      for i in range(2))
        iwi = hd[:, h0 + 3 * TW:h0 + 3 * TW + WS].bitcast(I32)

        def slots(gi, b):
            return disp[:, gi, b, :].rearrange("p (e s) -> p e s", s=RS)[:, :, 0:CS]

        names = ("w2_in k2 uT_done uT_act uT_dve lg2_done lgd_ready lge_ready oh_ready loc_done pair_act pair_dve "
                 "disp_ready cT_done cT_act cT_dve pA evA_act evA_dve gt_done gate_ready dt_done dt_act dt_dve "
                 "c1_done hv_ready hr_ready ht_ready pads_ready w_used o_ready r2_ready vec2").split()
        (w2_in, k2, uT_done, uT_act, uT_dve, lg2_done, lgd_ready, lge_ready, oh_ready, loc_done, pair_act, pair_dve,
         disp_ready, cT_done, cT_act, cT_dve, pA, evA_act, evA_dve, gt_done, gate_ready, dt_done, dt_act, dt_dve,
         c1_done, hv_ready, hr_ready, ht_ready, pads_ready, w_used, o_ready, r2_ready, vec2) = [
             sem(x) for x in names]
        NP2 = NG // 2
        U_DISP, U_UP = 0, 2 * NQ
        U_D2 = U_UP + E1
        U_DOWN = U_D2 + 2 * FC * NQ
        U_ALL = U_DOWN + E1 // 4
        VEC2_PRE, VEC2_STEPS = 46, 47
        N_C1 = 2 * TG + 2
        assert U_UP % 2 == 0 and U_D2 % 2 == 0 and U_DOWN % 2 == 0 and U_ALL % 2 == 0
        bg = lambda x: x.rearrange("p (b g) d -> p b g d", g=NG)

        block2 = ctx.enter_context(nc.Block())

        @block2.sync
        def _(sp):
            for dst, src in ((b124[:], a["L1_ffn_b1"]), (b224[:], a["L1_ffn_b2"]), (wg24[:], a["L1_ffn_Wg"]),
                             (lnw[:], a["L1_ffn_ln_out_w"].rearrange("(o d) -> o d", o=1).to_broadcast([P, D])),
                             (lnb[:], a["L1_ffn_ln_out_b"].rearrange("(o d) -> o d", o=1).to_broadcast([P, D]))):
                sp.dma_start(dst, src).then_inc(w2_in, 16)
            NC = E1 // NR
            w_dram = (a["L1_ffn_W1"].rearrange("e d f -> d e f"),
                      a["L1_ffn_W2"].rearrange("e (c p) d -> p e c d", p=P))

            def load(kind, e, k):
                if kind == 0:
                    src, dst = w_dram[0][:, bass.ds(e, 1), :], ring[:, k:k + 1, :]
                else:
                    src = w_dram[1][:, bass.ds(e, 1), :, :].rearrange("p e c d -> p (e c) d")
                    dst = ring[:, k, :].rearrange("p (c d) -> p c d", c=FC)
                sp.dma_start(dst, src).then_inc(slot_in[k], 16)

            for pair in range(NP2):
                for kind in range(2):
                    used, base = ((pA, pair * U_DOWN + U_UP), (w_used, pair * E1))[kind]
                    if pair or kind:
                        before, last = ((w_used, pair * E1), (pA, pair * U_DOWN + U_UP + E1))[kind]
                        for k in range(NR):
                            sp.wait_ge(before, last - NR + k + 1)
                            load(kind, k, k)
                    with sp.Fori(1, NC) as c:
                        for k in range(NR):
                            sp.wait_ge(used, c * NR + (base - NR + k + 1))
                            load(kind, c * NR + k, k)

        @block2.gpsimd
        def _(pool):
            g_ = nc.gpsimd
            g_.iota(iwi, pattern=[[1, WS]], base=0, channel_multiplier=0)
            g_.iota(eci[0:RS], pattern=[[2, NK]], base=0, channel_multiplier=0).then_inc(k2, 1)
            pool.wait_ge(k2, 1)
            g_.iota(eci[RS:P], pattern=[[2, NK]], base=1, channel_multiplier=0).then_inc(k2, 1)
            pool.wait_ge(k2, 2)
            g_.iota(i24i, pattern=[[0, NT], [1, E1]], base=0, channel_multiplier=0)
            g_.memset(one[:], 1.0)
            g_.memset(tri[:], 1.0).then_inc(k2, 1)
            pool.wait_ge(k2, 3)
            g_.affine_select(out=tri[:], in_=tri[:], compare_op=ALU.is_gt, fill=0.0, base=0, pattern=[[1, P]],
                             channel_multiplier=-1)
            g_.memset(xT[:, :, :, CS:RS], 0.0)
            for gi in range(2):
                for b in range(TG):
                    l = g_.memset(disp[:, gi, b, :].rearrange("p (e s) -> p e s", s=RS)[:, :, CS:RS], 0.0)
            l.then_inc(k2, 1)
            with pool.Fori(0, NP2) as pg:
                for m in range(2 * TG):
                    pool.wait_ge(hv_ready, pg * (2 * TG + 2) + (m + 1))
                    g_.tensor_tensor(rs6[:, 0:1], ve6[:, 0:1], half[:, 0:1], ALU.pow).then_inc(hr_ready, 1)
                pool.wait_ge(c1_done, pg * N_C1 + 2 * TG)
                g_.tensor_tensor(tick[:, 1:2], half[:, 0:1], half[:, 0:1], ALU.add)
                g_.memset(d2T[:, :, :, :, CS:RS].rearrange("p c e g s -> p (c e g) s"), 0.0).then_inc(pads_ready, 1)
                for m in range(2):
                    pool.wait_ge(hv_ready, pg * (2 * TG + 2) + (2 * TG + m + 1))
                    g_.tensor_tensor(rs6[:], ve6[:], half[:, 0:TG], ALU.pow).then_inc(hr_ready, 1)

        @block2.tensor
        def _(pe):
            mm, tr = nc.tensor.matmul, nc.tensor.transpose
            for i in range(NT // 4):
                for j in range(4):
                    l = tr(bank[i][:, j * P:(j + 1) * P], u_all[:, 4 * i + j, :], ident[:])
                l.then_inc(uT_done, 1)
            pe.wait_ge(w2_in, 16 * 5)
            pe.wait_ge(uT_act, 2)
            pe.wait_ge(uT_dve, 2)
            for t in range(NT):
                l = mm(bank[4][:, t * E1:(t + 1) * E1], uT[:, t * P:(t + 1) * P], wg24[:], start=True, stop=True)
            l.then_inc(lg2_done, 1)
            pe.wait_ge(oh_ready, 1)
            pe.wait_ge(k2, 4)
            W = NG * E1
            flat = [x.rearrange("p t e -> p (t e)") for x in (oh1b, oh2b)]
            for which in range(2):
                for t in range(TG):
                    terms = [(tri, which, t)] + [(one, which, p) for p in range(t)]
                    terms += [(one, 0, p) for p in range(TG)] if which else []
                    for i, (m, c, p) in enumerate(terms):
                        l = mm(bank[5 + which][:, t * W:(t + 1) * W], m[:], flat[c][:, p * W:(p + 1) * W],
                               start=(i == 0), stop=(i == len(terms) - 1))
            l.then_inc(loc_done, 1)
            pe.wait_ge(r2_ready, 1)

            with pe.Fori(0, NP2) as pg:
                def bank_a(u):
                    if u >= 4:
                        pe.wait_ge((evA_act, evA_dve)[u % 2], pg * (U_ALL // 2) + (u - 4) // 2 + 1)
                    return bank[u % 4]

                pe.wait_ge(pair_act, pg + 1)
                pe.wait_ge(pair_dve, pg + 1)
                for gi in range(2):
                    for b in range(TG):
                        l = tr(bank[4 + gi][0:E1, b * P:(b + 1) * P], combp[:, b, gi, :], ident[:])
                    l.then_inc(cT_done, 1)
                for gi in range(2):
                    pe.wait_ge(disp_ready, pg * 2 + gi + 1)
                    for q in range(NQ):
                        ps = bank_a(U_DISP + gi * NQ + q)
                        for b in range(TG):
                            l = mm(ps[:, 0:EQ * CS], ug[:, b, gi, :], slots(gi, b)[:, q * EQ:(q + 1) * EQ, :],
                                   start=(b == 0), stop=(b == TG - 1))
                        l.then_inc(pA, 1)
                for gi in range(2):
                    for k in range(NK):
                        for b in range(TG):
                            hot = disp[:, gi, b, :].bitcast(BF16).rearrange("p (s h) -> p s h", h=2)[:, :, 1]
                            l = mm(bank[6 + gi][:, k * NF:(k + 1) * NF], hot[:, k * P:(k + 1) * P], ftp[:, b, gi, :],
                                   start=(b == 0), stop=(b == TG - 1))
                    l.then_inc(gt_done, 1)
                pe.wait_ge(evA_act, pg * (U_ALL // 2) + U_UP // 2)
                pe.wait_ge(evA_dve, pg * (U_ALL // 2) + U_UP // 2)
                for e in range(E1):
                    ps = bank_a(U_UP + e)
                    pe.wait_ge(slot_in[e % NR], (pg * (2 * E1 // NR) + (e // NR + 1)) * 16)
                    mm(ps[:], xT[:, e, :, :], ring[:, e % NR, :], start=True, stop=True).then_inc(pA, 1)

                def slots_to_rows(i, gi):
                    for k in range(NK):
                        m = i * NK + k
                        if i == 0 and k < 2:
                            pe.wait_ge((cT_act, cT_dve)[k], pg + 1)
                        elif k < 2:
                            pe.wait_ge((dt_act, dt_dve)[k], pg * 2 * NK + i * NK // 2)
                        else:
                            pe.wait_ge((dt_act, dt_dve)[k % 2], pg * 2 * NK + (m - 2) // 2 + 1)
                        for b in range(TG):
                            l = tr(bank[4 + k % 2][:, b * P:(b + 1) * P], disp[:, gi, b, k * P:(k + 1) * P], ident[:])
                        l.then_inc(dt_done, 1)
                    pe.wait_ge(dt_act, pg * 2 * NK + (i + 1) * NK // 2)
                    pe.wait_ge(dt_dve, pg * 2 * NK + (i + 1) * NK // 2)

                for gi in range(2):
                    slots_to_rows(gi, gi)
                    if gi == 0:
                        pe.wait_ge(gate_ready, pg + 1)
                        pe.wait_ge(evA_act, pg * (U_ALL // 2) + U_D2 // 2)
                        pe.wait_ge(evA_dve, pg * (U_ALL // 2) + U_D2 // 2)
                    for b in range(TG):
                        m = gi * TG + b
                        if m >= 2:
                            pe.wait_ge(ht_ready, pg * 2 * TG + m - 1)
                        ps = bank[6 + b % 2]
                        mm(ps[:], cT24[:, gi, b * P:(b + 1) * P], b124[:], start=True, stop=False)
                        for k in range(NK):
                            l = mm(ps[:], dT[:, k, b * P:(b + 1) * P], hd2[:, gi, k, :], start=False, stop=(k == NK - 1))
                        l.then_inc(c1_done, 1)
                for gi in range(2):
                    pe.wait_ge(ht_ready, pg * 2 * TG + (gi + 1) * TG)
                    for c in range(FC):
                        for q in range(NQ):
                            ps = bank_a(U_D2 + (gi * FC + c) * NQ + q)
                            for b in range(TG):
                                l = mm(ps[:, 0:EQ * CS], ht[:, gi, b, c * P:(c + 1) * P],
                                       slots(gi, b)[:, q * EQ:(q + 1) * EQ, :], start=(b == 0), stop=(b == TG - 1))
                            l.then_inc(pA, 1)
                pe.wait_ge(evA_act, pg * (U_ALL // 2) + U_DOWN // 2)
                pe.wait_ge(evA_dve, pg * (U_ALL // 2) + U_DOWN // 2)
                pe.wait_ge(pads_ready, pg + 1)
                for e in range(E1):
                    if e % 4 == 0:
                        ps = bank_a(U_DOWN + e // 4)
                    pe.wait_ge(slot_in[e % NR], (pg * (2 * E1 // NR) + (E1 // NR + e // NR + 1)) * 16)
                    for c in range(FC):
                        l = mm(ps[:, (e % 4) * P:(e % 4 + 1) * P], d2T[:, c, e, :, :],
                               ring[:, e % NR, c * P:(c + 1) * P], start=(c == 0), stop=(c == FC - 1))
                    l.then_inc(w_used, 1)
                for gi in range(2):
                    slots_to_rows(2 + gi, gi)
                    if gi == 0:
                        pe.wait_ge(evA_act, pg * (U_ALL // 2) + U_ALL // 2)
                        pe.wait_ge(evA_dve, pg * (U_ALL // 2) + U_ALL // 2)
                    ps = bank[6 + gi]
                    for b in range(TG):
                        o = ps[:, b * P:(b + 1) * P]
                        mm(o, cT24[:, gi, b * P:(b + 1) * P], b224[:], start=True, stop=False)
                        for k in range(NK):
                            l = mm(o, dT[:, k, b * P:(b + 1) * P], yv[:, gi, k, :], start=False, stop=(k == NK - 1))
                    l.then_inc(c1_done, 1)

        @block2.scalar
        def _(act):
            af = nc.scalar.activation
            for i in (0, 2):
                act.wait_ge(uT_done, i + 1)
                af(uT[:, i * 512:(i + 1) * 512], bank[i][:], ACT.Copy).then_inc(uT_act, 1)
            act.wait_ge(lgd_ready, 1)
            af(tmp[4], tmp[4], ACT.Exp)
            af(sv[:, 4, :], sv[:, 4, :], ACT.Exp).then_inc(lge_ready, 1)

            with act.Fori(0, NP2) as pg:
                two = bass.ds(pg * 2, 2)

                def taken(u):
                    act.wait_ge(pA, pg * U_DOWN + u + 1)
                    return bank[u % 4]

                act.wait_ge(r2_ready, 1)
                af(ug[:], bg(u_all[:])[:, :, two, :], ACT.Copy).then_inc(pair_act, 1)
                act.wait_ge(cT_done, pg * 2 + 1)
                af(cT24[:, 0, :], bank[4][0:E1, :], ACT.Copy).then_inc(cT_act, 1)
                for n in range(0, 2 * NQ, 2):
                    gi, q = n // NQ, n % NQ
                    af(xT[:, q * EQ:(q + 1) * EQ, gi, 0:CS],
                       taken(U_DISP + n)[:, 0:EQ * CS].rearrange("p (e s) -> p e s", s=CS), ACT.Copy).then_inc(evA_act, 1)
                for e in range(0, E1, 2):
                    ps = taken(U_UP + e)
                    af(hd2[0:RS, 0, e // 2, :], ps[0:RS, :], ACT.Copy)
                    af(hd2[0:RS, 1, e // 2, :], ps[RS:P, :], ACT.Copy).then_inc(evA_act, 1)

                def rows(i, gi):
                    for k in range(0, NK, 2):
                        act.wait_ge(dt_done, pg * 4 * NK + (i * NK + k + 1))
                        if k == 0:
                            act.wait_ge(gate_ready, pg + 1)
                            if i:
                                act.wait_ge(c1_done, pg * N_C1 + (0, TG, 2 * TG, 2 * TG + 1)[i])
                        af(dT[:, k, :], bank[4][:], ACT.Copy, scale=gate[:, gi, k:k + 1]).then_inc(dt_act, 1)

                rows(0, 0)
                rows(1, 1)
                act.wait_ge(c1_done, pg * N_C1 + 2 * TG)
                for n in range(0, 2 * FC * NQ, 2):
                    gi, c, q = n // (FC * NQ), n // NQ % FC, n % NQ
                    r = gi * FC + c
                    af(d2T[:, c, q * EQ:(q + 1) * EQ, gi, 0:CS],
                       taken(U_D2 + n)[:, 0:EQ * CS].rearrange("p (e s) -> p e s", s=CS), ACT.Relu,
                       scale=lwp[:, r:r + 1], bias=lbp[:, r:r + 1]).then_inc(evA_act, 1)

                def outputs_of_experts(q):
                    act.wait_ge(w_used, pg * E1 + 4 * q + 4)
                    ps = bank[(U_DOWN + q) % 4][:].rearrange("p (k two d) -> p k two d", two=2, d=D)
                    for gi in range(2):
                        for par in range(2):
                            l = af(yv[par * RS:(par + 1) * RS, gi, 2 * q:2 * q + 2, :],
                                   ps[gi * RS:(gi + 1) * RS, :, par, :], ACT.Copy)
                    l.then_inc(evA_act, 1)

                for q in range(0, E1 // 4, 2):
                    outputs_of_experts(q)
                for gi in range(2):
                    rows(2 + gi, gi)
                for gi in range(2):
                    act.wait_ge(o_ready, pg * 2 + gi + 1)
                    dst = out.rearrange("b (g p) d -> p b g d", p=P)[:, :, bass.ds(pg * 2 + gi, 1), :]\
                        .rearrange("p b g d -> p (b g) d")
                    act.dma_start(dst, ob[:, gi, :, :]).then_inc(out_done, 16)
                act.wait_ge(out_done, pg * 32 + 32)

        @block2.vector
        def _(dve):
            v = nc.vector
            n = [0]

            def link0(ins):
                n[0] += 1
                ins.then_inc(vec2, 1)
                dve.wait_ge(vec2, n[0])

            def wide(col, w=E1):
                return col.unsqueeze(2).to_broadcast([P, NT, w])

            for i in (1, 3):
                dve.wait_ge(uT_done, i + 1)
                v.tensor_copy(uT[:, i * 512:(i + 1) * 512], bank[i][:]).then_inc(uT_dve, 1)
            lgs, key, oh1, oh2, ex, l2 = tmp
            m1, m2, n1, n2, e21, ssum, p1, p2, pos1, pos2, k1, k2_, den, t0, t1, t2 = (sv[:, i, :] for i in range(16))
            dve.wait_ge(k2, 4)
            v.tensor_copy(iw[:], iwi)
            v.tensor_copy(ecol[:], eci)
            link0(v.tensor_copy(i24, i24i))
            dve.wait_ge(lg2_done, 1)
            link0(v.tensor_copy(lgs, bank[4][:, 0:NT * E1].rearrange("p (t e) -> p t e", e=E1)))

            def argmax(src, top, idx, onehot):
                link0(v.tensor_reduce(top, src, AX.X, ALU.max))
                link0(v.tensor_tensor(key, src, wide(top), ALU.is_equal))
                link0(v.scalar_tensor_tensor(key, key, -64.0, i24, ALU.mult, ALU.add))
                link0(v.tensor_reduce(idx, key, AX.X, ALU.min))
                link0(v.tensor_tensor(onehot, key, wide(idx), ALU.is_equal))

            argmax(lgs, m1, n1, oh1)
            link0(v.scalar_tensor_tensor(l2, oh1, -BIG, lgs, ALU.mult, ALU.add))
            argmax(l2, m2, n2, oh2)
            v.tensor_copy(oh1b, oh1)
            v.tensor_copy(oh2b, oh2).then_inc(oh_ready, 1)
            v.tensor_tensor(ex, lgs, wide(m1), ALU.subtract)
            v.tensor_tensor(e21, m2, m1, ALU.subtract).then_inc(lgd_ready, 1)
            dve.wait_ge(lge_ready, 1)
            link0(v.tensor_reduce(ssum, ex, AX.X, ALU.add))
            link0(v.reciprocal(p1, ssum))
            link0(v.tensor_tensor(p2, p1, e21, ALU.mult))
            dve.wait_ge(loc_done, 1)
            for i, (oh, pos, kp, pr, idx) in enumerate(((oh1, pos1, k1, p1, n1), (oh2, pos2, k2_, p2, n2))):
                loc = bank[5 + i][:, 0:NT * E1].rearrange("p (t e) -> p t e", e=E1)
                link0(v.tensor_tensor(key, loc, oh, ALU.mult))
                link0(v.tensor_reduce(pos, key, AX.X, ALU.add))
                link0(v.tensor_scalar(kp, pos, float(CAP), None, ALU.is_lt))
                link0(v.scalar_tensor_tensor(t0, idx, float(CS), pos, ALU.mult, ALU.add))
                link0(v.tensor_scalar(t0, t0, float(64 * CS + 1), None, ALU.add))
                link0(v.tensor_tensor(t0, t0, kp, ALU.mult))
                v.tensor_scalar(sl[:, :, i], t0, -1.0, None, ALU.add)
                link0(v.tensor_tensor(pr, pr, kp, ALU.mult))
            link0(v.tensor_tensor(den, p1, p2, ALU.add))
            link0(v.tensor_scalar(den, den, 1e-9, None, ALU.max))
            link0(v.reciprocal(t0, den))
            v.tensor_tensor(p1, p1, t0, ALU.mult)
            link0(v.tensor_tensor(p2, p2, t0, ALU.mult))
            v.tensor_tensor(comb24[:], oh1, wide(p1), ALU.mult)
            link0(v.tensor_tensor(key, oh2, wide(p2), ALU.mult))
            v.tensor_tensor(comb24[:], comb24[:], key, ALU.add)
            link0(v.tensor_scalar(ft[:, :, 6], n1, 64.0, None, ALU.add))
            for i, g in enumerate((p1, p2)):
                link0(v.tensor_copy(ft[:, :, 3 * i], g))
                link0(v.tensor_tensor(t1, g, ft[:, :, 3 * i], ALU.subtract))
                link0(v.tensor_copy(ft[:, :, 3 * i + 1], t1))
                link0(v.tensor_tensor(t2, t1, ft[:, :, 3 * i + 1], ALU.subtract))
                link0(v.tensor_copy(ft[:, :, 3 * i + 2], t2))
            v.tensor_copy(t1, t2).then_inc(r2_ready, 1)
            dve.wait_ge(r2_ready, 1)
            assert n[0] == VEC2_PRE, n
            n[0] = 0

            with dve.Fori(0, NP2) as pg:
                two = bass.ds(pg * 2, 2)

                def link(ins):
                    n[0] += 1
                    ins.then_inc(vec2, 1)
                    dve.wait_ge(vec2, pg * VEC2_STEPS + VEC2_PRE + n[0])

                def taken(u):
                    dve.wait_ge(pA, pg * U_DOWN + u + 1)
                    return bank[u % 4]

                def over(col, w):
                    return col.unsqueeze(2).to_broadcast([P, TG, w])

                v.tensor_copy(slp[:], bg(sl[:])[:, :, two, :])
                v.tensor_copy(ftp[:], bg(ft[:])[:, :, two, :])
                v.tensor_copy(lwp[:], cols[:, R_LW:R_LW + NG * FC].rearrange("p (g c) -> p g c", c=FC)[:, two, :]
                              .rearrange("p g c -> p (g c)"))
                v.tensor_copy(lbp[:], cols[:, R_LB:R_LB + NG * FC].rearrange("p (g c) -> p g c", c=FC)[:, two, :]
                              .rearrange("p g c -> p (g c)"))
                v.tensor_copy(combp[:], bg(comb24[:])[:, :, two, :]).then_inc(pair_dve, 1)
                dve.wait_ge(pair_dve, pg + 1)
                for gi in range(2):
                    for b in range(TG):
                        l = v.tensor_scalar(slots(gi, b), iw[:].rearrange("p (e s) -> p e s", s=CS), slp[:, b, gi, 0:1], None, ALU.is_equal)
                    link(l)
                    for b in range(TG):
                        l = v.scalar_tensor_tensor(slots(gi, b), iw[:].rearrange("p (e s) -> p e s", s=CS), slp[:, b, gi, 1:2],
                                                   slots(gi, b), ALU.is_equal, ALU.add)
                    l.then_inc(disp_ready, 1)
                dve.wait_ge(cT_done, pg * 2 + 2)
                v.tensor_copy(cT24[:, 1, :], bank[5][0:E1, :]).then_inc(cT_dve, 1)
                for m in range(1, 2 * NQ, 2):
                    gi, q = m // NQ, m % NQ
                    v.tensor_copy(xT[:, q * EQ:(q + 1) * EQ, gi, 0:CS],
                                  taken(U_DISP + m)[:, 0:EQ * CS].rearrange("p (e s) -> p e s", s=CS))\
                        .then_inc(evA_dve, 1)
                dve.wait_ge(gt_done, pg * 2 + 2)
                for gi in range(2):
                    l = v.tensor_copy(gf[:, gi].rearrange("p k f -> p (k f)"), bank[6 + gi][:, 0:NK * NF])
                link(l)
                for gi in range(2):
                    v.tensor_tensor(gt[:, gi, :], gf[:, gi, :, 6], ecol[:], ALU.is_equal)
                    v.tensor_reduce(gate[:, gi, :], gf[:, gi, :, 0:3], AX.X, ALU.add)
                    l = v.tensor_reduce(gs[:, gi, :], gf[:, gi, :, 3:6], AX.X, ALU.add)
                link(l)
                link(v.tensor_tensor(gate[:], gate[:], gt[:], ALU.mult))
                link(v.tensor_tensor(gt[:], gs[:], gt[:], ALU.mult))
                link(v.tensor_tensor(gs[:], gs[:], gt[:], ALU.subtract))
                v.tensor_tensor(gate[:], gate[:], gs[:], ALU.add).then_inc(gate_ready, 1)
                for e in range(1, E1, 2):
                    ps = taken(U_UP + e)
                    v.tensor_copy(hd2[RS:P, 0, e // 2, :], ps[0:RS, :])
                    v.tensor_copy(hd2[RS:P, 1, e // 2, :], ps[RS:P, :]).then_inc(evA_dve, 1)

                def rows(i, gi):
                    for k in range(1, NK, 2):
                        dve.wait_ge(dt_done, pg * 4 * NK + (i * NK + k + 1))
                        if k == 1:
                            dve.wait_ge(gate_ready, pg + 1)
                            if i:
                                dve.wait_ge(c1_done, pg * N_C1 + (0, TG, 2 * TG, 2 * TG + 1)[i])
                        v.tensor_scalar(dT[:, k, :], bank[5][:], gate[:, gi, k:k + 1], None, ALU.mult)\
                            .then_inc(dt_dve, 1)

                def moments(src, m):
                    for b, x in enumerate(src):
                        l = v.bn_stats(st6[:, b, :], x)
                    link(l)
                    v.tensor_copy(tick[:, 0:1], half[:, 0:1])
                    for b in range(len(src)):
                        l = v.bn_aggr(mv6[:, b, :], st6[:, b, :])
                    link(l)
                    k = len(src)
                    v.tensor_scalar(ve6[:, 0:k], mv6[:, 0:k, 1], 1e-6, None, ALU.add).then_inc(hv_ready, 1)
                    dve.wait_ge(hr_ready, pg * N_C1 + m + 1)

                for gi in range(2):
                    rows(gi, gi)
                    for b in range(TG):
                        m = gi * TG + b
                        dve.wait_ge(c1_done, pg * N_C1 + m + 1)
                        ps = bank[6 + b % 2]
                        moments([ps[:]], m)
                        v.tensor_scalar(ht[:, gi, b, :], ps[:], mv6[:, 0, 0:1], rs6[:, 0:1], ALU.subtract, ALU.mult)\
                            .then_inc(ht_ready, 1)
                for m in range(1, 2 * FC * NQ, 2):
                    gi, c, q = m // (FC * NQ), m // NQ % FC, m % NQ
                    r = gi * FC + c
                    o = d2T[:, c, q * EQ:(q + 1) * EQ, gi, 0:CS]
                    link(v.tensor_scalar(o, taken(U_D2 + m)[:, 0:EQ * CS].rearrange("p (e s) -> p e s", s=CS),
                                         lwp[:, r:r + 1], lbp[:, r:r + 1], ALU.mult, ALU.add))
                    v.tensor_scalar(o, o, 0.0, None, ALU.max).then_inc(evA_dve, 1)
                for q in range(1, E1 // 4, 2):
                    dve.wait_ge(w_used, pg * E1 + 4 * q + 4)
                    ps = bank[(U_DOWN + q) % 4][:].rearrange("p (k two d) -> p k two d", two=2, d=D)
                    for gi in range(2):
                        for par in range(2):
                            l = v.tensor_copy(yv[par * RS:(par + 1) * RS, gi, 2 * q:2 * q + 2, :],
                                              ps[gi * RS:(gi + 1) * RS, :, par, :])
                    l.then_inc(evA_dve, 1)
                for gi in range(2):
                    rows(2 + gi, gi)
                    dve.wait_ge(c1_done, pg * N_C1 + 2 * TG + gi + 1)
                    zb = ob[:, gi]
                    link(v.tensor_tensor(zb, bank[6 + gi][:].rearrange("p (b d) -> p b d", b=TG), ug[:, :, gi, :],
                                         ALU.add))
                    moments([zb[:, b, :] for b in range(TG)], 2 * TG + gi)
                    for b in range(TG):
                        l = v.tensor_scalar(zb[:, b, :], zb[:, b, :], mv6[:, b, 0:1], rs6[:, b:b + 1],
                                            ALU.subtract, ALU.mult)
                    link(l)
                    link(v.tensor_tensor(zb, zb, lnw[:].unsqueeze(1).to_broadcast([P, TG, D]), ALU.mult))
                    link(v.tensor_tensor(zb, zb, lnb[:].unsqueeze(1).to_broadcast([P, TG, D]), ALU.add))
                    v.tensor_tensor(ob[:, gi, :, :], zb, bg(x_all[:])[:, :, bass.ds(pg * 2 + gi, 1), :]
                                    .rearrange("p b g d -> p (b g) d"), ALU.add).then_inc(o_ready, 1)
                assert n[0] == VEC2_STEPS, n


def kernel(**inputs):
    import numpy as _np
    import concourse.bacc as _bacc
    from concourse import mybir as _mybir
    from concourse.bass_utils import run_bass_kernel_spmd as _run

    nc = _bacc.Bacc("TRN2", target_bir_lowering=False, num_devices=1)
    arrays, args = {}, {}
    for name, value in inputs.items():
        v = _np.ascontiguousarray(value)
        arrays[f"in_{name}_dram"] = v
        args[name] = nc.dram_tensor(f"in_{name}_dram", v.shape, _mybir.dt.from_np(v.dtype), kind="ExternalInput").ap()
    x = inputs["x"]
    out = nc.dram_tensor("out_0_dram", x.shape, _mybir.dt.from_np(_np.dtype("float32")), kind="ExternalOutput").ap()
    decoder(nc, args, out)
    r = _run(nc, [arrays], core_ids=[0])
    return r.results[0]["out_0_dram"]
```

```python
from contextlib import ExitStack

import concourse.bass as bass
from concourse import mybir

F32 = mybir.dt.float32
BF16 = mybir.dt.bfloat16
I32 = mybir.dt.int32
ALU = mybir.AluOpType
ACT = mybir.ActivationFunctionType
AX = mybir.AxisListType

P = 128


def decoder(nc, a, out, stop=None):
    B, S, D = a["x"].shape
    T = S // P
    H, DH = 16, 64
    NPAIR = H * DH // P
    FF = a["L0_attn_w1"].shape[1]
    FC = FF // P
    SK = a["ctx_1024"].shape[1]
    E0 = a["L0_ffn_W1"].shape[0]
    DI = a["L1_attn_conv_w"].shape[0]
    IC = DI // P
    KC = a["L1_attn_conv_w"].shape[2]
    NS = a["L1_attn_A_log"].shape[1]
    NX = 2 * NS + 1
    E1 = a["L1_ffn_W1"].shape[0]
    V1 = DH + 1
    SCALE0 = float(D) ** -0.5
    BIG = 3.0e38
    assert D == P and T == 4 and FC == 4 and NPAIR == 8 and S == 512

    with ExitStack() as ctx:
        def sb(name, shape, dt=F32, at=ctx):
            return at.enter_context(nc.sbuf_tensor(name, shape, dt))

        def sem(name):
            return ctx.enter_context(nc.semaphore(name))

        bank = [ctx.enter_context(nc.psum_tensor(f"bank{i}", [P, 512], F32)) for i in range(8)]

        x_all = sb("x_all", [P, B * T, D])
        u_all = sb("u_all", [P, B * T, D])
        ident = sb("ident", [P, P])
        NROWS = 78
        rows = sb("rows", [NROWS, P])
        cols = sb("cols", [P, NROWS])
        tick = sb("tick", [P, 2])
        half = sb("half", [P, T])
        R_AB1, R_EB1, R_G1, R_BE1, R_G2, R_BE2, R_BQ, R_BK, R_CB, R_DS, R_LW, R_LB = (
            0, 4, 36, 37, 38, 39, 40, 41, 42, 44, 46, 62)

        NR = 8
        ring = sb("ring", [P, NR, FF])
        slot_in = [sem(f"slot_in{k}") for k in range(NR)]

        ph = ctx.enter_context(ExitStack())

        def s1(name, shape, dt=F32):
            return sb(name, shape, dt, ph)

        def two(name, shape, dt=F32):
            return [s1(f"{name}_{q}", shape, dt) for q in range(2)]

        wqk = s1("wqk", [P, 2, H * DH])
        wv = s1("wv", [P, H * DH])
        wo = s1("wo", [P, NPAIR, D])
        w1 = s1("w1", [P, FF])
        w2 = s1("w2", [P, FC, D])
        projd = s1("projd", [P, P])
        b2bc = s1("b2bc", [P, D])
        e0w1 = s1("e0w1", [P, E0, FF])
        e0w2 = s1("e0w2", [P, E0, FC, D])
        e0b2 = s1("e0b2", [E0, D])
        e0wg = s1("e0wg", [P, E0])
        e0bg = s1("e0bg", [P, E0])
        win = s1("win", [P, 2 * DI])
        wxp = s1("wxp", [P, IC, NX])
        wout = s1("wout", [P, IC, D])
        convw = s1("convw", [P, IC, KC])
        mask = s1("mask", [P, 3 * P])
        ones_row = s1("ones_row", [1, P])
        iota8i = s1("iota8i", [P, T, E0], I32)
        iota8 = s1("iota8", [P, T, E0])
        kxT = s1("kxT", [P, 2, B * SK])
        sxA = s1("sxA", [P, 2, B * SK])
        sx0 = s1("sx0", [1, B * SK])
        vx = s1("vx", [SK, 2, B, D])
        x_in = two("x_in", [P, T, D])
        st = two("st", [P, T, 6])
        mv = two("mv", [P, T, 2])
        ve = two("ve", [P, T])
        rs = two("rs", [P, T])
        r2 = two("r2", [P, T])
        xn = two("xn", [P, T, D])
        xh = two("xh", [P, T, D])
        xs = two("xs", [P, T, D])
        xr = two("xr", [P, T, D])
        hT = two("hT", [P, S])
        v_tm = s1("v_tm", [P, T, H, V1])
        eb = s1("eb", [P, 2, S])
        rb = s1("rb", [P, 2, S])
        qT = s1("qT", [P, 2, S])
        kT = s1("kT", [P, 2, S])
        ktm = s1("ktm", [P, 2, P])
        kv = s1("kv", [P, 2 * V1])
        stm = s1("stm", [P, 2, 2, 3 * P])
        dn = s1("dn", [P, T])
        rd = s1("rd", [P, T])
        atm = s1("atm", [P, 2, T, P])
        big = s1("big", [P, 8, S])
        pd = two("pd", [P, T, SK])
        pp = two("pp", [P, T, SK])
        mx = two("mx", [P, T])
        sm = two("sm", [P, T])
        ri = two("ri", [P, T])
        lg = s1("lg", [P, T, E0])
        oh1 = two("oh1", [P, T, E0])
        oh2 = two("oh2", [P, T, E0])
        key = s1("key", [P, T, E0])
        l2 = s1("l2", [P, T, E0])
        m1 = two("m1", [P, T])
        m2 = two("m2", [P, T])
        mn = two("mn", [P, T])
        g1 = s1("g1", [P, T])
        g2 = two("g2", [P, T])
        comb = two("comb", [P, T, E0])
        xpad = two("xpad", [P, IC, S + KC - 1])
        ssm = two("ssm", [P, T, NX])
        sp_x = two("sp_x", [P, 8, T])
        dB = two("dB", [P, T, NS])
        yT = [kT, big[:, 6:8]]

        stm_f = stm[:].rearrange("p a c k -> p (a c k)")
        atm_f = atm[:].rearrange("p a t d -> p (a t d)")

        def part(flat, n, at, rows=P):
            return flat[0:rows, at:at + n]

        wx = part(stm_f, 6 * D, 0).rearrange("p (a d) -> p a d", a=6)
        ctx_in = part(stm_f, B * D, 6 * D, SK).rearrange("p (b d) -> p b d", b=B)
        bvbc = part(stm_f, D, 6 * D + B * D, SK)
        ctxT = part(atm_f, B * SK, 0)
        wxT = part(atm_f, 3 * D, B * SK).rearrange("p (a d) -> p a d", a=3)
        pT = [part(stm_f, S, q * S, SK) for q in range(2)]
        hmT = [part(stm_f, DI, 2 * S + q * DI, NS) for q in range(2)]
        combT = [part(atm_f, S, q * S, E0) for q in range(2)]
        cT = [part(atm_f, S, q * S, NS) for q in range(2)]
        cv = [eb, big[:, 0:2]]
        xc = [rb, big[:, 2:4]]
        sz = [qT, big[:, 4:6]]
        yT = [kT, big[:, 6:8]]
        xcT = [v_tm[:, :, 4 * q:4 * q + 4, 0:DH] for q in range(2)]

        w_in = sem("w_in")
        x_loaded = [sem(f"x_loaded_{q}") for q in range(2)]
        consts = sem("consts")
        pre_pe = sem("pre_pe")
        pre_act = sem("pre_act")
        vec = sem("vec")
        out_done = sem("out_done")
        names = ("var_ready rstd_ready ln_ready lnT_done hT_ready v_done v_act v_dve qk_done phi_parts phi_ready "
                 "kt_done ktm_ready state_done state_ready scores_done st_ready apply_done attn_evac atT_done atT_evac "
                 "y_done ff_done ff_ready sc_done sd_ready p_ready pT_done pT_ready lg_done comb_ready combT_done "
                 "combT_ready up_done up_act up_dve acc_done xz_done xp_ready cv_ready xc_ready sz_ready ssm_done ct_done "
                 "xcT_done xcT_ready ct_ready ssm_ready abs_ready u_ready w_ready l_ready db_ready hm_done hm_ready yt_done "
                 "yt_ready xs_ready xa_ready x_free md_ready me_ready x_kept neg_ready").split()
        in_turn = ("v_done v_act v_dve qk_done phi_parts phi_ready neg_ready kt_done ktm_ready state_done "
                           "state_ready scores_done st_ready apply_done attn_evac atT_done atT_evac ff_done ff_ready up_done "
                           "up_act up_dve acc_done combT_done combT_ready").split()
        s = {n: sem(n) if n in in_turn else [sem(f"{n}_{q}") for q in range(2)] for n in names}
        (var_ready, rstd_ready, ln_ready, lnT_done, hT_ready, v_done, v_act, v_dve, qk_done, phi_parts, phi_ready,
         kt_done, ktm_ready, state_done, state_ready, scores_done, st_ready, apply_done, attn_evac, atT_done, atT_evac,
         y_done, ff_done, ff_ready, sc_done, sd_ready, p_ready, pT_done, pT_ready, lg_done, comb_ready, combT_done,
         combT_ready, up_done, up_act, up_dve, acc_done, xz_done, xp_ready, cv_ready, xc_ready, sz_ready, ssm_done,
         ct_done, xcT_done, xcT_ready, ct_ready, ssm_ready, abs_ready, u_ready, w_ready, l_ready, db_ready, hm_done,
         hm_ready, yt_done, yt_ready, xs_ready, xa_ready, x_free, md_ready, me_ready, x_kept, neg_ready) = [s[n] for n in names]

        VEC_PRE, VEC_STEPS = 2, 190
        N_LN, N_LN_ALL, N_POW, N_Y = 6, 7, 8, 14
        LN_ATT, LN_FFN, LN_X0, LN_MOE, LN_SSM, LN_X1 = range(6)

        Y_WO, Y_FFN, Y_X0, Y_BIAS, Y_E, Y_SSM, Y_X1 = 0, 1, 2, 3, 4, 4 + E0, 5 + E0
        W_DMAS = 38

        ATTENTION, EXPERTS = 2, 4

        def at(pr, step, n, k):
            return (pr + step) * n + (k - step * n) if step else pr * n + k

        block = ph.enter_context(nc.Block())

        @block.sync
        def _(sp):
            n = [0]

            def load(dst, src):
                sp.dma_start(dst, src).then_inc(w_in, 16)
                n[0] += 1

            def vec_rows(r, v):
                k = v.shape[0] // P
                load(rows[r:r + k, :], v.rearrange("(c p) -> c p", p=P))

            for q in range(2):
                sp.dma_start(x_in[q][:], a["x"][q].rearrange("(t p) d -> p t d", p=P)).then_inc(x_loaded[q], 16)
            load(wqk[:, 0, :], a["L0_attn_wq"])
            load(wqk[:, 1, :], a["L0_attn_wk"])
            load(wv[:], a["L0_attn_wv"])
            sp.wait_ge(consts, 3)
            load(projd[0:DH, 0:DH], a["L0_attn_proj"])
            load(projd[DH:P, DH:P], a["L0_attn_proj"])
            vec_rows(R_AB1, a["L0_attn_b1"])
            load(rows[R_EB1:R_EB1 + E0 * FC, :], a["L0_ffn_b1"].rearrange("e (c p) -> (e c) p", p=P))
            vec_rows(R_G1, a["L0_attn_g1"])
            vec_rows(R_BE1, a["L0_attn_beta1"])
            vec_rows(R_G2, a["L0_attn_g2"])
            vec_rows(R_BE2, a["L0_attn_beta2"])
            vec_rows(R_BQ, a["L0_xattn_bq"])
            vec_rows(R_BK, a["L0_xattn_bk"])
            vec_rows(R_CB, a["L1_attn_conv_b"])
            vec_rows(R_DS, a["L1_attn_D"])
            load(rows[R_LW:R_LW + 16, :], a["L1_ffn_ln_hid_w"].rearrange("g (c p) -> (g c) p", p=P))
            load(rows[R_LB:R_LB + 16, :], a["L1_ffn_ln_hid_b"].rearrange("g (c p) -> (g c) p", p=P))
            load(ctx_in[:], a["ctx_1024"].rearrange("b k d -> k b d"))
            for i, name in enumerate(("L0_xattn_Wq", "L0_xattn_Wk", "L0_xattn_Wv",
                                      "L1_xattn_Wq", "L1_xattn_Wk", "L1_xattn_Wv")):
                load(wx[:, i, :], a[name])
            load(bvbc[:], a["L0_xattn_bv"].rearrange("(o d) -> o d", o=1).to_broadcast([SK, D]))
            load(b2bc[:], a["L0_attn_b2"].rearrange("(o d) -> o d", o=1).to_broadcast([P, D]))
            load(wo[:], a["L0_attn_wo"].rearrange("(j p) n -> p j n", p=P))
            load(w1[:], a["L0_attn_w1"])
            load(w2[:], a["L0_attn_w2"].rearrange("(c p) n -> p c n", p=P))
            load(e0w1[:], a["L0_ffn_W1"].rearrange("e d f -> d e f"))
            load(e0w2[:], a["L0_ffn_W2"].rearrange("e (c p) d -> p e c d", p=P))
            load(e0b2[:], a["L0_ffn_b2"])
            load(e0wg[:], a["L0_ffn_Wg"])
            load(e0bg[:], a["L0_ffn_bg"].rearrange("(o d) -> o d", o=1).to_broadcast([P, E0]))
            load(win[:], a["L1_attn_W_in"])
            load(wxp[:], a["L1_attn_W_xproj"].rearrange("(c p) n -> p c n", p=P))
            load(wout[:], a["L1_attn_W_out"].rearrange("(c p) n -> p c n", p=P))
            load(convw[:], a["L1_attn_conv_w"].rearrange("(c p) o k -> p c (o k)", p=P))
            assert n[0] == W_DMAS
            for k in range(NR):
                sp.dma_start(ring[:, k, :], a["L1_ffn_W1"][k]).then_inc(slot_in[k], 16)
            with sp.Fori(1, B // 2) as pr:
                for q in range(2):
                    sp.wait_ge(x_free[q], pr)
                    src = a["x"].rearrange("b (t p) d -> p b t d", p=P)[:, bass.ds(pr * 2 + q, 1), :, :]
                    sp.dma_start(x_in[q][:], src.rearrange("p b t d -> p (b t) d")).then_inc(x_loaded[q], 16)

        @block.gpsimd
        def _(pool):
            nc.gpsimd.memset(ident[:], 0.0).then_inc(consts, 1)
            nc.gpsimd.memset(mask[:], 1.0).then_inc(consts, 1)
            nc.gpsimd.memset(projd[:], 0.0).then_inc(consts, 1)
            pool.wait_ge(consts, 3)
            nc.gpsimd.affine_select(out=ident[:], in_=ident[:], compare_op=ALU.not_equal, fill=1.0, base=0,
                                    pattern=[[-1, P]], channel_multiplier=1)
            for c in (0, 2):
                nc.gpsimd.affine_select(out=mask[:, c * P:(c + 1) * P], in_=mask[:, c * P:(c + 1) * P],
                                        compare_op=ALU.is_ge, fill=0.0, base=0, pattern=[[1, P]],
                                        channel_multiplier=-1)
            nc.gpsimd.iota(iota8i[:], pattern=[[0, T], [1, E0]], base=0, channel_multiplier=0)
            nc.gpsimd.memset(ones_row[:], 1.0)
            nc.gpsimd.memset(half[:], -0.5)
            nc.gpsimd.memset(v_tm[:, :, :, DH:V1], 1.0)
            for q in range(2):
                l = nc.gpsimd.memset(xpad[q][:, :, 0:KC - 1], 0.0)
            l.then_inc(consts, 1)
            pool.wait_ge(consts, 4)
            pool.wait_ge(w_in, 16 * W_DMAS)
            with pool.Fori(0, B // 2) as pr:
                def inverse_root(q, k, dst):
                    pool.wait_ge(var_ready[q], at(pr, q, N_POW, k + 1))
                    nc.gpsimd.tensor_tensor(dst[:], ve[q][:], half[:], ALU.pow).then_inc(rstd_ready[q], 1)

                for q in range(2):
                    pool.wait_ge(x_loaded[q], at(pr, q, 16, 16))
                    nc.gpsimd.tensor_tensor(xs[q][:], x_in[q][:], b2bc[:].unsqueeze(1).to_broadcast([P, T, D]),
                                            ALU.add).then_inc(xs_ready[q], 1)
                    inverse_root(q, 0, rs[q])
                    inverse_root(q, 1, r2[q])
                for q in range(2):
                    pool.wait_ge(xa_ready[q], pr + 1)
                    pool.wait_ge(xs_ready[q], at(pr, q, 2, 1))
                    nc.gpsimd.tensor_tensor(xs[q][:], xs[q][:], xn[q][:], ALU.add).then_inc(xs_ready[q], 1)
                    inverse_root(q, 2, rs[q])
                for k in range(3, N_POW):
                    for q in range(2):
                        inverse_root(q, k, rs[q])

        @block.tensor
        def _(pe):
            mm, tr = nc.tensor.matmul, nc.tensor.transpose
            pe.wait_ge(w_in, 16 * W_DMAS)
            pe.wait_ge(consts, 4)
            tr(bank[7][:, 0:NROWS], rows[:], ident[0:NROWS, 0:NROWS]).then_inc(pre_pe, 1)
            for g in range(4):
                w, j0 = g // 2, 4 * (g % 2)
                for j in range(4):
                    l = tr(bank[g][:, j * P:(j + 1) * P], wqk[:, w, (j0 + j) * P:(j0 + j + 1) * P], ident[:])
                l.then_inc(pre_pe, 1)
            for g in range(4):
                pe.wait_ge(pre_act, 2 + g if g < 2 else 4 + g)
                for j in range(4):
                    l = mm(bank[4 + g % 2][:, j * P:(j + 1) * P], big[:, g, j * P:(j + 1) * P], projd[:],
                           start=True, stop=True)
                l.then_inc(pre_pe, 1)
            for b in range(B):
                l = tr(bank[0][:, b * SK:(b + 1) * SK], ctx_in[:, b, :], ident[0:SK, 0:SK])
            l.then_inc(pre_pe, 1)
            for i, w in enumerate((0, 4, 5)):
                l = tr(bank[1][:, i * P:(i + 1) * P], wx[:, w, :], ident[:])
            l.then_inc(pre_pe, 1)
            pe.wait_ge(pre_act, 11)
            mm(bank[2][:, 0:B * SK], wx[:, 1, :], ctxT[:], start=True, stop=True)
            mm(bank[3][:, 0:B * SK], wxT[:, 1, :], ctxT[:], start=True, stop=True).then_inc(pre_pe, 1)
            for i, w in enumerate((wx[:, 2, :], wxT[:, 2, :])):
                for b in range(B):
                    l = mm(bank[6 + i][0:SK, b * P:(b + 1) * P], ctxT[:, b * SK:(b + 1) * SK], w,
                           start=True, stop=True)
            l.then_inc(pre_pe, 1)
            pe.wait_ge(pre_act, 13)
            mm(bank[0][:, 0:B * SK], wxT[:, 0, :], kxT[:, 0, :], start=True, stop=True)
            mm(bank[1][:, 0:B * SK], wx[:, 3, :], kxT[:, 1, :], start=True, stop=True)
            mm(bank[2][0:1, 0:B * SK], cols[:, R_BQ:R_BQ + 1], kxT[:, 0, :], start=True, stop=True).then_inc(pre_pe, 1)
            pe.wait_ge(pre_act, 17)
            pe.wait_ge(vec, VEC_PRE)

            with pe.Fori(0, B // 2) as pr:
                ps_q, ps_k, ps_s, ps_o, ps_x, ps_t = bank[0], bank[1], bank[2:4], bank[4:6], bank[6], bank[7]
                four, y_bank = (*ps_s, *ps_o), (ps_q, ps_k)

                def to_features(q, k):
                    pe.wait_ge(ln_ready[q], at(pr, q, N_LN_ALL, k + 1))
                    for t in range(T):
                        l = tr(ps_t[:, t * P:(t + 1) * P], xh[q][:, t, :], ident[:])
                    l.then_inc(lnT_done[q], 1)
                    pe.wait_ge(hT_ready[q], at(pr, q, N_LN, k + 1))

                def down(q, dst, hid, w, n):
                    for t in range(T):
                        for c in range(n):
                            l = mm(dst[:, t * P:(t + 1) * P], hid[:, c, t * P:(t + 1) * P], w[:, c, :],
                                   start=(c == 0), stop=(c == n - 1))
                    l.then_inc(y_done[q], 1)

                def attention(q):
                    to_features(q, LN_ATT)
                    for n in range(2 * T):
                        t, h = n // 2, n % 2
                        if n >= 4:
                            pe.wait_ge((v_act, v_dve)[n % 2], at(pr, ATTENTION + q, 2 * T, q * T + (n - 4) // 2 + 1))
                        mm(four[n % 4][:], hT[q][:, t * P:(t + 1) * P], wv[:, h * 512:(h + 1) * 512],
                           start=True, stop=True).then_inc(v_done, 1)

                    def project(w, j):
                        if j:
                            pe.wait_ge(phi_ready, at(pr, ATTENTION + q, 2 * 2 * NPAIR, q * 2 * NPAIR + (2 * j - 1 + w)))
                        mm((ps_q, ps_k)[w][:], wqk[:, w, j * P:(j + 1) * P], hT[q][:], start=True, stop=True)\
                            .then_inc(qk_done, 1)

                    def scores(j, hh):
                        i, h0 = 2 * j + hh, hh * DH
                        r = slice(h0, h0 + DH)
                        if i == 0:
                            pe.wait_ge(v_act, at(pr, ATTENTION + q, 2 * T, q * T + T))
                            pe.wait_ge(v_dve, at(pr, ATTENTION + q, 2 * T, q * T + T))
                        else:
                            pe.wait_ge(st_ready, at(pr, ATTENTION + q, 2 * 2 * H, q * 2 * H + 2 * i))
                        pe.wait_ge(phi_ready, at(pr, ATTENTION + q, 2 * 2 * NPAIR, q * 2 * NPAIR + 2 * j + 2))
                        for c in range(2):
                            t0 = 2 * c * P
                            mm(ps_s[c][:, 0:2 * P], kT[r, j % 2, t0:t0 + P], qT[r, j % 2, t0:t0 + 2 * P],
                               start=True, stop=True)
                            mm(ps_s[c][:, 2 * P:3 * P], kT[r, j % 2, t0 + P:t0 + 2 * P],
                               qT[r, j % 2, t0 + P:t0 + 2 * P], start=True, stop=True).then_inc(scores_done, 1)

                    def keys_to_tokens(j):
                        if j:
                            pe.wait_ge(state_ready, at(pr, ATTENTION + q, 2 * NPAIR, q * NPAIR + j))
                        for t in range(2):
                            l = tr(ps_x[:, t * P:(t + 1) * P], kT[:, j % 2, t * P:(t + 1) * P], ident[:])
                        l.then_inc(kt_done, 1)

                    def state(j):
                        pe.wait_ge(ktm_ready, at(pr, ATTENTION + q, 2 * NPAIR, q * NPAIR + j + 1))
                        for t in range(2):
                            l = mm(ps_x[:, 2 * P:2 * P + 2 * V1], ktm[:, t, :],
                                   v_tm[:, t, 2 * j:2 * j + 2, :].rearrange("p h v -> p (h v)"),
                                   start=(t == 0), stop=(t == 1))
                        l.then_inc(state_done, 1)

                    def apply(j, hh):
                        i, h = 2 * j + hh, 2 * j + hh
                        r = slice(hh * DH, hh * DH + DH)
                        pe.wait_ge(st_ready, at(pr, ATTENTION + q, 2 * 2 * H, q * 2 * H + 2 * i + 2))
                        if hh == 0:
                            pe.wait_ge(state_ready, at(pr, ATTENTION + q, 2 * NPAIR, q * NPAIR + j + 1))
                        if j:
                            pe.wait_ge(attn_evac, at(pr, ATTENTION + q, 2 * H, q * H + i - 1))
                        for c in range(2):
                            for tt in range(2):
                                o = ps_o[hh][:, (2 * c + tt) * V1:(2 * c + tt + 1) * V1]
                                w = stm[:, i % 2, c, :]
                                l = mm(o, w[:, tt * P:(tt + 1) * P], v_tm[:, 2 * c, h, :],
                                       start=True, stop=(c == 0 and tt == 0))
                                if tt:
                                    l = mm(o, w[:, 2 * P:3 * P], v_tm[:, 2 * c + 1, h, :], start=False, stop=(c == 0))
                                if c:
                                    q0 = (2 * c + tt) * P
                                    l = mm(o, qT[r, j % 2, q0:q0 + P], kv[r, hh * V1:(hh + 1) * V1],
                                           start=False, stop=True)
                        l.then_inc(apply_done, 1)

                    def attn_to_features(j):
                        pe.wait_ge(attn_evac, at(pr, ATTENTION + q, 2 * 2 * NPAIR, q * 2 * NPAIR + 2 * j + 2))
                        if j:
                            pe.wait_ge(atT_evac, at(pr, ATTENTION + q, 2 * NPAIR, q * NPAIR + j))
                        for t in range(T):
                            l = tr(ps_t[:, t * P:(t + 1) * P], atm[:, j % 2, t, :], ident[:])
                        l.then_inc(atT_done, 1)

                    if q == 0:
                        project(0, 0)
                    else:
                        pe.wait_ge(xa_ready[0], pr + 1)
                        project(0, 0)
                    project(1, 0)
                    for j in range(NPAIR):
                        scores(j, 0)
                        keys_to_tokens(j)
                        if j + 1 < NPAIR:
                            project(0, j + 1)
                        scores(j, 1)
                        if j:
                            attn_to_features(j - 1)
                        state(j)
                        if j + 1 < NPAIR:
                            project(1, j + 1)
                        apply(j, 0)
                        apply(j, 1)
                    attn_to_features(NPAIR - 1)

                    pe.wait_ge(atT_evac, at(pr, ATTENTION + q, 2 * NPAIR, q * NPAIR + NPAIR))
                    down(q, y_bank[q], big, wo, NPAIR)

                def ffn(q):
                    to_features(q, LN_FFN)
                    for c in range(FC):
                        mm(four[c][:], w1[:, c * P:(c + 1) * P], hT[q][:], start=True, stop=True).then_inc(ff_done, 1)
                    pe.wait_ge(ff_ready, at(pr, ATTENTION + q, 2 * FC, q * FC + FC))
                    down(q, y_bank[q], big, w2, FC)

                def cross_scores(q, i):
                    to_features(q, (LN_X0, LN_X1)[i])
                    keys = sxA[:, i, :].rearrange("p (b k) -> p b k", b=B)[:, bass.ds(pr * 2 + q, 1), :]\
                        .rearrange("p b k -> p (b k)")
                    for t in range(T):
                        o = ps_s[q][:, t * SK:(t + 1) * SK]
                        l = mm(o, hT[q][:, t * P:(t + 1) * P], keys, start=True, stop=(i == 1))
                        if i == 0:
                            l = mm(o, ones_row[:], sx0[:].rearrange("p (b k) -> p b k", b=B)[:, bass.ds(pr * 2 + q, 1), :]
                                   .rearrange("p b k -> p (b k)"), start=False, stop=True)
                    l.then_inc(sc_done[q], 1)

                def cross_probs(q, i):
                    pe.wait_ge(p_ready[q], at(pr, q, 2, i + 1))
                    if q:
                        pe.wait_ge(pT_ready[0], pr * 2 + (i + 1))
                    for t in range(T):
                        l = tr(ps_t[0:SK, t * P:(t + 1) * P], pp[q][:, t, :], ident[:])
                    l.then_inc(pT_done[q], 1)

                def cross_values(q, i):
                    pe.wait_ge(pT_ready[q], at(pr, q, 2, i + 1))
                    vals = vx[:, i, bass.ds(pr * 2 + q, 1), :].rearrange("p b k -> p (b k)")
                    for t in range(T):
                        l = mm(y_bank[q][:, t * P:(t + 1) * P], pT[q][:, t * P:(t + 1) * P], vals, start=True, stop=True)
                    l.then_inc(y_done[q], 1)

                def router(q):
                    to_features(q, LN_MOE)
                    for t in range(T):
                        l = mm((ps_x, ps_k)[q][:, t * E0:(t + 1) * E0], hT[q][:, t * P:(t + 1) * P], e0wg[:], start=True, stop=True)
                    l.then_inc(lg_done[q], 1)

                def experts(q):
                    def up(e):
                        for c in range(FC):
                            if e:
                                pe.wait_ge((up_act, up_dve)[c % 2], at(pr, EXPERTS + q, 2 * 2 * E0, q * 2 * E0 + 2 * (e - 1) + c // 2 + 1))
                            mm(four[(c + 2) % 4][:], e0w1[:, e, c * P:(c + 1) * P], hT[q][:], start=True, stop=True)\
                                .then_inc(up_done, 1)

                    pe.wait_ge(comb_ready[q], pr + 1)
                    for t in range(T):
                        l = tr(ps_t[0:E0, t * P:(t + 1) * P], comb[q][:, t, :], ident[:])
                    l.then_inc(combT_done, 1)
                    up(0)
                    pe.wait_ge(combT_ready, pr * 2 + q + 1)
                    if q:
                        pe.wait_ge(acc_done, pr * (2 * E0) + E0)
                    for t in range(T):
                        l = mm(ps_q[:, t * P:(t + 1) * P], combT[q][:, t * P:(t + 1) * P], e0b2[:], start=True, stop=True)
                    l.then_inc(y_done[q], 1)
                    for e in range(E0):
                        if e + 1 < E0:
                            up(e + 1)
                        pe.wait_ge(up_act, at(pr, EXPERTS + q, 2 * 2 * E0, q * 2 * E0 + 2 * e + 2))
                        pe.wait_ge(up_dve, at(pr, EXPERTS + q, 2 * 2 * E0, q * 2 * E0 + 2 * e + 2))
                        if e:
                            pe.wait_ge(acc_done, at(pr, EXPERTS + q, 2 * E0, q * E0 + e))
                        down(q, (ps_k, ps_q)[e % 2], big[:, 4 * (e % 2):4 * (e % 2) + 4, :], e0w2[:, e], FC)

                def ssm_in(q):
                    to_features(q, LN_SSM)
                    if q:
                        pe.wait_ge(xp_ready[0], pr * IC + IC)
                        pe.wait_ge(sz_ready[0], pr * IC + IC)
                    for c in range(4):
                        mm(four[c][:], win[:, c * P:(c + 1) * P], hT[q][:], start=True, stop=True).then_inc(xz_done[q], 1)

                def ssm_proj(q):
                    pe.wait_ge(xc_ready[q], at(pr, q, IC, IC))
                    for t in range(T):
                        for c in range(IC):
                            l = mm((ps_x, ps_s[1])[q][:, t * NX:(t + 1) * NX], xc[q][:, c, t * P:(t + 1) * P], wxp[:, c, :],
                                   start=(c == 0), stop=(c == IC - 1))
                    l.then_inc(ssm_done[q], 1)
                    if q:
                        pe.wait_ge(xcT_ready[0], pr * IC + IC)
                        pe.wait_ge(ct_ready[0], pr + 1)
                    for c in range(IC):
                        for t in range(T):
                            l = tr((ps_t, ps_q)[c][:, t * P:(t + 1) * P], xc[q][:, c, t * P:(t + 1) * P], ident[:])
                    l.then_inc(xcT_done[q], 1)
                    for c in range(IC):
                        l = mm(ps_k[0:NS, :], wxp[:, c, 1 + NS:NX], xc[q][:, c, :], start=(c == 0), stop=(c == IC - 1))
                    l.then_inc(ct_done[q], 1)

                def ssm_mean(q):
                    pe.wait_ge(db_ready[q], pr + 1)
                    pe.wait_ge(xcT_ready[q], at(pr, q, IC, IC))
                    for t in range(T):
                        l = mm(ps_s[q][0:NS, 0:DI], dB[q][:, t, :], xcT[q][:, t, :, :], start=(t == 0), stop=(t == T - 1))
                    l.then_inc(hm_done[q], 1)

                def ssm_out(q):
                    pe.wait_ge(ct_ready[q], pr + 1)
                    pe.wait_ge(hm_ready[q], pr + 1)
                    pe.wait_ge(sz_ready[q], at(pr, q, IC, IC))
                    if q:
                        pe.wait_ge(yt_ready[0], pr * IC + IC)
                    for c in range(IC):
                        mm(ps_o[c][:], hmT[q][:, c * P:(c + 1) * P], cT[q][:], start=True, stop=True).then_inc(yt_done[q], 1)

                def ssm_down(q):
                    pe.wait_ge(yt_ready[q], at(pr, q, IC, IC))
                    down(q, y_bank[q], yT[q], wout, IC)
                for q in range(2):
                    attention(q)
                for q in range(2):
                    ffn(q)
                for q in range(2):
                    cross_scores(q, 0)
                for q in range(2):
                    cross_probs(q, 0)
                for q in range(2):
                    cross_values(q, 0)
                for q in range(2):
                    router(q)
                for q in range(2):
                    experts(q)
                for q in range(2):
                    ssm_in(q)
                for q in range(2):
                    ssm_proj(q)
                for q in range(2):
                    ssm_mean(q)
                for q in range(2):
                    ssm_out(q)
                for q in range(2):
                    ssm_down(q)
                for q in range(2):
                    cross_scores(q, 1)
                for q in range(2):
                    cross_probs(q, 1)
                for q in range(2):
                    cross_values(q, 1)

        @block.scalar
        def _(act):
            af = nc.scalar.activation
            n = [0]

            def pre(ins):
                n[0] += 1
                ins.then_inc(pre_act, 1)

            act.wait_ge(pre_pe, 1)
            pre(af(cols[:], bank[7][:, 0:NROWS], ACT.Copy))
            for g in range(4):
                act.wait_ge(pre_pe, 2 + g)
                pre(af(big[:, g, :], bank[g][:], ACT.Copy))
            for g in range(4):
                act.wait_ge(pre_pe, 6 + g)
                pre(af(wqk[:, g // 2, (g % 2) * 512:(g % 2) * 512 + 512], bank[4 + g % 2][:], ACT.Copy))
            act.wait_ge(pre_pe, 10)
            pre(af(ctxT[:], bank[0][:, 0:B * SK], ACT.Copy))
            act.wait_ge(pre_pe, 11)
            pre(af(wxT[:].rearrange("p a d -> p (a d)"), bank[1][:, 0:3 * D], ACT.Copy))
            act.wait_ge(pre_pe, 12)
            act.wait_ge(pre_act, 1)
            pre(af(kxT[:, 0, :], bank[2][:, 0:B * SK], ACT.Identity, bias=cols[:, R_BK:R_BK + 1]))
            pre(af(kxT[:, 1, :], bank[3][:, 0:B * SK], ACT.Copy))
            act.wait_ge(pre_pe, 13)
            pre(af(vx[:, 1, :, :].rearrange("p b d -> p (b d)"), bank[7][0:SK, :], ACT.Copy))
            act.wait_ge(pre_pe, 14)
            pre(af(sxA[:, 0, :], bank[0][:, 0:B * SK], ACT.Copy))
            pre(af(sxA[:, 1, :], bank[1][:, 0:B * SK], ACT.Copy))
            pre(af(sx0[:], bank[2][0:1, 0:B * SK], ACT.Copy))
            assert n[0] == 17

            with act.Fori(0, B // 2) as pr:
                ps_q, ps_k, ps_s, ps_o, ps_x, ps_t = bank[0], bank[1], bank[2:4], bank[4:6], bank[6], bank[7]
                four, y_bank = (*ps_s, *ps_o), (ps_q, ps_k)

                def features(q, k, g=None, be=None):
                    act.wait_ge(lnT_done[q], at(pr, q, N_LN, k + 1))
                    if g is None:
                        af(hT[q][:], ps_t[:], ACT.Copy).then_inc(hT_ready[q], 1)
                    else:
                        af(hT[q][:], ps_t[:], ACT.Identity, scale=cols[:, g:g + 1], bias=cols[:, be:be + 1])\
                            .then_inc(hT_ready[q], 1)

                def attention(q):
                    features(q, LN_ATT, R_G1, R_BE1)
                    for t in range(T):
                        act.wait_ge(v_done, at(pr, ATTENTION + q, 2 * 2 * T, q * 2 * T + 2 * t + 1))
                        af(v_tm[:, t, 0:H // 2, 0:DH], four[2 * t % 4][:].rearrange("p (h d) -> p h d", d=DH),
                           ACT.Copy).then_inc(v_act, 1)

                    def parts(w, j):
                        m = 2 * j + w
                        act.wait_ge(qk_done, at(pr, ATTENTION + q, 2 * 2 * NPAIR, q * 2 * NPAIR + m + 1))
                        if m >= 2:
                            act.wait_ge(phi_ready, at(pr, ATTENTION + q, 2 * 2 * NPAIR, q * 2 * NPAIR + m - 1))
                        af(rb[:, m % 2, :], (ps_q, ps_k)[w][:], ACT.Relu, scale=-1.0).then_inc(neg_ready, 1)
                        act.wait_ge(neg_ready, at(pr, ATTENTION + q, 2 * 2 * NPAIR, q * 2 * NPAIR + m + 1))
                        af(eb[:, m % 2, :], rb[:, m % 2, :], ACT.Exp, scale=-1.0).then_inc(phi_parts, 1)

                    parts(0, 0)
                    parts(1, 0)
                    for j in range(NPAIR):
                        act.wait_ge(kt_done, at(pr, ATTENTION + q, 2 * NPAIR, q * NPAIR + j + 1))
                        af(ktm[:], ps_x[:, 0:2 * P].rearrange("p (t d) -> p t d", t=2), ACT.Copy).then_inc(ktm_ready, 1)
                        if j + 1 < NPAIR:
                            parts(0, j + 1)
                        if j:
                            act.wait_ge(atT_done, at(pr, ATTENTION + q, 2 * NPAIR, q * NPAIR + j))
                            af(big[:, j - 1, :], ps_t[:], ACT.Copy).then_inc(atT_evac, 1)
                        act.wait_ge(state_done, at(pr, ATTENTION + q, 2 * NPAIR, q * NPAIR + j + 1))
                        if j:
                            act.wait_ge(apply_done, at(pr, ATTENTION + q, 2 * H, q * H + 2 * j))
                        af(kv[:], ps_x[:, 2 * P:2 * P + 2 * V1], ACT.Copy).then_inc(state_ready, 1)
                        if j + 1 < NPAIR:
                            parts(1, j + 1)
                    act.wait_ge(atT_done, at(pr, ATTENTION + q, 2 * NPAIR, q * NPAIR + NPAIR))
                    af(big[:, NPAIR - 1, :], ps_t[:], ACT.Copy).then_inc(atT_evac, 1)

                def ffn(q):
                    features(q, LN_FFN, R_G2, R_BE2)
                    for c in range(FC):
                        act.wait_ge(ff_done, at(pr, ATTENTION + q, 2 * FC, q * FC + c + 1))
                        af(big[:, c, :], four[c][:], ACT.Gelu, bias=cols[:, R_AB1 + c:R_AB1 + c + 1]).then_inc(ff_ready, 1)

                def cross_scores(q, i):
                    features(q, (LN_X0, LN_X1)[i])

                def cross_softmax(q, i):
                    act.wait_ge(sd_ready[q], at(pr, q, 2, i + 1))
                    af(pp[q][:], pd[q][:], ACT.Exp, scale=SCALE0).then_inc(p_ready[q], 1)

                def cross_probs(q, i):
                    act.wait_ge(pT_done[q], at(pr, q, 2, i + 1))
                    af(pT[q][:], ps_t[0:SK, :], ACT.Copy).then_inc(pT_ready[q], 1)

                def router(q):
                    features(q, LN_MOE)

                def router_weights(q):
                    act.wait_ge(md_ready[q], pr + 1)
                    af(g2[q][:], mn[q][:], ACT.Exp).then_inc(me_ready[q], 1)

                def experts(q):
                    act.wait_ge(combT_done, pr * 2 + q + 1)
                    af(combT[q][:], ps_t[0:E0, :], ACT.Copy).then_inc(combT_ready, 1)
                    for e in range(E0):
                        for c in (0, 2):
                            act.wait_ge(up_done, at(pr, EXPERTS + q, 2 * FC * E0, q * FC * E0 + FC * e + c + 1))
                            if e >= 2:
                                act.wait_ge(y_done[q], at(pr, q, N_Y, Y_E + e - 1))
                            r = R_EB1 + FC * e + c
                            af(big[:, 4 * (e % 2) + c, :], four[(c + 2) % 4][:], ACT.Relu, bias=cols[:, r:r + 1])\
                                .then_inc(up_act, 1)

                def ssm_in(q):
                    features(q, LN_SSM)
                    for c in range(IC):
                        act.wait_ge(xz_done[q], at(pr, q, 4, c + 1))
                        af(xpad[q][:, c, KC - 1:], four[c][:], ACT.Copy).then_inc(xp_ready[q], 1)
                    for c in range(IC):
                        act.wait_ge(xz_done[q], at(pr, q, 4, IC + c + 1))
                        af(sz[q][:, c, :], four[IC + c][:], ACT.Silu).then_inc(sz_ready[q], 1)

                def ssm_conv(q):
                    for c in range(IC):
                        act.wait_ge(cv_ready[q], at(pr, q, IC, c + 1))
                        af(xc[q][:, c, :], cv[q][:, c, :], ACT.Silu).then_inc(xc_ready[q], 1)

                def ssm_proj(q):
                    act.wait_ge(xcT_done[q], pr + 1)
                    for c in range(IC):
                        af(xcT[q][:, :, 2 * c:2 * c + 2, :], (ps_t, ps_q)[c][:].rearrange("p (t h d) -> p t h d", t=T, d=DH),
                           ACT.Copy).then_inc(xcT_ready[q], 1)
                    act.wait_ge(ct_done[q], pr + 1)
                    af(cT[q][:], ps_k[0:NS, :], ACT.Copy).then_inc(ct_ready[q], 1)

                def ssm_mean(q):
                    act.wait_ge(abs_ready[q], pr + 1)
                    af(sp_x[q][:, 2, :], sp_x[q][:, 1, :], ACT.Exp).then_inc(u_ready[q], 1)
                    act.wait_ge(w_ready[q], pr + 1)
                    af(sp_x[q][:, 4, :], sp_x[q][:, 3, :], ACT.Ln).then_inc(l_ready[q], 1)

                def ssm_out(q):
                    act.wait_ge(hm_done[q], pr + 1)
                    af(hmT[q][:], ps_s[q][0:NS, 0:DI], ACT.Copy).then_inc(hm_ready[q], 1)

                def keep(q):
                    act.wait_ge(ln_ready[q], at(pr, q, N_LN_ALL, N_LN_ALL))
                    af(x_all[:, bass.ds(pr * (2 * T) + q * T, T), :], xr[q][:], ACT.Copy)
                    af(u_all[:, bass.ds(pr * (2 * T) + q * T, T), :], xh[q][:], ACT.Copy).then_inc(x_kept[q], 1)
                for q in range(2):
                    attention(q)
                for q in range(2):
                    ffn(q)
                for q in range(2):
                    cross_scores(q, 0)
                for q in range(2):
                    cross_softmax(q, 0)
                for q in range(2):
                    cross_probs(q, 0)
                for q in range(2):
                    router(q)
                for q in range(2):
                    router_weights(q)
                for q in range(2):
                    experts(q)
                for q in range(2):
                    ssm_in(q)
                for q in range(2):
                    ssm_conv(q)
                for q in range(2):
                    ssm_proj(q)
                for q in range(2):
                    ssm_mean(q)
                for q in range(2):
                    ssm_out(q)
                for q in range(2):
                    cross_scores(q, 1)
                for q in range(2):
                    cross_softmax(q, 1)
                for q in range(2):
                    cross_probs(q, 1)
                for q in range(2):
                    keep(q)

        @block.vector
        def _(dve):
            v = nc.vector
            n = [0]

            dve.wait_ge(consts, 4)
            v.tensor_copy(iota8[:], iota8i[:]).then_inc(vec, 1)
            dve.wait_ge(pre_pe, 13)
            v.tensor_tensor(vx[:, 0, :, :], bank[6][0:SK, :].rearrange("p (b d) -> p b d", b=B),
                            bvbc[:].unsqueeze(1).to_broadcast([SK, B, D]), ALU.add).then_inc(vec, 1)
            dve.wait_ge(vec, VEC_PRE)

            with dve.Fori(0, B // 2) as pr:
                ps_q, ps_k, ps_s, ps_o, ps_x, ps_t = bank[0], bank[1], bank[2:4], bank[4:6], bank[6], bank[7]
                four, y_bank = (*ps_s, *ps_o), (ps_q, ps_k)

                def link(ins):
                    n[0] += 1
                    ins.then_inc(vec, 1)
                    dve.wait_ge(vec, pr * VEC_STEPS + VEC_PRE + n[0])

                def tiles(ps):
                    return ps[:].rearrange("p (t d) -> p t d", t=T)

                def over(col, w):
                    return col.unsqueeze(2).to_broadcast([P, T, w])

                def moments(q, src, eps=1e-5):
                    for t in range(T):
                        l = v.bn_stats(st[q][:, t, :], src[:, t, :])
                    link(l)
                    v.tensor_copy(tick[:, 0:1], half[:, 0:1])
                    for t in range(T):
                        l = v.bn_aggr(mv[q][:, t, :], st[q][:, t, :])
                    link(l)
                    v.tensor_scalar(ve[q][:], mv[q][:, :, 1], eps, None, ALU.add).then_inc(var_ready[q], 1)

                def normalize(q, dst, src, k):
                    dve.wait_ge(rstd_ready[q], at(pr, q, N_POW, k + 1))
                    for t in range(T):
                        l = v.tensor_scalar(dst[:, t, :], src[:, t, :], mv[q][:, t, 0:1], rs[q][:, t:t + 1],
                                            ALU.subtract, ALU.mult)
                    return l

                def ln_in(q):
                    dve.wait_ge(x_loaded[q], at(pr, q, 16, 16))
                    moments(q, x_in[q])
                    link(normalize(q, xn[q], x_in[q], 0))
                    dve.wait_ge(xs_ready[q], at(pr, q, 2, 1))
                    v.tensor_tensor(r2[q][:], mv[q][:, :, 1], rs[q][:], ALU.mult).then_inc(x_free[q], 1)
                    dve.wait_ge(x_free[q], pr + 1)
                    link(v.tensor_tensor(r2[q][:], r2[q][:], rs[q][:], ALU.mult))
                    v.tensor_scalar(ve[q][:], r2[q][:], 1e-5, None, ALU.add).then_inc(var_ready[q], 1)
                    dve.wait_ge(rstd_ready[q], at(pr, q, N_POW, 2))
                    for t in range(T):
                        l = v.tensor_scalar(xh[q][:, t, :], xn[q][:, t, :], r2[q][:, t:t + 1], None, ALU.mult)
                    l.then_inc(ln_ready[q], 1)

                def attention(q):
                    for t in range(T):
                        dve.wait_ge(v_done, at(pr, ATTENTION + q, 2 * 2 * T, q * 2 * T + 2 * t + 2))
                        v.tensor_copy(v_tm[:, t, H // 2:H, 0:DH], four[(2 * t + 1) % 4][:]
                                      .rearrange("p (h d) -> p h d", d=DH)).then_inc(v_dve, 1)

                    def phi(w, j):
                        m = 2 * j + w
                        dve.wait_ge(phi_parts, at(pr, ATTENTION + q, 2 * 2 * NPAIR, q * 2 * NPAIR + m + 1))
                        if j >= 2:
                            dve.wait_ge(apply_done, at(pr, ATTENTION + q, 2 * H, q * H + 2 * (j - 1)))
                        v.scalar_tensor_tensor((qT, kT)[w][:, j % 2, :], (ps_q, ps_k)[w][:], 0.0, eb[:, m % 2, :],
                                               ALU.max, ALU.add).then_inc(phi_ready, 1)

                    def causal(i):
                        if i >= 2:
                            dve.wait_ge(apply_done, at(pr, ATTENTION + q, 2 * H, q * H + i - 1))
                        for c in range(2):
                            dve.wait_ge(scores_done, at(pr, ATTENTION + q, 2 * 2 * H, q * 2 * H + 2 * i + c + 1))
                            v.tensor_tensor(stm[:, i % 2, c, :], ps_s[c][:, 0:3 * P], mask[:], ALU.mult)\
                                .then_inc(st_ready, 1)

                    def attn_out(i):
                        j, hh = i // 2, i % 2
                        dve.wait_ge(apply_done, at(pr, ATTENTION + q, 2 * H, q * H + i + 1))
                        if j >= 2:
                            dve.wait_ge(atT_done, at(pr, ATTENTION + q, 2 * NPAIR, q * NPAIR + j - 1))
                        o = ps_o[hh][:, 0:T * V1].rearrange("p (t e) -> p t e", e=V1)
                        link(v.tensor_scalar(dn[:], o[:, :, DH], 1e-6, None, ALU.add))
                        link(v.reciprocal(rd[:], dn[:]))
                        v.tensor_tensor(atm[:, j % 2, :, hh * DH:(hh + 1) * DH], o[:, :, 0:DH], over(rd[:], DH),
                                        ALU.mult).then_inc(attn_evac, 1)

                    phi(0, 0)
                    phi(1, 0)
                    for j in range(NPAIR):
                        causal(2 * j)
                        if j + 1 < NPAIR:
                            phi(0, j + 1)
                        causal(2 * j + 1)
                        if j + 1 < NPAIR:
                            phi(1, j + 1)
                        attn_out(2 * j)
                        attn_out(2 * j + 1)

                    dve.wait_ge(y_done[q], at(pr, q, N_Y, Y_WO + 1))
                    v.tensor_tensor(xn[q][:], tiles(y_bank[q]), xn[q][:], ALU.add).then_inc(xa_ready[q], 1)
                    dve.wait_ge(xa_ready[q], pr + 1)
                    moments(q, xn[q])
                    normalize(q, xh[q], xn[q], 2).then_inc(ln_ready[q], 1)

                def ffn(q):
                    dve.wait_ge(y_done[q], at(pr, q, N_Y, Y_FFN + 1))
                    dve.wait_ge(xs_ready[q], at(pr, q, 2, 2))
                    link(v.tensor_tensor(xr[q][:], tiles(y_bank[q]), xs[q][:], ALU.add))
                    moments(q, xr[q])
                    normalize(q, xh[q], xr[q], 3).then_inc(ln_ready[q], 1)

                def cross_scores(q, i):
                    dve.wait_ge(sc_done[q], at(pr, q, 2, i + 1))
                    sc = ps_s[q][:, 0:T * SK].rearrange("p (t k) -> p t k", t=T)
                    link(v.tensor_reduce(mx[q][:], sc, AX.X, ALU.max))
                    v.tensor_tensor(pd[q][:], sc, over(mx[q][:], SK), ALU.subtract).then_inc(sd_ready[q], 1)

                def cross_probs(q, i):
                    dve.wait_ge(p_ready[q], at(pr, q, 2, i + 1))
                    link(v.tensor_reduce(sm[q][:], pp[q][:], AX.X, ALU.add))
                    link(v.reciprocal(ri[q][:], sm[q][:]))

                def cross_values(q, i):
                    dve.wait_ge(y_done[q], at(pr, q, N_Y, (Y_X0, Y_X1)[i] + 1))
                    for t in range(T):
                        l = v.scalar_tensor_tensor(xr[q][:, t, :], y_bank[q][:, t * P:(t + 1) * P], ri[q][:, t:t + 1],
                                                   xr[q][:, t, :], ALU.mult, ALU.add)
                    link(l)
                    moments(q, xr[q])
                    normalize(q, xh[q], xr[q], (4, 7)[i]).then_inc(ln_ready[q], 1)

                def router(q):
                    dve.wait_ge(lg_done[q], pr + 1)
                    link(v.tensor_tensor(lg[:], (ps_x, ps_k)[q][:, 0:T * E0].rearrange("p (t e) -> p t e", t=T),
                                         e0bg[:].unsqueeze(1).to_broadcast([P, T, E0]), ALU.add))

                    def argmax(src, top, onehot):
                        link(v.tensor_reduce(top[:], src[:], AX.X, ALU.max))
                        link(v.tensor_tensor(key[:], src[:], over(top[:], E0), ALU.is_equal))
                        link(v.scalar_tensor_tensor(key[:], key[:], -64.0, iota8[:], ALU.mult, ALU.add))
                        link(v.tensor_reduce(mn[q][:], key[:], AX.X, ALU.min))
                        link(v.tensor_tensor(onehot[:], key[:], over(mn[q][:], E0), ALU.is_equal))

                    argmax(lg, m1[q], oh1[q])
                    link(v.scalar_tensor_tensor(l2[:], oh1[q][:], -BIG, lg[:], ALU.mult, ALU.add))
                    argmax(l2, m2[q], oh2[q])
                    v.tensor_tensor(mn[q][:], m2[q][:], m1[q][:], ALU.subtract).then_inc(md_ready[q], 1)

                def router_weights(q):
                    dve.wait_ge(me_ready[q], pr + 1)
                    link(v.tensor_scalar(m1[q][:], g2[q][:], 1.0, None, ALU.add))
                    link(v.reciprocal(g1[:], m1[q][:]))
                    link(v.tensor_tensor(g2[q][:], g2[q][:], g1[:], ALU.mult))
                    v.tensor_tensor(comb[q][:], oh1[q][:], over(g1[:], E0), ALU.mult)
                    link(v.tensor_tensor(key[:], oh2[q][:], over(g2[q][:], E0), ALU.mult))
                    v.tensor_tensor(comb[q][:], comb[q][:], key[:], ALU.add).then_inc(comb_ready[q], 1)
                    dve.wait_ge(comb_ready[q], pr + 1)

                def experts(q):
                    def hidden(e):
                        for c in (1, 3):
                            dve.wait_ge(up_done, at(pr, EXPERTS + q, 2 * FC * E0, q * FC * E0 + FC * e + c + 1))
                            if e >= 2:
                                dve.wait_ge(y_done[q], at(pr, q, N_Y, Y_E + e - 1))
                            r = R_EB1 + FC * e + c
                            v.tensor_scalar(big[:, 4 * (e % 2) + c, :], four[(c + 2) % 4][:], cols[:, r:r + 1], 0.0,
                                            ALU.add, ALU.max).then_inc(up_dve, 1)

                    hidden(0)
                    dve.wait_ge(y_done[q], at(pr, q, N_Y, Y_BIAS + 1))
                    link(v.tensor_tensor(xr[q][:], tiles(ps_q), xr[q][:], ALU.add))
                    for e in range(E0):
                        if e + 1 < E0:
                            hidden(e + 1)
                        dve.wait_ge(y_done[q], at(pr, q, N_Y, Y_E + e + 1))
                        for t in range(T):
                            l = v.scalar_tensor_tensor(xr[q][:, t, :], (ps_k, ps_q)[e % 2][:, t * P:(t + 1) * P],
                                                       comb[q][:, t, e:e + 1], xr[q][:, t, :], ALU.mult, ALU.add)
                        l.then_inc(acc_done, 1)
                        dve.wait_ge(acc_done, at(pr, EXPERTS + q, 2 * E0, q * E0 + e + 1))

                    moments(q, xr[q])
                    normalize(q, xh[q], xr[q], 5).then_inc(ln_ready[q], 1)

                def ssm_conv(q):
                    for c in range(IC):
                        dve.wait_ge(xp_ready[q], at(pr, q, IC, c + 1))
                        r = R_CB + c
                        link(v.tensor_scalar(cv[q][:, c, :], xpad[q][:, c, KC - 1:KC - 1 + S], convw[:, c, KC - 1:KC],
                                             cols[:, r:r + 1], ALU.mult, ALU.add))
                        for k in range(KC - 1):
                            l = v.scalar_tensor_tensor(cv[q][:, c, :], xpad[q][:, c, k:k + S], convw[:, c, k:k + 1],
                                                       cv[q][:, c, :], ALU.mult, ALU.add)
                            if k < KC - 2:
                                link(l)
                        l.then_inc(cv_ready[q], 1)

                def ssm_proj(q):
                    dve.wait_ge(ssm_done[q], pr + 1)
                    link(v.tensor_copy(ssm[q][:].rearrange("p t n -> p (t n)"), (ps_x, ps_s[1])[q][:, 0:T * NX]))
                    x0, neg, u, w, ln, d, z, dl = ssm[q][:, :, 0], *(sp_x[q][:, i, :] for i in (0, 2, 3, 4, 5, 6, 7))
                    link(v.tensor_scalar(neg, x0, -1.0, None, ALU.mult))
                    v.tensor_tensor(sp_x[q][:, 1, :], x0, neg, ALU.min).then_inc(abs_ready[q], 1)
                    dve.wait_ge(u_ready[q], pr + 1)
                    v.tensor_scalar(w, u, 1.0, None, ALU.add).then_inc(w_ready[q], 1)
                    dve.wait_ge(w_ready[q], pr + 1)
                    link(v.tensor_scalar(d, w, -1.0, None, ALU.add))
                    link(v.tensor_scalar(z, d, 0.0, None, ALU.is_equal))
                    link(v.tensor_tensor(d, d, z, ALU.add))
                    link(v.reciprocal(neg, d))
                    link(v.tensor_tensor(neg, neg, u, ALU.mult))
                    link(v.tensor_tensor(z, z, u, ALU.mult))
                    dve.wait_ge(l_ready[q], pr + 1)
                    link(v.tensor_tensor(ln, ln, neg, ALU.mult))
                    link(v.tensor_tensor(ln, ln, z, ALU.add))
                    link(v.scalar_tensor_tensor(dl, x0, 0.0, ln, ALU.max, ALU.add))
                    link(v.tensor_scalar(dl, dl, 1.0 / S, None, ALU.mult))
                    v.tensor_tensor(dB[q][:], ssm[q][:, :, 1:1 + NS], over(dl, NS), ALU.mult).then_inc(db_ready[q], 1)

                def ssm_out(q):
                    for c in range(IC):
                        dve.wait_ge(yt_done[q], at(pr, q, IC, c + 1))
                        r = R_DS + c
                        link(v.scalar_tensor_tensor(yT[q][:, c, :], xc[q][:, c, :], cols[:, r:r + 1], ps_o[c][:],
                                                    ALU.mult, ALU.add))
                        v.tensor_tensor(yT[q][:, c, :], yT[q][:, c, :], sz[q][:, c, :], ALU.mult).then_inc(yt_ready[q], 1)

                def ssm_down(q):
                    dve.wait_ge(y_done[q], at(pr, q, N_Y, Y_SSM + 1))
                    link(v.tensor_tensor(xr[q][:], tiles(y_bank[q]), xr[q][:], ALU.add))
                    moments(q, xr[q])
                    normalize(q, xh[q], xr[q], 6).then_inc(ln_ready[q], 1)

                def kept(q):
                    dve.wait_ge(x_kept[q], pr + 1)
                for q in range(2):
                    ln_in(q)
                for q in range(2):
                    attention(q)
                for q in range(2):
                    ffn(q)
                for q in range(2):
                    cross_scores(q, 0)
                for q in range(2):
                    cross_probs(q, 0)
                for q in range(2):
                    cross_values(q, 0)
                for q in range(2):
                    router(q)
                for q in range(2):
                    router_weights(q)
                for q in range(2):
                    experts(q)
                for q in range(2):
                    ssm_conv(q)
                for q in range(2):
                    ssm_proj(q)
                for q in range(2):
                    ssm_out(q)
                for q in range(2):
                    ssm_down(q)
                for q in range(2):
                    cross_scores(q, 1)
                for q in range(2):
                    cross_probs(q, 1)
                for q in range(2):
                    cross_values(q, 1)
                for q in range(2):
                    kept(q)
                assert n[0] == VEC_STEPS, n

        ph.close()
        NG = T
        NT = B * T
        TG = B
        CAP = -(-2 * (B * S // NG) // E1)
        CS = CAP + CAP % 2
        RS = P // 2
        NK = E1 // 2
        EQ = 8
        NQ = E1 // EQ
        WS = E1 * CS
        NF = 7
        assert CS <= RS and EQ * CS <= 512 and NG % 2 == 0

        hd = sb("hd", [P, 2 * NK * FF])
        disp = sb("disp", [P, 2, TG, E1 * RS])
        dT = sb("dT", [P, NK, TG * P])
        xT = sb("xT", [P, E1, 2, RS])
        ht = sb("ht", [P, 2, TG, FF])
        ug = sb("ug", [P, TG, 2, D])
        iw = sb("iw", [P, WS])
        cT24 = sb("cT24", [E1, 2, TG * P])
        b124 = sb("b124", [E1, FF])
        b224 = sb("b224", [E1, D])
        lnw = sb("lnw", [P, D])
        lnb = sb("lnb", [P, D])
        wg24 = sb("wg24", [P, E1])
        comb24 = sb("comb24", [P, NT, E1])
        combp = sb("combp", [P, TG, 2, E1])
        sl = sb("sl", [P, NT, 2])
        slp = sb("slp", [P, TG, 2, 2])
        ft = sb("ft", [P, NT, NF], BF16)
        ftp = sb("ftp", [P, TG, 2, NF], BF16)
        lwp = sb("lwp", [P, 2 * FC])
        lbp = sb("lbp", [P, 2 * FC])
        ecol = sb("ecol", [P, NK])
        gf = sb("gf", [P, 2, NK, NF])
        gs = sb("gs", [P, 2, NK])
        gt = sb("gt", [P, 2, NK])
        gate = sb("gate", [P, 2, NK])
        tri = sb("tri", [P, P], BF16)
        one = sb("one", [P, P], BF16)
        st6 = sb("st6", [P, TG, 6])
        mv6 = sb("mv6", [P, TG, 2])
        ve6 = sb("ve6", [P, TG])
        rs6 = sb("rs6", [P, TG])
        ob = sb("ob", [P, 2, TG, D])
        sv = sb("sv", [P, 16, NT])

        hd2 = hd[:].rearrange("p (g k f) -> p g k f", g=2, k=NK)
        d2T = hd[:].rearrange("p (c e g s) -> p c e g s", c=FC, e=E1, g=2)
        yv = ht[:].rearrange("p g t f -> p (g t f)")[:, 0:2 * NK * D].rearrange("p (g k d) -> p g k d", g=2, k=NK)
        uT = hd[:, 0:NT * P]
        TW = NT * E1
        tmp = [hd[:, NT * P + i * TW:NT * P + (i + 1) * TW].rearrange("p (t e) -> p t e", e=E1) for i in range(6)]
        h0 = NT * P + 6 * TW
        i24 = hd[:, h0:h0 + TW].rearrange("p (t e) -> p t e", e=E1)
        i24i = hd[:, h0 + TW:h0 + 2 * TW].bitcast(I32).rearrange("p (t e) -> p t e", e=E1)
        eci = hd[:, h0 + 2 * TW:h0 + 2 * TW + NK].bitcast(I32)
        h1 = h0 + 3 * TW + WS
        oh1b, oh2b = (hd[:, h1 + i * TW:h1 + i * TW + TW // 2].bitcast(BF16).rearrange("p (t e) -> p t e", e=E1)
                      for i in range(2))
        iwi = hd[:, h0 + 3 * TW:h0 + 3 * TW + WS].bitcast(I32)

        def slots(gi, b):
            return disp[:, gi, b, :].rearrange("p (e s) -> p e s", s=RS)[:, :, 0:CS]

        names = ("w2_in k2 uT_done uT_act uT_dve lg2_done lgd_ready lge_ready oh_ready loc_done pair_act pair_dve "
                 "disp_ready cT_done cT_act cT_dve pA evA_act evA_dve gt_done gate_ready dt_done dt_act dt_dve "
                 "c1_done hv_ready hr_ready ht_ready pads_ready w_used o_ready r2_ready vec2").split()
        (w2_in, k2, uT_done, uT_act, uT_dve, lg2_done, lgd_ready, lge_ready, oh_ready, loc_done, pair_act, pair_dve,
         disp_ready, cT_done, cT_act, cT_dve, pA, evA_act, evA_dve, gt_done, gate_ready, dt_done, dt_act, dt_dve,
         c1_done, hv_ready, hr_ready, ht_ready, pads_ready, w_used, o_ready, r2_ready, vec2) = [
             sem(x) for x in names]
        NP2 = NG // 2
        U_DISP, U_UP = 0, 2 * NQ
        U_D2 = U_UP + E1
        U_DOWN = U_D2 + 2 * FC * NQ
        U_ALL = U_DOWN + E1 // 4
        VEC2_PRE, VEC2_STEPS = 46, 47
        N_C1 = 2 * TG + 2
        assert U_UP % 2 == 0 and U_D2 % 2 == 0 and U_DOWN % 2 == 0 and U_ALL % 2 == 0
        bg = lambda x: x.rearrange("p (b g) d -> p b g d", g=NG)

        block2 = ctx.enter_context(nc.Block())

        @block2.sync
        def _(sp):
            for dst, src in ((b124[:], a["L1_ffn_b1"]), (b224[:], a["L1_ffn_b2"]), (wg24[:], a["L1_ffn_Wg"]),
                             (lnw[:], a["L1_ffn_ln_out_w"].rearrange("(o d) -> o d", o=1).to_broadcast([P, D])),
                             (lnb[:], a["L1_ffn_ln_out_b"].rearrange("(o d) -> o d", o=1).to_broadcast([P, D]))):
                sp.dma_start(dst, src).then_inc(w2_in, 16)
            NC = E1 // NR
            w_dram = (a["L1_ffn_W1"].rearrange("e d f -> d e f"),
                      a["L1_ffn_W2"].rearrange("e (c p) d -> p e c d", p=P))

            def load(kind, e, k):
                if kind == 0:
                    src, dst = w_dram[0][:, bass.ds(e, 1), :], ring[:, k:k + 1, :]
                else:
                    src = w_dram[1][:, bass.ds(e, 1), :, :].rearrange("p e c d -> p (e c) d")
                    dst = ring[:, k, :].rearrange("p (c d) -> p c d", c=FC)
                sp.dma_start(dst, src).then_inc(slot_in[k], 16)

            for pair in range(NP2):
                for kind in range(2):
                    used, base = ((pA, pair * U_DOWN + U_UP), (w_used, pair * E1))[kind]
                    if pair or kind:
                        before, last = ((w_used, pair * E1), (pA, pair * U_DOWN + U_UP + E1))[kind]
                        for k in range(NR):
                            sp.wait_ge(before, last - NR + k + 1)
                            load(kind, k, k)
                    with sp.Fori(1, NC) as c:
                        for k in range(NR):
                            sp.wait_ge(used, c * NR + (base - NR + k + 1))
                            load(kind, c * NR + k, k)

        @block2.gpsimd
        def _(pool):
            g_ = nc.gpsimd
            g_.iota(iwi, pattern=[[1, WS]], base=0, channel_multiplier=0)
            g_.iota(eci[0:RS], pattern=[[2, NK]], base=0, channel_multiplier=0).then_inc(k2, 1)
            pool.wait_ge(k2, 1)
            g_.iota(eci[RS:P], pattern=[[2, NK]], base=1, channel_multiplier=0).then_inc(k2, 1)
            pool.wait_ge(k2, 2)
            g_.iota(i24i, pattern=[[0, NT], [1, E1]], base=0, channel_multiplier=0)
            g_.memset(one[:], 1.0)
            g_.memset(tri[:], 1.0).then_inc(k2, 1)
            pool.wait_ge(k2, 3)
            g_.affine_select(out=tri[:], in_=tri[:], compare_op=ALU.is_gt, fill=0.0, base=0, pattern=[[1, P]],
                             channel_multiplier=-1)
            g_.memset(xT[:, :, :, CS:RS], 0.0)
            for gi in range(2):
                for b in range(TG):
                    l = g_.memset(disp[:, gi, b, :].rearrange("p (e s) -> p e s", s=RS)[:, :, CS:RS], 0.0)
            l.then_inc(k2, 1)
            with pool.Fori(0, NP2) as pg:
                for m in range(2 * TG):
                    pool.wait_ge(hv_ready, pg * (2 * TG + 2) + (m + 1))
                    g_.tensor_tensor(rs6[:, 0:1], ve6[:, 0:1], half[:, 0:1], ALU.pow).then_inc(hr_ready, 1)
                pool.wait_ge(c1_done, pg * N_C1 + 2 * TG)
                g_.tensor_tensor(tick[:, 1:2], half[:, 0:1], half[:, 0:1], ALU.add)
                g_.memset(d2T[:, :, :, :, CS:RS].rearrange("p c e g s -> p (c e g) s"), 0.0).then_inc(pads_ready, 1)
                for m in range(2):
                    pool.wait_ge(hv_ready, pg * (2 * TG + 2) + (2 * TG + m + 1))
                    g_.tensor_tensor(rs6[:], ve6[:], half[:, 0:TG], ALU.pow).then_inc(hr_ready, 1)

        @block2.tensor
        def _(pe):
            mm, tr = nc.tensor.matmul, nc.tensor.transpose
            for i in range(NT // 4):
                for j in range(4):
                    l = tr(bank[i][:, j * P:(j + 1) * P], u_all[:, 4 * i + j, :], ident[:])
                l.then_inc(uT_done, 1)
            pe.wait_ge(w2_in, 16 * 5)
            pe.wait_ge(uT_act, 2)
            pe.wait_ge(uT_dve, 2)
            for t in range(NT):
                l = mm(bank[4][:, t * E1:(t + 1) * E1], uT[:, t * P:(t + 1) * P], wg24[:], start=True, stop=True)
            l.then_inc(lg2_done, 1)
            pe.wait_ge(oh_ready, 1)
            pe.wait_ge(k2, 4)
            W = NG * E1
            flat = [x.rearrange("p t e -> p (t e)") for x in (oh1b, oh2b)]
            for which in range(2):
                for t in range(TG):
                    terms = [(tri, which, t)] + [(one, which, p) for p in range(t)]
                    terms += [(one, 0, p) for p in range(TG)] if which else []
                    for i, (m, c, p) in enumerate(terms):
                        l = mm(bank[5 + which][:, t * W:(t + 1) * W], m[:], flat[c][:, p * W:(p + 1) * W],
                               start=(i == 0), stop=(i == len(terms) - 1))
            l.then_inc(loc_done, 1)
            pe.wait_ge(r2_ready, 1)

            with pe.Fori(0, NP2) as pg:
                def bank_a(u):
                    if u >= 4:
                        pe.wait_ge((evA_act, evA_dve)[u % 2], pg * (U_ALL // 2) + (u - 4) // 2 + 1)
                    return bank[u % 4]

                pe.wait_ge(pair_act, pg + 1)
                pe.wait_ge(pair_dve, pg + 1)
                for gi in range(2):
                    for b in range(TG):
                        l = tr(bank[4 + gi][0:E1, b * P:(b + 1) * P], combp[:, b, gi, :], ident[:])
                    l.then_inc(cT_done, 1)
                for gi in range(2):
                    pe.wait_ge(disp_ready, pg * 2 + gi + 1)
                    for q in range(NQ):
                        ps = bank_a(U_DISP + gi * NQ + q)
                        for b in range(TG):
                            l = mm(ps[:, 0:EQ * CS], ug[:, b, gi, :], slots(gi, b)[:, q * EQ:(q + 1) * EQ, :],
                                   start=(b == 0), stop=(b == TG - 1))
                        l.then_inc(pA, 1)
                for gi in range(2):
                    for k in range(NK):
                        for b in range(TG):
                            hot = disp[:, gi, b, :].bitcast(BF16).rearrange("p (s h) -> p s h", h=2)[:, :, 1]
                            l = mm(bank[6 + gi][:, k * NF:(k + 1) * NF], hot[:, k * P:(k + 1) * P], ftp[:, b, gi, :],
                                   start=(b == 0), stop=(b == TG - 1))
                    l.then_inc(gt_done, 1)
                pe.wait_ge(evA_act, pg * (U_ALL // 2) + U_UP // 2)
                pe.wait_ge(evA_dve, pg * (U_ALL // 2) + U_UP // 2)
                for e in range(E1):
                    ps = bank_a(U_UP + e)
                    pe.wait_ge(slot_in[e % NR], (pg * (2 * E1 // NR) + (e // NR + 1)) * 16)
                    mm(ps[:], xT[:, e, :, :], ring[:, e % NR, :], start=True, stop=True).then_inc(pA, 1)

                def slots_to_rows(i, gi):
                    for k in range(NK):
                        m = i * NK + k
                        if i == 0 and k < 2:
                            pe.wait_ge((cT_act, cT_dve)[k], pg + 1)
                        elif k < 2:
                            pe.wait_ge((dt_act, dt_dve)[k], pg * 2 * NK + i * NK // 2)
                        else:
                            pe.wait_ge((dt_act, dt_dve)[k % 2], pg * 2 * NK + (m - 2) // 2 + 1)
                        for b in range(TG):
                            l = tr(bank[4 + k % 2][:, b * P:(b + 1) * P], disp[:, gi, b, k * P:(k + 1) * P], ident[:])
                        l.then_inc(dt_done, 1)
                    pe.wait_ge(dt_act, pg * 2 * NK + (i + 1) * NK // 2)
                    pe.wait_ge(dt_dve, pg * 2 * NK + (i + 1) * NK // 2)

                for gi in range(2):
                    slots_to_rows(gi, gi)
                    if gi == 0:
                        pe.wait_ge(gate_ready, pg + 1)
                        pe.wait_ge(evA_act, pg * (U_ALL // 2) + U_D2 // 2)
                        pe.wait_ge(evA_dve, pg * (U_ALL // 2) + U_D2 // 2)
                    for b in range(TG):
                        m = gi * TG + b
                        if m >= 2:
                            pe.wait_ge(ht_ready, pg * 2 * TG + m - 1)
                        ps = bank[6 + b % 2]
                        mm(ps[:], cT24[:, gi, b * P:(b + 1) * P], b124[:], start=True, stop=False)
                        for k in range(NK):
                            l = mm(ps[:], dT[:, k, b * P:(b + 1) * P], hd2[:, gi, k, :], start=False, stop=(k == NK - 1))
                        l.then_inc(c1_done, 1)
                for gi in range(2):
                    pe.wait_ge(ht_ready, pg * 2 * TG + (gi + 1) * TG)
                    for c in range(FC):
                        for q in range(NQ):
                            ps = bank_a(U_D2 + (gi * FC + c) * NQ + q)
                            for b in range(TG):
                                l = mm(ps[:, 0:EQ * CS], ht[:, gi, b, c * P:(c + 1) * P],
                                       slots(gi, b)[:, q * EQ:(q + 1) * EQ, :], start=(b == 0), stop=(b == TG - 1))
                            l.then_inc(pA, 1)
                pe.wait_ge(evA_act, pg * (U_ALL // 2) + U_DOWN // 2)
                pe.wait_ge(evA_dve, pg * (U_ALL // 2) + U_DOWN // 2)
                pe.wait_ge(pads_ready, pg + 1)
                for e in range(E1):
                    if e % 4 == 0:
                        ps = bank_a(U_DOWN + e // 4)
                    pe.wait_ge(slot_in[e % NR], (pg * (2 * E1 // NR) + (E1 // NR + e // NR + 1)) * 16)
                    for c in range(FC):
                        l = mm(ps[:, (e % 4) * P:(e % 4 + 1) * P], d2T[:, c, e, :, :],
                               ring[:, e % NR, c * P:(c + 1) * P], start=(c == 0), stop=(c == FC - 1))
                    l.then_inc(w_used, 1)
                for gi in range(2):
                    slots_to_rows(2 + gi, gi)
                    if gi == 0:
                        pe.wait_ge(evA_act, pg * (U_ALL // 2) + U_ALL // 2)
                        pe.wait_ge(evA_dve, pg * (U_ALL // 2) + U_ALL // 2)
                    ps = bank[6 + gi]
                    for b in range(TG):
                        o = ps[:, b * P:(b + 1) * P]
                        mm(o, cT24[:, gi, b * P:(b + 1) * P], b224[:], start=True, stop=False)
                        for k in range(NK):
                            l = mm(o, dT[:, k, b * P:(b + 1) * P], yv[:, gi, k, :], start=False, stop=(k == NK - 1))
                    l.then_inc(c1_done, 1)

        @block2.scalar
        def _(act):
            af = nc.scalar.activation
            for i in (0, 2):
                act.wait_ge(uT_done, i + 1)
                af(uT[:, i * 512:(i + 1) * 512], bank[i][:], ACT.Copy).then_inc(uT_act, 1)
            act.wait_ge(lgd_ready, 1)
            af(tmp[4], tmp[4], ACT.Exp)
            af(sv[:, 4, :], sv[:, 4, :], ACT.Exp).then_inc(lge_ready, 1)

            with act.Fori(0, NP2) as pg:
                two = bass.ds(pg * 2, 2)

                def taken(u):
                    act.wait_ge(pA, pg * U_DOWN + u + 1)
                    return bank[u % 4]

                act.wait_ge(r2_ready, 1)
                af(ug[:], bg(u_all[:])[:, :, two, :], ACT.Copy).then_inc(pair_act, 1)
                act.wait_ge(cT_done, pg * 2 + 1)
                af(cT24[:, 0, :], bank[4][0:E1, :], ACT.Copy).then_inc(cT_act, 1)
                for n in range(0, 2 * NQ, 2):
                    gi, q = n // NQ, n % NQ
                    af(xT[:, q * EQ:(q + 1) * EQ, gi, 0:CS],
                       taken(U_DISP + n)[:, 0:EQ * CS].rearrange("p (e s) -> p e s", s=CS), ACT.Copy).then_inc(evA_act, 1)
                for e in range(0, E1, 2):
                    ps = taken(U_UP + e)
                    af(hd2[0:RS, 0, e // 2, :], ps[0:RS, :], ACT.Copy)
                    af(hd2[0:RS, 1, e // 2, :], ps[RS:P, :], ACT.Copy).then_inc(evA_act, 1)

                def rows(i, gi):
                    for k in range(0, NK, 2):
                        act.wait_ge(dt_done, pg * 4 * NK + (i * NK + k + 1))
                        if k == 0:
                            act.wait_ge(gate_ready, pg + 1)
                            if i:
                                act.wait_ge(c1_done, pg * N_C1 + (0, TG, 2 * TG, 2 * TG + 1)[i])
                        af(dT[:, k, :], bank[4][:], ACT.Copy, scale=gate[:, gi, k:k + 1]).then_inc(dt_act, 1)

                rows(0, 0)
                rows(1, 1)
                act.wait_ge(c1_done, pg * N_C1 + 2 * TG)
                for n in range(0, 2 * FC * NQ, 2):
                    gi, c, q = n // (FC * NQ), n // NQ % FC, n % NQ
                    r = gi * FC + c
                    af(d2T[:, c, q * EQ:(q + 1) * EQ, gi, 0:CS],
                       taken(U_D2 + n)[:, 0:EQ * CS].rearrange("p (e s) -> p e s", s=CS), ACT.Relu,
                       scale=lwp[:, r:r + 1], bias=lbp[:, r:r + 1]).then_inc(evA_act, 1)

                def outputs_of_experts(q):
                    act.wait_ge(w_used, pg * E1 + 4 * q + 4)
                    ps = bank[(U_DOWN + q) % 4][:].rearrange("p (k two d) -> p k two d", two=2, d=D)
                    for gi in range(2):
                        for par in range(2):
                            l = af(yv[par * RS:(par + 1) * RS, gi, 2 * q:2 * q + 2, :],
                                   ps[gi * RS:(gi + 1) * RS, :, par, :], ACT.Copy)
                    l.then_inc(evA_act, 1)

                for q in range(0, E1 // 4, 2):
                    outputs_of_experts(q)
                for gi in range(2):
                    rows(2 + gi, gi)
                for gi in range(2):
                    act.wait_ge(o_ready, pg * 2 + gi + 1)
                    dst = out.rearrange("b (g p) d -> p b g d", p=P)[:, :, bass.ds(pg * 2 + gi, 1), :]\
                        .rearrange("p b g d -> p (b g) d")
                    act.dma_start(dst, ob[:, gi, :, :]).then_inc(out_done, 16)
                act.wait_ge(out_done, pg * 32 + 32)

        @block2.vector
        def _(dve):
            v = nc.vector
            n = [0]

            def link0(ins):
                n[0] += 1
                ins.then_inc(vec2, 1)
                dve.wait_ge(vec2, n[0])

            def wide(col, w=E1):
                return col.unsqueeze(2).to_broadcast([P, NT, w])

            for i in (1, 3):
                dve.wait_ge(uT_done, i + 1)
                v.tensor_copy(uT[:, i * 512:(i + 1) * 512], bank[i][:]).then_inc(uT_dve, 1)
            lgs, key, oh1, oh2, ex, l2 = tmp
            m1, m2, n1, n2, e21, ssum, p1, p2, pos1, pos2, k1, k2_, den, t0, t1, t2 = (sv[:, i, :] for i in range(16))
            dve.wait_ge(k2, 4)
            v.tensor_copy(iw[:], iwi)
            v.tensor_copy(ecol[:], eci)
            link0(v.tensor_copy(i24, i24i))
            dve.wait_ge(lg2_done, 1)
            link0(v.tensor_copy(lgs, bank[4][:, 0:NT * E1].rearrange("p (t e) -> p t e", e=E1)))

            def argmax(src, top, idx, onehot):
                link0(v.tensor_reduce(top, src, AX.X, ALU.max))
                link0(v.tensor_tensor(key, src, wide(top), ALU.is_equal))
                link0(v.scalar_tensor_tensor(key, key, -64.0, i24, ALU.mult, ALU.add))
                link0(v.tensor_reduce(idx, key, AX.X, ALU.min))
                link0(v.tensor_tensor(onehot, key, wide(idx), ALU.is_equal))

            argmax(lgs, m1, n1, oh1)
            link0(v.scalar_tensor_tensor(l2, oh1, -BIG, lgs, ALU.mult, ALU.add))
            argmax(l2, m2, n2, oh2)
            v.tensor_copy(oh1b, oh1)
            v.tensor_copy(oh2b, oh2).then_inc(oh_ready, 1)
            v.tensor_tensor(ex, lgs, wide(m1), ALU.subtract)
            v.tensor_tensor(e21, m2, m1, ALU.subtract).then_inc(lgd_ready, 1)
            dve.wait_ge(lge_ready, 1)
            link0(v.tensor_reduce(ssum, ex, AX.X, ALU.add))
            link0(v.reciprocal(p1, ssum))
            link0(v.tensor_tensor(p2, p1, e21, ALU.mult))
            dve.wait_ge(loc_done, 1)
            for i, (oh, pos, kp, pr, idx) in enumerate(((oh1, pos1, k1, p1, n1), (oh2, pos2, k2_, p2, n2))):
                loc = bank[5 + i][:, 0:NT * E1].rearrange("p (t e) -> p t e", e=E1)
                link0(v.tensor_tensor(key, loc, oh, ALU.mult))
                link0(v.tensor_reduce(pos, key, AX.X, ALU.add))
                link0(v.tensor_scalar(kp, pos, float(CAP), None, ALU.is_lt))
                link0(v.scalar_tensor_tensor(t0, idx, float(CS), pos, ALU.mult, ALU.add))
                link0(v.tensor_scalar(t0, t0, float(64 * CS + 1), None, ALU.add))
                link0(v.tensor_tensor(t0, t0, kp, ALU.mult))
                v.tensor_scalar(sl[:, :, i], t0, -1.0, None, ALU.add)
                link0(v.tensor_tensor(pr, pr, kp, ALU.mult))
            link0(v.tensor_tensor(den, p1, p2, ALU.add))
            link0(v.tensor_scalar(den, den, 1e-9, None, ALU.max))
            link0(v.reciprocal(t0, den))
            v.tensor_tensor(p1, p1, t0, ALU.mult)
            link0(v.tensor_tensor(p2, p2, t0, ALU.mult))
            v.tensor_tensor(comb24[:], oh1, wide(p1), ALU.mult)
            link0(v.tensor_tensor(key, oh2, wide(p2), ALU.mult))
            v.tensor_tensor(comb24[:], comb24[:], key, ALU.add)
            link0(v.tensor_scalar(ft[:, :, 6], n1, 64.0, None, ALU.add))
            for i, g in enumerate((p1, p2)):
                link0(v.tensor_copy(ft[:, :, 3 * i], g))
                link0(v.tensor_tensor(t1, g, ft[:, :, 3 * i], ALU.subtract))
                link0(v.tensor_copy(ft[:, :, 3 * i + 1], t1))
                link0(v.tensor_tensor(t2, t1, ft[:, :, 3 * i + 1], ALU.subtract))
                link0(v.tensor_copy(ft[:, :, 3 * i + 2], t2))
            v.tensor_copy(t1, t2).then_inc(r2_ready, 1)
            dve.wait_ge(r2_ready, 1)
            assert n[0] == VEC2_PRE, n
            n[0] = 0

            with dve.Fori(0, NP2) as pg:
                two = bass.ds(pg * 2, 2)

                def link(ins):
                    n[0] += 1
                    ins.then_inc(vec2, 1)
                    dve.wait_ge(vec2, pg * VEC2_STEPS + VEC2_PRE + n[0])

                def taken(u):
                    dve.wait_ge(pA, pg * U_DOWN + u + 1)
                    return bank[u % 4]

                def over(col, w):
                    return col.unsqueeze(2).to_broadcast([P, TG, w])

                v.tensor_copy(slp[:], bg(sl[:])[:, :, two, :])
                v.tensor_copy(ftp[:], bg(ft[:])[:, :, two, :])
                v.tensor_copy(lwp[:], cols[:, R_LW:R_LW + NG * FC].rearrange("p (g c) -> p g c", c=FC)[:, two, :]
                              .rearrange("p g c -> p (g c)"))
                v.tensor_copy(lbp[:], cols[:, R_LB:R_LB + NG * FC].rearrange("p (g c) -> p g c", c=FC)[:, two, :]
                              .rearrange("p g c -> p (g c)"))
                v.tensor_copy(combp[:], bg(comb24[:])[:, :, two, :]).then_inc(pair_dve, 1)
                dve.wait_ge(pair_dve, pg + 1)
                for gi in range(2):
                    for b in range(TG):
                        l = v.tensor_scalar(slots(gi, b), iw[:].rearrange("p (e s) -> p e s", s=CS), slp[:, b, gi, 0:1], None, ALU.is_equal)
                    link(l)
                    for b in range(TG):
                        l = v.scalar_tensor_tensor(slots(gi, b), iw[:].rearrange("p (e s) -> p e s", s=CS), slp[:, b, gi, 1:2],
                                                   slots(gi, b), ALU.is_equal, ALU.add)
                    l.then_inc(disp_ready, 1)
                dve.wait_ge(cT_done, pg * 2 + 2)
                v.tensor_copy(cT24[:, 1, :], bank[5][0:E1, :]).then_inc(cT_dve, 1)
                for m in range(1, 2 * NQ, 2):
                    gi, q = m // NQ, m % NQ
                    v.tensor_copy(xT[:, q * EQ:(q + 1) * EQ, gi, 0:CS],
                                  taken(U_DISP + m)[:, 0:EQ * CS].rearrange("p (e s) -> p e s", s=CS))\
                        .then_inc(evA_dve, 1)
                dve.wait_ge(gt_done, pg * 2 + 2)
                for gi in range(2):
                    l = v.tensor_copy(gf[:, gi].rearrange("p k f -> p (k f)"), bank[6 + gi][:, 0:NK * NF])
                link(l)
                for gi in range(2):
                    v.tensor_tensor(gt[:, gi, :], gf[:, gi, :, 6], ecol[:], ALU.is_equal)
                    v.tensor_reduce(gate[:, gi, :], gf[:, gi, :, 0:3], AX.X, ALU.add)
                    l = v.tensor_reduce(gs[:, gi, :], gf[:, gi, :, 3:6], AX.X, ALU.add)
                link(l)
                link(v.tensor_tensor(gate[:], gate[:], gt[:], ALU.mult))
                link(v.tensor_tensor(gt[:], gs[:], gt[:], ALU.mult))
                link(v.tensor_tensor(gs[:], gs[:], gt[:], ALU.subtract))
                v.tensor_tensor(gate[:], gate[:], gs[:], ALU.add).then_inc(gate_ready, 1)
                for e in range(1, E1, 2):
                    ps = taken(U_UP + e)
                    v.tensor_copy(hd2[RS:P, 0, e // 2, :], ps[0:RS, :])
                    v.tensor_copy(hd2[RS:P, 1, e // 2, :], ps[RS:P, :]).then_inc(evA_dve, 1)

                def rows(i, gi):
                    for k in range(1, NK, 2):
                        dve.wait_ge(dt_done, pg * 4 * NK + (i * NK + k + 1))
                        if k == 1:
                            dve.wait_ge(gate_ready, pg + 1)
                            if i:
                                dve.wait_ge(c1_done, pg * N_C1 + (0, TG, 2 * TG, 2 * TG + 1)[i])
                        v.tensor_scalar(dT[:, k, :], bank[5][:], gate[:, gi, k:k + 1], None, ALU.mult)\
                            .then_inc(dt_dve, 1)

                def moments(src, m):
                    for b, x in enumerate(src):
                        l = v.bn_stats(st6[:, b, :], x)
                    link(l)
                    v.tensor_copy(tick[:, 0:1], half[:, 0:1])
                    for b in range(len(src)):
                        l = v.bn_aggr(mv6[:, b, :], st6[:, b, :])
                    link(l)
                    k = len(src)
                    v.tensor_scalar(ve6[:, 0:k], mv6[:, 0:k, 1], 1e-6, None, ALU.add).then_inc(hv_ready, 1)
                    dve.wait_ge(hr_ready, pg * N_C1 + m + 1)

                for gi in range(2):
                    rows(gi, gi)
                    for b in range(TG):
                        m = gi * TG + b
                        dve.wait_ge(c1_done, pg * N_C1 + m + 1)
                        ps = bank[6 + b % 2]
                        moments([ps[:]], m)
                        v.tensor_scalar(ht[:, gi, b, :], ps[:], mv6[:, 0, 0:1], rs6[:, 0:1], ALU.subtract, ALU.mult)\
                            .then_inc(ht_ready, 1)
                for m in range(1, 2 * FC * NQ, 2):
                    gi, c, q = m // (FC * NQ), m // NQ % FC, m % NQ
                    r = gi * FC + c
                    o = d2T[:, c, q * EQ:(q + 1) * EQ, gi, 0:CS]
                    link(v.tensor_scalar(o, taken(U_D2 + m)[:, 0:EQ * CS].rearrange("p (e s) -> p e s", s=CS),
                                         lwp[:, r:r + 1], lbp[:, r:r + 1], ALU.mult, ALU.add))
                    v.tensor_scalar(o, o, 0.0, None, ALU.max).then_inc(evA_dve, 1)
                for q in range(1, E1 // 4, 2):
                    dve.wait_ge(w_used, pg * E1 + 4 * q + 4)
                    ps = bank[(U_DOWN + q) % 4][:].rearrange("p (k two d) -> p k two d", two=2, d=D)
                    for gi in range(2):
                        for par in range(2):
                            l = v.tensor_copy(yv[par * RS:(par + 1) * RS, gi, 2 * q:2 * q + 2, :],
                                              ps[gi * RS:(gi + 1) * RS, :, par, :])
                    l.then_inc(evA_dve, 1)
                for gi in range(2):
                    rows(2 + gi, gi)
                    dve.wait_ge(c1_done, pg * N_C1 + 2 * TG + gi + 1)
                    zb = ob[:, gi]
                    link(v.tensor_tensor(zb, bank[6 + gi][:].rearrange("p (b d) -> p b d", b=TG), ug[:, :, gi, :],
                                         ALU.add))
                    moments([zb[:, b, :] for b in range(TG)], 2 * TG + gi)
                    for b in range(TG):
                        l = v.tensor_scalar(zb[:, b, :], zb[:, b, :], mv6[:, b, 0:1], rs6[:, b:b + 1],
                                            ALU.subtract, ALU.mult)
                    link(l)
                    link(v.tensor_tensor(zb, zb, lnw[:].unsqueeze(1).to_broadcast([P, TG, D]), ALU.mult))
                    link(v.tensor_tensor(zb, zb, lnb[:].unsqueeze(1).to_broadcast([P, TG, D]), ALU.add))
                    v.tensor_tensor(ob[:, gi, :, :], zb, bg(x_all[:])[:, :, bass.ds(pg * 2 + gi, 1), :]
                                    .rearrange("p b g d -> p (b g) d"), ALU.add).then_inc(o_ready, 1)
                assert n[0] == VEC2_STEPS, n


def kernel(**inputs):
    import numpy as _np
    import concourse.bacc as _bacc
    from concourse import mybir as _mybir
    from concourse.bass_utils import run_bass_kernel_spmd as _run

    nc = _bacc.Bacc("TRN2", target_bir_lowering=False, num_devices=1)
    arrays, args = {}, {}
    for name, value in inputs.items():
        v = _np.ascontiguousarray(value)
        arrays[f"in_{name}_dram"] = v
        args[name] = nc.dram_tensor(f"in_{name}_dram", v.shape, _mybir.dt.from_np(v.dtype), kind="ExternalInput").ap()
    x = inputs["x"]
    out = nc.dram_tensor("out_0_dram", x.shape, _mybir.dt.from_np(_np.dtype("float32")), kind="ExternalOutput").ap()
    decoder(nc, args, out)
    r = _run(nc, [arrays], core_ids=[0])
    return r.results[0]["out_0_dram"]
```

```python
from contextlib import ExitStack

import concourse.bass as bass
from concourse import mybir

F32 = mybir.dt.float32
BF16 = mybir.dt.bfloat16
F32R = mybir.dt.float32r
I32 = mybir.dt.int32
ALU = mybir.AluOpType
ACT = mybir.ActivationFunctionType
AX = mybir.AxisListType

P = 128


def decoder(nc, a, out):
    B, S, D = a["x"].shape
    T = S // P
    H, DH = 16, 64
    NPAIR = H * DH // P
    FF = a["L0_attn_w1"].shape[1]
    FC = FF // P
    SK = a["ctx_1024"].shape[1]
    E0 = a["L0_ffn_W1"].shape[0]
    DI = a["L1_attn_conv_w"].shape[0]
    IC = DI // P
    KC = a["L1_attn_conv_w"].shape[2]
    NS = a["L1_attn_A_log"].shape[1]
    NX = 2 * NS + 1
    E1 = a["L1_ffn_W1"].shape[0]
    V1 = DH + 1
    SCALE0 = float(D) ** -0.5
    BIG = 3.0e38
    assert D == P and T == 4 and FC == 4 and NPAIR == 8 and S == 512

    with ExitStack() as ctx:
        def sb(name, shape, dt=F32, at=ctx):
            return at.enter_context(nc.sbuf_tensor(name, shape, dt))

        def sem(name):
            return ctx.enter_context(nc.semaphore(name))

        bank = [ctx.enter_context(nc.psum_tensor(f"bank{i}", [P, 512], F32)) for i in range(8)]

        x_all = sb("x_all", [P, B * T, D])
        u_all = sb("u_all", [P, B * T, D])
        ident = sb("ident", [P, P])
        NROWS = 78
        rows = sb("rows", [NROWS, P])
        cols = sb("cols", [P, NROWS])
        tick = sb("tick", [P, 2])
        half = sb("half", [P, T])
        R_AB1, R_EB1, R_G1, R_BE1, R_G2, R_BE2, R_BQ, R_BK, R_CB, R_DS, R_LW, R_LB = (
            0, 4, 36, 37, 38, 39, 40, 41, 42, 44, 46, 62)

        NR = 6
        ring = sb("ring", [P, NR, FF])
        slot_in = [sem(f"slot_in{k}") for k in range(NR)]

        ph = ctx.enter_context(ExitStack())

        def s1(name, shape, dt=F32):
            return sb(name, shape, dt, ph)

        def two(name, shape, dt=F32):
            return [s1(f"{name}_{q}", shape, dt) for q in range(2)]

        wqk = s1("wqk", [P, 2, H * DH])
        wv = s1("wv", [P, H * DH])
        wo = s1("wo", [P, NPAIR, D])
        w1 = s1("w1", [P, FF])
        w2 = s1("w2", [P, FC, D])
        projd = s1("projd", [P, P])
        b2bc = s1("b2bc", [P, D])
        e0w1 = s1("e0w1", [P, E0, FF])
        e0w2 = s1("e0w2", [P, E0, FC, D])
        e0b2 = s1("e0b2", [E0, D])
        e0wg = s1("e0wg", [P, E0])
        e0bg = s1("e0bg", [P, E0])
        win = s1("win", [P, 2 * DI])
        wxp = s1("wxp", [P, IC, NX])
        wout = s1("wout", [P, IC, D])
        convw = s1("convw", [P, IC, KC])
        mask = s1("mask", [P, 3 * P])
        ones_row = s1("ones_row", [1, P])
        iota8i = s1("iota8i", [P, T, E0], I32)
        iota8 = s1("iota8", [P, T, E0])
        kxT = s1("kxT", [P, 2, B * SK])
        sxA = s1("sxA", [P, 2, B * SK])
        sx0 = s1("sx0", [1, B * SK])
        vx = s1("vx", [SK, 2, B, D])
        x_in = two("x_in", [P, T, D])
        st = two("st", [P, T, 6])
        mv = two("mv", [P, T, 2])
        ve = two("ve", [P, T])
        rs = two("rs", [P, T])
        r2 = two("r2", [P, T])
        xn = two("xn", [P, T, D])
        xh = two("xh", [P, T, D])
        xs = two("xs", [P, T, D])
        xr = two("xr", [P, T, D])
        hT = two("hT", [P, S])
        v_tm = s1("v_tm", [P, T, H, V1])
        eb = s1("eb", [P, 2, S])
        rb = s1("rb", [P, 2, S])
        qT = s1("qT", [P, 2, S])
        kT = s1("kT", [P, 2, S])
        ktm = s1("ktm", [P, 2, P])
        kv = s1("kv", [P, 2 * V1])
        stm = s1("stm", [P, 2, 2, 3 * P])
        dn = s1("dn", [P, T])
        rd = s1("rd", [P, T])
        atm = s1("atm", [P, 2, T, P])
        big = s1("big", [P, 8, S])
        pd = two("pd", [P, T, SK])
        pp = two("pp", [P, T, SK])
        mx = two("mx", [P, T])
        sm = two("sm", [P, T])
        ri = two("ri", [P, T])
        lg = s1("lg", [P, T, E0])
        oh1 = two("oh1", [P, T, E0])
        oh2 = two("oh2", [P, T, E0])
        key = s1("key", [P, T, E0])
        l2 = s1("l2", [P, T, E0])
        m1 = two("m1", [P, T])
        m2 = two("m2", [P, T])
        mn = two("mn", [P, T])
        g1 = s1("g1", [P, T])
        g2 = two("g2", [P, T])
        comb = two("comb", [P, T, E0])
        xpad = two("xpad", [P, IC, S + KC - 1])
        ssm = two("ssm", [P, T, NX])
        sp_x = two("sp_x", [P, 8, T])
        dB = two("dB", [P, T, NS])
        yT = [kT, big[:, 6:8]]

        stm_f = stm[:].rearrange("p a c k -> p (a c k)")
        atm_f = atm[:].rearrange("p a t d -> p (a t d)")

        def part(flat, n, at, rows=P):
            return flat[0:rows, at:at + n]

        wx = part(stm_f, 6 * D, 0).rearrange("p (a d) -> p a d", a=6)
        ctx_in = part(stm_f, B * D, 6 * D, SK).rearrange("p (b d) -> p b d", b=B)
        bvbc = part(stm_f, D, 6 * D + B * D, SK)
        ctxT = part(atm_f, B * SK, 0)
        wxT = part(atm_f, 3 * D, B * SK).rearrange("p (a d) -> p a d", a=3)
        pT = [part(stm_f, S, q * S, SK) for q in range(2)]
        hmT = [part(stm_f, DI, 2 * S + q * DI, NS) for q in range(2)]
        combT = [part(atm_f, S, q * S, E0) for q in range(2)]
        cT = [part(atm_f, S, q * S, NS) for q in range(2)]
        cv = [eb, big[:, 0:2]]
        xc = [rb, big[:, 2:4]]
        sz = [qT, big[:, 4:6]]
        yT = [kT, big[:, 6:8]]
        xcT = [v_tm[:, :, 4 * q:4 * q + 4, 0:DH] for q in range(2)]

        w_first = sem("w_first")
        w_in = sem("w_in")
        w_late = sem("w_late")
        x_loaded = [sem(f"x_loaded_{q}") for q in range(2)]
        consts = sem("consts")
        pre_pe = sem("pre_pe")
        pre_act = sem("pre_act")
        vec = sem("vec")
        out_done = sem("out_done")
        names = ("var_ready rstd_ready ln_ready lnT_done hT_ready v_done v_act v_dve qk_done phi_parts phi_ready "
                 "kt_done ktm_ready state_done state_ready scores_done st_ready apply_done attn_evac atT_done atT_evac "
                 "y_done ff_done ff_ready sc_done sd_ready p_ready pT_done pT_ready lg_done comb_ready combT_done "
                 "combT_ready up_done up_act up_dve acc_done xz_done xp_ready cv_ready xc_ready sz_ready ssm_done ct_done "
                 "xcT_done xcT_ready ct_ready abs_ready u_ready w_ready l_ready db_ready hm_done hm_ready yt_done "
                 "yt_ready xs_ready xa_ready x_free md_ready me_ready x_kept neg_ready").split()
        in_turn = ("v_done v_act v_dve qk_done phi_parts phi_ready neg_ready kt_done ktm_ready state_done "
                           "state_ready scores_done st_ready apply_done attn_evac atT_done atT_evac ff_done ff_ready up_done "
                           "up_act up_dve acc_done combT_done combT_ready xz_done xp_ready sz_ready cv_ready xc_ready").split()
        s = {n: sem(n) if n in in_turn else [sem(f"{n}_{q}") for q in range(2)] for n in names}
        (var_ready, rstd_ready, ln_ready, lnT_done, hT_ready, v_done, v_act, v_dve, qk_done, phi_parts, phi_ready,
         kt_done, ktm_ready, state_done, state_ready, scores_done, st_ready, apply_done, attn_evac, atT_done, atT_evac,
         y_done, ff_done, ff_ready, sc_done, sd_ready, p_ready, pT_done, pT_ready, lg_done, comb_ready, combT_done,
         combT_ready, up_done, up_act, up_dve, acc_done, xz_done, xp_ready, cv_ready, xc_ready, sz_ready, ssm_done,
         ct_done, xcT_done, xcT_ready, ct_ready, abs_ready, u_ready, w_ready, l_ready, db_ready, hm_done,
         hm_ready, yt_done, yt_ready, xs_ready, xa_ready, x_free, md_ready, me_ready, x_kept, neg_ready) = [s[n] for n in names]

        VEC_PRE, VEC_STEPS = 2, 190
        N_LN, N_LN_ALL, N_POW, N_Y = 6, 7, 8, 14
        LN_ATT, LN_FFN, LN_X0, LN_MOE, LN_SSM, LN_X1 = range(6)

        Y_WO, Y_FFN, Y_X0, Y_BIAS, Y_E, Y_SSM, Y_X1 = 0, 1, 2, 3, 4, 4 + E0, 5 + E0
        W_FIRST, W_ATT, W_LATE = 24, 5, 9

        ATTENTION, EXPERTS, STATE_SPACE = 2, 4, 6

        def at(pr, step, n, k):
            return (pr + step) * n + (k - step * n) if step else pr * n + k

        block = ph.enter_context(nc.Block())

        @block.sync
        def _(sp):
            n = [0]

            def load(dst, src, done=w_first):
                sp.dma_start(dst, src).then_inc(done, 16)
                n[0] += 1

            def vec_rows(r, v):
                k = v.shape[0] // P
                load(rows[r:r + k, :], v.rearrange("(c p) -> c p", p=P))

            load(wqk[:, 0, :], a["L0_attn_wq"])
            load(wqk[:, 1, :], a["L0_attn_wk"])
            for q in range(2):
                sp.dma_start(x_in[q][:], a["x"][q].rearrange("(t p) d -> p t d", p=P)).then_inc(x_loaded[q], 16)
            sp.wait_ge(consts, 3)
            load(projd[0:DH, 0:DH], a["L0_attn_proj"])
            load(projd[DH:P, DH:P], a["L0_attn_proj"])
            vec_rows(R_AB1, a["L0_attn_b1"])
            load(rows[R_EB1:R_EB1 + E0 * FC, :], a["L0_ffn_b1"].rearrange("e (c p) -> (e c) p", p=P))
            vec_rows(R_G1, a["L0_attn_g1"])
            vec_rows(R_BE1, a["L0_attn_beta1"])
            vec_rows(R_G2, a["L0_attn_g2"])
            vec_rows(R_BE2, a["L0_attn_beta2"])
            vec_rows(R_BQ, a["L0_xattn_bq"])
            vec_rows(R_BK, a["L0_xattn_bk"])
            vec_rows(R_CB, a["L1_attn_conv_b"])
            vec_rows(R_DS, a["L1_attn_D"])
            load(rows[R_LW:R_LW + 16, :], a["L1_ffn_ln_hid_w"].rearrange("g (c p) -> (g c) p", p=P))
            load(rows[R_LB:R_LB + 16, :], a["L1_ffn_ln_hid_b"].rearrange("g (c p) -> (g c) p", p=P))
            load(w1[:], a["L0_attn_w1"], w_in)
            load(w2[:], a["L0_attn_w2"].rearrange("(c p) n -> p c n", p=P), w_in)
            load(e0w1[:], a["L0_ffn_W1"].rearrange("e d f -> d e f"), w_late)
            load(e0w2[:], a["L0_ffn_W2"].rearrange("e (c p) d -> p e c d", p=P), w_late)
            load(win[:], a["L1_attn_W_in"], w_late)
            for k in range(NR):
                sp.dma_start(ring[:, k, :], a["L1_ffn_W1"][k]).then_inc(slot_in[k], 16)
            with sp.Fori(1, B // 2) as pr:
                for q in range(2):
                    sp.wait_ge(x_free[q], pr)
                    src = a["x"].rearrange("b (t p) d -> p b t d", p=P)[:, bass.ds(pr * 2 + q, 1), :, :]
                    sp.dma_start(x_in[q][:], src.rearrange("p b t d -> p (b t) d")).then_inc(x_loaded[q], 16)

        @block.gpsimd
        def _(pool):
            nc.gpsimd.memset(ident[:], 0.0).then_inc(consts, 1)
            nc.gpsimd.memset(mask[:], 1.0).then_inc(consts, 1)
            nc.gpsimd.memset(projd[:], 0.0).then_inc(consts, 1)
            pool.wait_ge(consts, 3)
            nc.gpsimd.affine_select(out=ident[:], in_=ident[:], compare_op=ALU.not_equal, fill=1.0, base=0,
                                    pattern=[[-1, P]], channel_multiplier=1)
            for c in (0, 2):
                nc.gpsimd.affine_select(out=mask[:, c * P:(c + 1) * P], in_=mask[:, c * P:(c + 1) * P],
                                        compare_op=ALU.is_ge, fill=0.0, base=0, pattern=[[1, P]],
                                        channel_multiplier=-1)
            nc.gpsimd.iota(iota8i[:], pattern=[[0, T], [1, E0]], base=0, channel_multiplier=0)
            nc.gpsimd.memset(ones_row[:], 1.0)
            nc.gpsimd.memset(half[:], -0.5)
            nc.gpsimd.memset(v_tm[:, :, :, DH:V1], 1.0)
            for q in range(2):
                l = nc.gpsimd.memset(xpad[q][:, :, 0:KC - 1], 0.0)
            l.then_inc(consts, 1)
            pool.wait_ge(consts, 4)
            pool.wait_ge(w_in, 16 * W_ATT)
            with pool.Fori(0, B // 2) as pr:
                def inverse_root(q, k, dst):
                    pool.wait_ge(var_ready[q], at(pr, q, N_POW, k + 1))
                    nc.gpsimd.tensor_tensor(dst[:], ve[q][:], half[:], ALU.pow).then_inc(rstd_ready[q], 1)

                for q in range(2):
                    pool.wait_ge(x_loaded[q], at(pr, q, 16, 16))
                    nc.gpsimd.tensor_tensor(xs[q][:], x_in[q][:], b2bc[:].unsqueeze(1).to_broadcast([P, T, D]),
                                            ALU.add).then_inc(xs_ready[q], 1)
                    inverse_root(q, 0, rs[q])
                    inverse_root(q, 1, r2[q])
                for q in range(2):
                    pool.wait_ge(xa_ready[q], pr + 1)
                    pool.wait_ge(xs_ready[q], at(pr, q, 2, 1))
                    nc.gpsimd.tensor_tensor(xs[q][:], xs[q][:], xn[q][:], ALU.add).then_inc(xs_ready[q], 1)
                    inverse_root(q, 2, rs[q])
                for k in range(3, N_POW):
                    for q in range(2):
                        inverse_root(q, k, rs[q])

        @block.tensor
        def _(pe):
            mm, tr = nc.tensor.matmul, nc.tensor.transpose
            pe.wait_ge(w_first, 16 * W_FIRST)
            pe.wait_ge(consts, 4)
            tr(bank[7][:, 0:NROWS], rows[:], ident[0:NROWS, 0:NROWS]).then_inc(pre_pe, 1)
            for g in range(4):
                w, j0 = g // 2, 4 * (g % 2)
                for j in range(4):
                    l = tr(bank[g][:, j * P:(j + 1) * P], wqk[:, w, (j0 + j) * P:(j0 + j + 1) * P], ident[:])
                l.then_inc(pre_pe, 1)
            for g in range(4):
                pe.wait_ge(pre_act, 2 + g if g < 2 else 4 + g)
                for j in range(4):
                    l = mm(bank[4 + g % 2][:, j * P:(j + 1) * P], big[:, g, j * P:(j + 1) * P], projd[:],
                           start=True, stop=True)
                l.then_inc(pre_pe, 1)
            for b in range(B):
                l = tr(bank[0][:, b * SK:(b + 1) * SK], ctx_in[:, b, :], ident[0:SK, 0:SK])
            l.then_inc(pre_pe, 1)
            for i, w in enumerate((0, 4, 5)):
                l = tr(bank[1][:, i * P:(i + 1) * P], wx[:, w, :], ident[:])
            l.then_inc(pre_pe, 1)
            pe.wait_ge(pre_act, 11)
            mm(bank[2][:, 0:B * SK], wx[:, 1, :], ctxT[:], start=True, stop=True)
            mm(bank[3][:, 0:B * SK], wxT[:, 1, :], ctxT[:], start=True, stop=True).then_inc(pre_pe, 1)
            for i, w in enumerate((wx[:, 2, :], wxT[:, 2, :])):
                for b in range(B):
                    l = mm(bank[6 + i][0:SK, b * P:(b + 1) * P], ctxT[:, b * SK:(b + 1) * SK], w,
                           start=True, stop=True)
            l.then_inc(pre_pe, 1)
            pe.wait_ge(pre_act, 13)
            mm(bank[0][:, 0:B * SK], wxT[:, 0, :], kxT[:, 0, :], start=True, stop=True)
            mm(bank[1][:, 0:B * SK], wx[:, 3, :], kxT[:, 1, :], start=True, stop=True)
            mm(bank[2][0:1, 0:B * SK], cols[:, R_BQ:R_BQ + 1], kxT[:, 0, :], start=True, stop=True).then_inc(pre_pe, 1)
            pe.wait_ge(pre_act, 17)
            pe.wait_ge(vec, VEC_PRE)

            pe.wait_ge(w_in, 16 * W_ATT)
            with pe.Fori(0, B // 2) as pr:
                ps_q, ps_k, ps_s, ps_o, ps_x, ps_t = bank[0], bank[1], bank[2:4], bank[4:6], bank[6], bank[7]
                four, y_bank = (*ps_s, *ps_o), (ps_q, ps_k)

                def to_features(q, k):
                    pe.wait_ge(ln_ready[q], at(pr, q, N_LN_ALL, k + 1))
                    for t in range(T):
                        l = tr(ps_t[:, t * P:(t + 1) * P], xh[q][:, t, :], ident[:])
                    l.then_inc(lnT_done[q], 1)
                    pe.wait_ge(hT_ready[q], at(pr, q, N_LN, k + 1))

                def down(q, dst, hid, w, n):
                    for t in range(T):
                        for c in range(n):
                            l = mm(dst[:, t * P:(t + 1) * P], hid[:, c, t * P:(t + 1) * P], w[:, c, :],
                                   start=(c == 0), stop=(c == n - 1))
                    l.then_inc(y_done[q], 1)

                def attention(q):
                    to_features(q, LN_ATT)
                    for n in range(2 * T):
                        t, h = n // 2, n % 2
                        if n >= 4:
                            pe.wait_ge((v_act, v_dve)[n % 2], at(pr, ATTENTION + q, 2 * T, q * T + (n - 4) // 2 + 1))
                        mm(four[n % 4][:], hT[q][:, t * P:(t + 1) * P], wv[:, h * 512:(h + 1) * 512],
                           start=True, stop=True).then_inc(v_done, 1)

                    def project(w, j):
                        if j:
                            pe.wait_ge(phi_ready, at(pr, ATTENTION + q, 2 * 2 * NPAIR, q * 2 * NPAIR + (2 * j - 1 + w)))
                        mm((ps_q, ps_k)[w][:], wqk[:, w, j * P:(j + 1) * P], hT[q][:], start=True, stop=True)\
                            .then_inc(qk_done, 1)

                    def scores(j, hh):
                        i, h0 = 2 * j + hh, hh * DH
                        r = slice(h0, h0 + DH)
                        if i == 0:
                            pe.wait_ge(v_act, at(pr, ATTENTION + q, 2 * T, q * T + T))
                            pe.wait_ge(v_dve, at(pr, ATTENTION + q, 2 * T, q * T + T))
                        else:
                            pe.wait_ge(st_ready, at(pr, ATTENTION + q, 2 * 2 * H, q * 2 * H + 2 * i))
                        pe.wait_ge(phi_ready, at(pr, ATTENTION + q, 2 * 2 * NPAIR, q * 2 * NPAIR + 2 * j + 2))
                        for c in range(2):
                            t0 = 2 * c * P
                            mm(ps_s[c][:, 0:2 * P], kT[r, j % 2, t0:t0 + P], qT[r, j % 2, t0:t0 + 2 * P],
                               start=True, stop=True)
                            mm(ps_s[c][:, 2 * P:3 * P], kT[r, j % 2, t0 + P:t0 + 2 * P],
                               qT[r, j % 2, t0 + P:t0 + 2 * P], start=True, stop=True).then_inc(scores_done, 1)

                    def keys_to_tokens(j):
                        if j:
                            pe.wait_ge(state_ready, at(pr, ATTENTION + q, 2 * NPAIR, q * NPAIR + j))
                        for t in range(2):
                            l = tr(ps_x[:, t * P:(t + 1) * P], kT[:, j % 2, t * P:(t + 1) * P], ident[:])
                        l.then_inc(kt_done, 1)

                    def state(j):
                        pe.wait_ge(ktm_ready, at(pr, ATTENTION + q, 2 * NPAIR, q * NPAIR + j + 1))
                        for t in range(2):
                            l = mm(ps_x[:, 2 * P:2 * P + 2 * V1], ktm[:, t, :],
                                   v_tm[:, t, 2 * j:2 * j + 2, :].rearrange("p h v -> p (h v)"),
                                   start=(t == 0), stop=(t == 1))
                        l.then_inc(state_done, 1)

                    def apply(j, hh):
                        i, h = 2 * j + hh, 2 * j + hh
                        r = slice(hh * DH, hh * DH + DH)
                        pe.wait_ge(st_ready, at(pr, ATTENTION + q, 2 * 2 * H, q * 2 * H + 2 * i + 2))
                        if hh == 0:
                            pe.wait_ge(state_ready, at(pr, ATTENTION + q, 2 * NPAIR, q * NPAIR + j + 1))
                        if j:
                            pe.wait_ge(attn_evac, at(pr, ATTENTION + q, 2 * H, q * H + i - 1))
                        for c in range(2):
                            for tt in range(2):
                                o = ps_o[hh][:, (2 * c + tt) * V1:(2 * c + tt + 1) * V1]
                                w = stm[:, i % 2, c, :]
                                l = mm(o, w[:, tt * P:(tt + 1) * P], v_tm[:, 2 * c, h, :],
                                       start=True, stop=(c == 0 and tt == 0))
                                if tt:
                                    l = mm(o, w[:, 2 * P:3 * P], v_tm[:, 2 * c + 1, h, :], start=False, stop=(c == 0))
                                if c:
                                    q0 = (2 * c + tt) * P
                                    l = mm(o, qT[r, j % 2, q0:q0 + P], kv[r, hh * V1:(hh + 1) * V1],
                                           start=False, stop=True)
                        l.then_inc(apply_done, 1)

                    def attn_to_features(j):
                        pe.wait_ge(attn_evac, at(pr, ATTENTION + q, 2 * 2 * NPAIR, q * 2 * NPAIR + 2 * j + 2))
                        if j:
                            pe.wait_ge(atT_evac, at(pr, ATTENTION + q, 2 * NPAIR, q * NPAIR + j))
                        for t in range(T):
                            l = tr(ps_t[:, t * P:(t + 1) * P], atm[:, j % 2, t, :], ident[:])
                        l.then_inc(atT_done, 1)

                    if q:
                        pe.wait_ge(xa_ready[0], pr + 1)
                    project(0, 0)
                    project(1, 0)
                    for j in range(NPAIR):
                        scores(j, 0)
                        keys_to_tokens(j)
                        if j + 1 < NPAIR:
                            project(0, j + 1)
                        scores(j, 1)
                        if j:
                            attn_to_features(j - 1)
                        state(j)
                        if j + 1 < NPAIR:
                            project(1, j + 1)
                        apply(j, 0)
                        apply(j, 1)
                    attn_to_features(NPAIR - 1)

                    pe.wait_ge(atT_evac, at(pr, ATTENTION + q, 2 * NPAIR, q * NPAIR + NPAIR))
                    down(q, y_bank[q], big, wo, NPAIR)

                def ffn(q):
                    to_features(q, LN_FFN)
                    for c in range(FC):
                        mm(four[c][:], w1[:, c * P:(c + 1) * P], hT[q][:], start=True, stop=True).then_inc(ff_done, 1)
                    pe.wait_ge(ff_ready, at(pr, ATTENTION + q, 2 * FC, q * FC + FC))
                    down(q, y_bank[q], big, w2, FC)

                def cross_scores(q, i):
                    to_features(q, (LN_X0, LN_X1)[i])
                    keys = sxA[:, i, :].rearrange("p (b k) -> p b k", b=B)[:, bass.ds(pr * 2 + q, 1), :]\
                        .rearrange("p b k -> p (b k)")
                    for t in range(T):
                        o = ps_s[q][:, t * SK:(t + 1) * SK]
                        l = mm(o, hT[q][:, t * P:(t + 1) * P], keys, start=True, stop=(i == 1))
                        if i == 0:
                            l = mm(o, ones_row[:], sx0[:].rearrange("p (b k) -> p b k", b=B)[:, bass.ds(pr * 2 + q, 1), :]
                                   .rearrange("p b k -> p (b k)"), start=False, stop=True)
                    l.then_inc(sc_done[q], 1)

                def cross_probs(q, i):
                    pe.wait_ge(p_ready[q], at(pr, q, 2, i + 1))
                    if q:
                        pe.wait_ge(pT_ready[0], pr * 2 + (i + 1))
                    for t in range(T):
                        l = tr(ps_t[0:SK, t * P:(t + 1) * P], pp[q][:, t, :], ident[:])
                    l.then_inc(pT_done[q], 1)

                def cross_values(q, i):
                    pe.wait_ge(pT_ready[q], at(pr, q, 2, i + 1))
                    vals = vx[:, i, bass.ds(pr * 2 + q, 1), :].rearrange("p b k -> p (b k)")
                    for t in range(T):
                        l = mm(y_bank[q][:, t * P:(t + 1) * P], pT[q][:, t * P:(t + 1) * P], vals, start=True, stop=True)
                    l.then_inc(y_done[q], 1)

                def router(q):
                    pe.wait_ge(w_late, 16 * W_LATE)
                    to_features(q, LN_MOE)
                    for t in range(T):
                        l = mm((ps_x, ps_k)[q][:, t * E0:(t + 1) * E0], hT[q][:, t * P:(t + 1) * P], e0wg[:], start=True, stop=True)
                    l.then_inc(lg_done[q], 1)

                def experts(q):
                    def up(e):
                        for c in range(FC):
                            if e:
                                pe.wait_ge((up_act, up_dve)[c % 2], at(pr, EXPERTS + q, 2 * 2 * E0, q * 2 * E0 + 2 * (e - 1) + c // 2 + 1))
                            mm(four[(c + 2) % 4][:], e0w1[:, e, c * P:(c + 1) * P], hT[q][:], start=True, stop=True)\
                                .then_inc(up_done, 1)

                    pe.wait_ge(comb_ready[q], pr + 1)
                    for t in range(T):
                        l = tr(ps_t[0:E0, t * P:(t + 1) * P], comb[q][:, t, :], ident[:])
                    l.then_inc(combT_done, 1)
                    up(0)
                    pe.wait_ge(combT_ready, pr * 2 + q + 1)
                    if q:
                        pe.wait_ge(acc_done, pr * (2 * E0) + E0)
                    for t in range(T):
                        l = mm(ps_q[:, t * P:(t + 1) * P], combT[q][:, t * P:(t + 1) * P], e0b2[:], start=True, stop=True)
                    l.then_inc(y_done[q], 1)
                    for e in range(E0):
                        if e + 1 < E0:
                            up(e + 1)
                        pe.wait_ge(up_act, at(pr, EXPERTS + q, 2 * 2 * E0, q * 2 * E0 + 2 * e + 2))
                        pe.wait_ge(up_dve, at(pr, EXPERTS + q, 2 * 2 * E0, q * 2 * E0 + 2 * e + 2))
                        if e:
                            pe.wait_ge(acc_done, at(pr, EXPERTS + q, 2 * E0, q * E0 + e))
                        down(q, (ps_k, ps_q)[e % 2], big[:, 4 * (e % 2):4 * (e % 2) + 4, :], e0w2[:, e], FC)

                def ssm_in(q):
                    to_features(q, LN_SSM)
                    if q:
                        pe.wait_ge(xp_ready, at(pr, STATE_SPACE, 2 * IC, IC))
                        pe.wait_ge(sz_ready, at(pr, STATE_SPACE, 2 * IC, IC))
                    for c in range(4):
                        mm(four[c][:], win[:, c * P:(c + 1) * P], hT[q][:], start=True, stop=True).then_inc(xz_done, 1)

                def ssm_proj(q):
                    pe.wait_ge(xc_ready, at(pr, STATE_SPACE + q, 2 * IC, q * IC + IC))
                    for t in range(T):
                        for c in range(IC):
                            l = mm((ps_x, ps_s[1])[q][:, t * NX:(t + 1) * NX], xc[q][:, c, t * P:(t + 1) * P], wxp[:, c, :],
                                   start=(c == 0), stop=(c == IC - 1))
                    l.then_inc(ssm_done[q], 1)
                    if q:
                        pe.wait_ge(xcT_ready[0], pr * IC + IC)
                        pe.wait_ge(ct_ready[0], pr + 1)
                    for c in range(IC):
                        for t in range(T):
                            l = tr((ps_t, ps_q)[c][:, t * P:(t + 1) * P], xc[q][:, c, t * P:(t + 1) * P], ident[:])
                    l.then_inc(xcT_done[q], 1)
                    for c in range(IC):
                        l = mm(ps_k[0:NS, :], wxp[:, c, 1 + NS:NX], xc[q][:, c, :], start=(c == 0), stop=(c == IC - 1))
                    l.then_inc(ct_done[q], 1)

                def ssm_mean(q):
                    pe.wait_ge(db_ready[q], pr + 1)
                    pe.wait_ge(xcT_ready[q], at(pr, q, IC, IC))
                    for t in range(T):
                        l = mm(ps_s[q][0:NS, 0:DI], dB[q][:, t, :], xcT[q][:, t, :, :], start=(t == 0), stop=(t == T - 1))
                    l.then_inc(hm_done[q], 1)

                def ssm_out(q):
                    pe.wait_ge(ct_ready[q], pr + 1)
                    pe.wait_ge(hm_ready[q], pr + 1)
                    pe.wait_ge(sz_ready, at(pr, STATE_SPACE + q, 2 * IC, q * IC + IC))
                    if q:
                        pe.wait_ge(yt_ready[0], pr * IC + IC)
                    for c in range(IC):
                        mm(ps_o[c][:], hmT[q][:, c * P:(c + 1) * P], cT[q][:], start=True, stop=True).then_inc(yt_done[q], 1)

                def ssm_down(q):
                    pe.wait_ge(yt_ready[q], at(pr, q, IC, IC))
                    down(q, y_bank[q], yT[q], wout, IC)
                for q in range(2):
                    attention(q)
                for q in range(2):
                    ffn(q)
                for q in range(2):
                    cross_scores(q, 0)
                for q in range(2):
                    cross_probs(q, 0)
                for q in range(2):
                    cross_values(q, 0)
                for q in range(2):
                    router(q)
                for q in range(2):
                    experts(q)
                for q in range(2):
                    ssm_in(q)
                for q in range(2):
                    ssm_proj(q)
                for q in range(2):
                    ssm_mean(q)
                for q in range(2):
                    ssm_out(q)
                for q in range(2):
                    ssm_down(q)
                for q in range(2):
                    cross_scores(q, 1)
                for q in range(2):
                    cross_probs(q, 1)
                for q in range(2):
                    cross_values(q, 1)

        @block.scalar
        def _(act):
            af = nc.scalar.activation
            n = [0]

            def pre(ins):
                n[0] += 1
                ins.then_inc(pre_act, 1)

            def load(dst, src, done=w_first):
                act.dma_start(dst, src).then_inc(done, 16)

            load(ctx_in[:], a["ctx_1024"].rearrange("b k d -> k b d"))
            for i, name in enumerate(("L0_xattn_Wq", "L0_xattn_Wk", "L0_xattn_Wv",
                                      "L1_xattn_Wq", "L1_xattn_Wk", "L1_xattn_Wv")):
                load(wx[:, i, :], a[name])
            load(bvbc[:], a["L0_xattn_bv"].rearrange("(o d) -> o d", o=1).to_broadcast([SK, D]))
            load(b2bc[:], a["L0_attn_b2"].rearrange("(o d) -> o d", o=1).to_broadcast([P, D]), w_in)
            load(wv[:], a["L0_attn_wv"], w_in)
            load(wo[:], a["L0_attn_wo"].rearrange("(j p) n -> p j n", p=P), w_in)
            load(e0b2[:], a["L0_ffn_b2"], w_late)
            load(e0wg[:], a["L0_ffn_Wg"], w_late)
            load(e0bg[:], a["L0_ffn_bg"].rearrange("(o d) -> o d", o=1).to_broadcast([P, E0]), w_late)
            load(wxp[:], a["L1_attn_W_xproj"].rearrange("(c p) n -> p c n", p=P), w_late)
            load(wout[:], a["L1_attn_W_out"].rearrange("(c p) n -> p c n", p=P), w_late)
            load(convw[:], a["L1_attn_conv_w"].rearrange("(c p) o k -> p c (o k)", p=P), w_late)
            act.wait_ge(pre_pe, 1)
            pre(af(cols[:], bank[7][:, 0:NROWS], ACT.Copy))
            for g in range(4):
                act.wait_ge(pre_pe, 2 + g)
                pre(af(big[:, g, :], bank[g][:], ACT.Copy))
            for g in range(4):
                act.wait_ge(pre_pe, 6 + g)
                pre(af(wqk[:, g // 2, (g % 2) * 512:(g % 2) * 512 + 512], bank[4 + g % 2][:], ACT.Copy))
            act.wait_ge(pre_pe, 10)
            pre(af(ctxT[:], bank[0][:, 0:B * SK], ACT.Copy))
            act.wait_ge(pre_pe, 11)
            pre(af(wxT[:].rearrange("p a d -> p (a d)"), bank[1][:, 0:3 * D], ACT.Copy))
            act.wait_ge(pre_pe, 12)
            act.wait_ge(pre_act, 1)
            pre(af(kxT[:, 0, :], bank[2][:, 0:B * SK], ACT.Identity, bias=cols[:, R_BK:R_BK + 1]))
            pre(af(kxT[:, 1, :], bank[3][:, 0:B * SK], ACT.Copy))
            act.wait_ge(pre_pe, 13)
            pre(af(vx[:, 1, :, :].rearrange("p b d -> p (b d)"), bank[7][0:SK, :], ACT.Copy))
            act.wait_ge(pre_pe, 14)
            pre(af(sxA[:, 0, :], bank[0][:, 0:B * SK], ACT.Copy))
            pre(af(sxA[:, 1, :], bank[1][:, 0:B * SK], ACT.Copy))
            pre(af(sx0[:], bank[2][0:1, 0:B * SK], ACT.Copy))
            assert n[0] == 17

            with act.Fori(0, B // 2) as pr:
                ps_q, ps_k, ps_s, ps_o, ps_x, ps_t = bank[0], bank[1], bank[2:4], bank[4:6], bank[6], bank[7]
                four, y_bank = (*ps_s, *ps_o), (ps_q, ps_k)

                def features(q, k, g=None, be=None):
                    act.wait_ge(lnT_done[q], at(pr, q, N_LN, k + 1))
                    if g is None:
                        af(hT[q][:], ps_t[:], ACT.Copy).then_inc(hT_ready[q], 1)
                    else:
                        af(hT[q][:], ps_t[:], ACT.Identity, scale=cols[:, g:g + 1], bias=cols[:, be:be + 1])\
                            .then_inc(hT_ready[q], 1)

                def attention(q):
                    features(q, LN_ATT, R_G1, R_BE1)
                    for t in range(T):
                        act.wait_ge(v_done, at(pr, ATTENTION + q, 2 * 2 * T, q * 2 * T + 2 * t + 1))
                        af(v_tm[:, t, 0:H // 2, 0:DH], four[2 * t % 4][:].rearrange("p (h d) -> p h d", d=DH),
                           ACT.Copy).then_inc(v_act, 1)

                    def parts(w, j):
                        m = 2 * j + w
                        act.wait_ge(qk_done, at(pr, ATTENTION + q, 2 * 2 * NPAIR, q * 2 * NPAIR + m + 1))
                        if m >= 2:
                            act.wait_ge(phi_ready, at(pr, ATTENTION + q, 2 * 2 * NPAIR, q * 2 * NPAIR + m - 1))
                        af(rb[:, m % 2, :], (ps_q, ps_k)[w][:], ACT.Relu, scale=-1.0).then_inc(neg_ready, 1)
                        act.wait_ge(neg_ready, at(pr, ATTENTION + q, 2 * 2 * NPAIR, q * 2 * NPAIR + m + 1))
                        af(eb[:, m % 2, :], rb[:, m % 2, :], ACT.Exp, scale=-1.0).then_inc(phi_parts, 1)

                    parts(0, 0)
                    parts(1, 0)
                    for j in range(NPAIR):
                        act.wait_ge(kt_done, at(pr, ATTENTION + q, 2 * NPAIR, q * NPAIR + j + 1))
                        af(ktm[:], ps_x[:, 0:2 * P].rearrange("p (t d) -> p t d", t=2), ACT.Copy).then_inc(ktm_ready, 1)
                        if j + 1 < NPAIR:
                            parts(0, j + 1)
                        if j:
                            act.wait_ge(atT_done, at(pr, ATTENTION + q, 2 * NPAIR, q * NPAIR + j))
                            af(big[:, j - 1, :], ps_t[:], ACT.Copy).then_inc(atT_evac, 1)
                        act.wait_ge(state_done, at(pr, ATTENTION + q, 2 * NPAIR, q * NPAIR + j + 1))
                        if j:
                            act.wait_ge(apply_done, at(pr, ATTENTION + q, 2 * H, q * H + 2 * j))
                        af(kv[:], ps_x[:, 2 * P:2 * P + 2 * V1], ACT.Copy).then_inc(state_ready, 1)
                        if j + 1 < NPAIR:
                            parts(1, j + 1)
                    act.wait_ge(atT_done, at(pr, ATTENTION + q, 2 * NPAIR, q * NPAIR + NPAIR))
                    af(big[:, NPAIR - 1, :], ps_t[:], ACT.Copy).then_inc(atT_evac, 1)

                def ffn(q):
                    features(q, LN_FFN, R_G2, R_BE2)
                    for c in range(FC):
                        act.wait_ge(ff_done, at(pr, ATTENTION + q, 2 * FC, q * FC + c + 1))
                        af(big[:, c, :], four[c][:], ACT.Gelu, bias=cols[:, R_AB1 + c:R_AB1 + c + 1]).then_inc(ff_ready, 1)

                def cross_scores(q, i):
                    features(q, (LN_X0, LN_X1)[i])

                def cross_softmax(q, i):
                    act.wait_ge(sd_ready[q], at(pr, q, 2, i + 1))
                    af(pp[q][:], pd[q][:], ACT.Exp, scale=SCALE0).then_inc(p_ready[q], 1)

                def cross_probs(q, i):
                    act.wait_ge(pT_done[q], at(pr, q, 2, i + 1))
                    af(pT[q][:], ps_t[0:SK, :], ACT.Copy).then_inc(pT_ready[q], 1)

                def router(q):
                    features(q, LN_MOE)

                def router_weights(q):
                    act.wait_ge(md_ready[q], pr + 1)
                    af(g2[q][:], mn[q][:], ACT.Exp).then_inc(me_ready[q], 1)

                def experts(q):
                    act.wait_ge(combT_done, pr * 2 + q + 1)
                    af(combT[q][:], ps_t[0:E0, :], ACT.Copy).then_inc(combT_ready, 1)
                    for e in range(E0):
                        for c in (0, 2):
                            act.wait_ge(up_done, at(pr, EXPERTS + q, 2 * FC * E0, q * FC * E0 + FC * e + c + 1))
                            if e >= 2:
                                act.wait_ge(y_done[q], at(pr, q, N_Y, Y_E + e - 1))
                            r = R_EB1 + FC * e + c
                            af(big[:, 4 * (e % 2) + c, :], four[(c + 2) % 4][:], ACT.Relu, bias=cols[:, r:r + 1])\
                                .then_inc(up_act, 1)

                def ssm_in(q):
                    features(q, LN_SSM)
                    for c in range(IC):
                        act.wait_ge(xz_done, at(pr, STATE_SPACE + q, 2 * 4, q * 4 + c + 1))
                        af(xpad[q][:, c, KC - 1:], four[c][:], ACT.Copy).then_inc(xp_ready, 1)
                    for c in range(IC):
                        act.wait_ge(xz_done, at(pr, STATE_SPACE + q, 2 * 4, q * 4 + IC + c + 1))
                        af(sz[q][:, c, :], four[IC + c][:], ACT.Silu).then_inc(sz_ready, 1)

                def ssm_conv(q):
                    for c in range(IC):
                        act.wait_ge(cv_ready, at(pr, STATE_SPACE + q, 2 * IC, q * IC + c + 1))
                        af(xc[q][:, c, :], cv[q][:, c, :], ACT.Silu).then_inc(xc_ready, 1)

                def ssm_proj(q):
                    act.wait_ge(xcT_done[q], pr + 1)
                    for c in range(IC):
                        af(xcT[q][:, :, 2 * c:2 * c + 2, :], (ps_t, ps_q)[c][:].rearrange("p (t h d) -> p t h d", t=T, d=DH),
                           ACT.Copy).then_inc(xcT_ready[q], 1)
                    act.wait_ge(ct_done[q], pr + 1)
                    af(cT[q][:], ps_k[0:NS, :], ACT.Copy).then_inc(ct_ready[q], 1)

                def ssm_mean(q):
                    act.wait_ge(abs_ready[q], pr + 1)
                    af(sp_x[q][:, 2, :], sp_x[q][:, 1, :], ACT.Exp).then_inc(u_ready[q], 1)
                    act.wait_ge(w_ready[q], pr + 1)
                    af(sp_x[q][:, 4, :], sp_x[q][:, 3, :], ACT.Ln).then_inc(l_ready[q], 1)

                def ssm_out(q):
                    act.wait_ge(hm_done[q], pr + 1)
                    af(hmT[q][:], ps_s[q][0:NS, 0:DI], ACT.Copy).then_inc(hm_ready[q], 1)

                def keep(q):
                    act.wait_ge(ln_ready[q], at(pr, q, N_LN_ALL, N_LN_ALL))
                    af(x_all[:, bass.ds(pr * (2 * T) + q * T, T), :], xr[q][:], ACT.Copy)
                    af(u_all[:, bass.ds(pr * (2 * T) + q * T, T), :], xh[q][:], ACT.Copy).then_inc(x_kept[q], 1)
                for q in range(2):
                    attention(q)
                for q in range(2):
                    ffn(q)
                for q in range(2):
                    cross_scores(q, 0)
                for q in range(2):
                    cross_softmax(q, 0)
                for q in range(2):
                    cross_probs(q, 0)
                for q in range(2):
                    router(q)
                for q in range(2):
                    router_weights(q)
                for q in range(2):
                    experts(q)
                for q in range(2):
                    ssm_in(q)
                for q in range(2):
                    ssm_conv(q)
                for q in range(2):
                    ssm_proj(q)
                for q in range(2):
                    ssm_mean(q)
                for q in range(2):
                    ssm_out(q)
                for q in range(2):
                    cross_scores(q, 1)
                for q in range(2):
                    cross_softmax(q, 1)
                for q in range(2):
                    cross_probs(q, 1)
                for q in range(2):
                    keep(q)

        @block.vector
        def _(dve):
            v = nc.vector
            n = [0]

            dve.wait_ge(consts, 4)
            v.tensor_copy(iota8[:], iota8i[:]).then_inc(vec, 1)
            dve.wait_ge(pre_pe, 13)
            v.tensor_tensor(vx[:, 0, :, :], bank[6][0:SK, :].rearrange("p (b d) -> p b d", b=B),
                            bvbc[:].unsqueeze(1).to_broadcast([SK, B, D]), ALU.add).then_inc(vec, 1)
            dve.wait_ge(vec, VEC_PRE)

            with dve.Fori(0, B // 2) as pr:
                ps_q, ps_k, ps_s, ps_o, ps_x, ps_t = bank[0], bank[1], bank[2:4], bank[4:6], bank[6], bank[7]
                four, y_bank = (*ps_s, *ps_o), (ps_q, ps_k)

                def link(ins):
                    n[0] += 1
                    ins.then_inc(vec, 1)
                    dve.wait_ge(vec, pr * VEC_STEPS + VEC_PRE + n[0])

                def tiles(ps):
                    return ps[:].rearrange("p (t d) -> p t d", t=T)

                def over(col, w):
                    return col.unsqueeze(2).to_broadcast([P, T, w])

                def moments(q, src, eps=1e-5):
                    for t in range(T):
                        l = v.bn_stats(st[q][:, t, :], src[:, t, :])
                    link(l)
                    v.tensor_copy(tick[:, 0:1], half[:, 0:1])
                    for t in range(T):
                        l = v.bn_aggr(mv[q][:, t, :], st[q][:, t, :])
                    link(l)
                    v.tensor_scalar(ve[q][:], mv[q][:, :, 1], eps, None, ALU.add).then_inc(var_ready[q], 1)

                def normalize(q, dst, src, k):
                    dve.wait_ge(rstd_ready[q], at(pr, q, N_POW, k + 1))
                    for t in range(T):
                        l = v.tensor_scalar(dst[:, t, :], src[:, t, :], mv[q][:, t, 0:1], rs[q][:, t:t + 1],
                                            ALU.subtract, ALU.mult)
                    return l

                def ln_in(q):
                    dve.wait_ge(x_loaded[q], at(pr, q, 16, 16))
                    moments(q, x_in[q])
                    link(normalize(q, xn[q], x_in[q], 0))
                    dve.wait_ge(xs_ready[q], at(pr, q, 2, 1))
                    v.tensor_tensor(r2[q][:], mv[q][:, :, 1], rs[q][:], ALU.mult).then_inc(x_free[q], 1)
                    dve.wait_ge(x_free[q], pr + 1)
                    link(v.tensor_tensor(r2[q][:], r2[q][:], rs[q][:], ALU.mult))
                    v.tensor_scalar(ve[q][:], r2[q][:], 1e-5, None, ALU.add).then_inc(var_ready[q], 1)
                    dve.wait_ge(rstd_ready[q], at(pr, q, N_POW, 2))
                    for t in range(T):
                        l = v.tensor_scalar(xh[q][:, t, :], xn[q][:, t, :], r2[q][:, t:t + 1], None, ALU.mult)
                    l.then_inc(ln_ready[q], 1)

                def attention(q):
                    for t in range(T):
                        dve.wait_ge(v_done, at(pr, ATTENTION + q, 2 * 2 * T, q * 2 * T + 2 * t + 2))
                        v.tensor_copy(v_tm[:, t, H // 2:H, 0:DH], four[(2 * t + 1) % 4][:]
                                      .rearrange("p (h d) -> p h d", d=DH)).then_inc(v_dve, 1)

                    def phi(w, j):
                        m = 2 * j + w
                        dve.wait_ge(phi_parts, at(pr, ATTENTION + q, 2 * 2 * NPAIR, q * 2 * NPAIR + m + 1))
                        if j >= 2:
                            dve.wait_ge(apply_done, at(pr, ATTENTION + q, 2 * H, q * H + 2 * (j - 1)))
                        v.scalar_tensor_tensor((qT, kT)[w][:, j % 2, :], (ps_q, ps_k)[w][:], 0.0, eb[:, m % 2, :],
                                               ALU.max, ALU.add).then_inc(phi_ready, 1)

                    def causal(i):
                        if i >= 2:
                            dve.wait_ge(apply_done, at(pr, ATTENTION + q, 2 * H, q * H + i - 1))
                        for c in range(2):
                            dve.wait_ge(scores_done, at(pr, ATTENTION + q, 2 * 2 * H, q * 2 * H + 2 * i + c + 1))
                            v.tensor_tensor(stm[:, i % 2, c, :], ps_s[c][:, 0:3 * P], mask[:], ALU.mult)\
                                .then_inc(st_ready, 1)

                    def attn_out(i):
                        j, hh = i // 2, i % 2
                        dve.wait_ge(apply_done, at(pr, ATTENTION + q, 2 * H, q * H + i + 1))
                        if j >= 2:
                            dve.wait_ge(atT_done, at(pr, ATTENTION + q, 2 * NPAIR, q * NPAIR + j - 1))
                        o = ps_o[hh][:, 0:T * V1].rearrange("p (t e) -> p t e", e=V1)
                        link(v.tensor_scalar(dn[:], o[:, :, DH], 1e-6, None, ALU.add))
                        link(v.reciprocal(rd[:], dn[:]))
                        v.tensor_tensor(atm[:, j % 2, :, hh * DH:(hh + 1) * DH], o[:, :, 0:DH], over(rd[:], DH),
                                        ALU.mult).then_inc(attn_evac, 1)

                    phi(0, 0)
                    phi(1, 0)
                    for j in range(NPAIR):
                        causal(2 * j)
                        if j + 1 < NPAIR:
                            phi(0, j + 1)
                        causal(2 * j + 1)
                        if j + 1 < NPAIR:
                            phi(1, j + 1)
                        attn_out(2 * j)
                        attn_out(2 * j + 1)

                    dve.wait_ge(y_done[q], at(pr, q, N_Y, Y_WO + 1))
                    v.tensor_tensor(xn[q][:], tiles(y_bank[q]), xn[q][:], ALU.add).then_inc(xa_ready[q], 1)
                    dve.wait_ge(xa_ready[q], pr + 1)
                    moments(q, xn[q])
                    normalize(q, xh[q], xn[q], 2).then_inc(ln_ready[q], 1)

                def ffn(q):
                    dve.wait_ge(y_done[q], at(pr, q, N_Y, Y_FFN + 1))
                    dve.wait_ge(xs_ready[q], at(pr, q, 2, 2))
                    link(v.tensor_tensor(xr[q][:], tiles(y_bank[q]), xs[q][:], ALU.add))
                    moments(q, xr[q])
                    normalize(q, xh[q], xr[q], 3).then_inc(ln_ready[q], 1)

                def cross_scores(q, i):
                    dve.wait_ge(sc_done[q], at(pr, q, 2, i + 1))
                    sc = ps_s[q][:, 0:T * SK].rearrange("p (t k) -> p t k", t=T)
                    link(v.tensor_reduce(mx[q][:], sc, AX.X, ALU.max))
                    v.tensor_tensor(pd[q][:], sc, over(mx[q][:], SK), ALU.subtract).then_inc(sd_ready[q], 1)

                def cross_probs(q, i):
                    dve.wait_ge(p_ready[q], at(pr, q, 2, i + 1))
                    link(v.tensor_reduce(sm[q][:], pp[q][:], AX.X, ALU.add))
                    link(v.reciprocal(ri[q][:], sm[q][:]))

                def cross_values(q, i):
                    dve.wait_ge(y_done[q], at(pr, q, N_Y, (Y_X0, Y_X1)[i] + 1))
                    for t in range(T):
                        l = v.scalar_tensor_tensor(xr[q][:, t, :], y_bank[q][:, t * P:(t + 1) * P], ri[q][:, t:t + 1],
                                                   xr[q][:, t, :], ALU.mult, ALU.add)
                    link(l)
                    moments(q, xr[q])
                    normalize(q, xh[q], xr[q], (4, 7)[i]).then_inc(ln_ready[q], 1)

                def router(q):
                    dve.wait_ge(lg_done[q], pr + 1)
                    link(v.tensor_tensor(lg[:], (ps_x, ps_k)[q][:, 0:T * E0].rearrange("p (t e) -> p t e", t=T),
                                         e0bg[:].unsqueeze(1).to_broadcast([P, T, E0]), ALU.add))

                    def argmax(src, top, onehot):
                        link(v.tensor_reduce(top[:], src[:], AX.X, ALU.max))
                        link(v.tensor_tensor(key[:], src[:], over(top[:], E0), ALU.is_equal))
                        link(v.scalar_tensor_tensor(key[:], key[:], -64.0, iota8[:], ALU.mult, ALU.add))
                        link(v.tensor_reduce(mn[q][:], key[:], AX.X, ALU.min))
                        link(v.tensor_tensor(onehot[:], key[:], over(mn[q][:], E0), ALU.is_equal))

                    argmax(lg, m1[q], oh1[q])
                    link(v.scalar_tensor_tensor(l2[:], oh1[q][:], -BIG, lg[:], ALU.mult, ALU.add))
                    argmax(l2, m2[q], oh2[q])
                    v.tensor_tensor(mn[q][:], m2[q][:], m1[q][:], ALU.subtract).then_inc(md_ready[q], 1)

                def router_weights(q):
                    dve.wait_ge(me_ready[q], pr + 1)
                    link(v.tensor_scalar(m1[q][:], g2[q][:], 1.0, None, ALU.add))
                    link(v.reciprocal(g1[:], m1[q][:]))
                    link(v.tensor_tensor(g2[q][:], g2[q][:], g1[:], ALU.mult))
                    v.tensor_tensor(comb[q][:], oh1[q][:], over(g1[:], E0), ALU.mult)
                    link(v.tensor_tensor(key[:], oh2[q][:], over(g2[q][:], E0), ALU.mult))
                    v.tensor_tensor(comb[q][:], comb[q][:], key[:], ALU.add).then_inc(comb_ready[q], 1)
                    dve.wait_ge(comb_ready[q], pr + 1)

                def experts(q):
                    def hidden(e):
                        for c in (1, 3):
                            dve.wait_ge(up_done, at(pr, EXPERTS + q, 2 * FC * E0, q * FC * E0 + FC * e + c + 1))
                            if e >= 2:
                                dve.wait_ge(y_done[q], at(pr, q, N_Y, Y_E + e - 1))
                            r = R_EB1 + FC * e + c
                            v.tensor_scalar(big[:, 4 * (e % 2) + c, :], four[(c + 2) % 4][:], cols[:, r:r + 1], 0.0,
                                            ALU.add, ALU.max).then_inc(up_dve, 1)

                    hidden(0)
                    dve.wait_ge(y_done[q], at(pr, q, N_Y, Y_BIAS + 1))
                    link(v.tensor_tensor(xr[q][:], tiles(ps_q), xr[q][:], ALU.add))
                    for e in range(E0):
                        if e + 1 < E0:
                            hidden(e + 1)
                        dve.wait_ge(y_done[q], at(pr, q, N_Y, Y_E + e + 1))
                        for t in range(T):
                            l = v.scalar_tensor_tensor(xr[q][:, t, :], (ps_k, ps_q)[e % 2][:, t * P:(t + 1) * P],
                                                       comb[q][:, t, e:e + 1], xr[q][:, t, :], ALU.mult, ALU.add)
                        l.then_inc(acc_done, 1)
                        dve.wait_ge(acc_done, at(pr, EXPERTS + q, 2 * E0, q * E0 + e + 1))

                    moments(q, xr[q])
                    normalize(q, xh[q], xr[q], 5).then_inc(ln_ready[q], 1)

                def ssm_conv(q):
                    for c in range(IC):
                        dve.wait_ge(xp_ready, at(pr, STATE_SPACE + q, 2 * IC, q * IC + c + 1))
                        r = R_CB + c
                        link(v.tensor_scalar(cv[q][:, c, :], xpad[q][:, c, KC - 1:KC - 1 + S], convw[:, c, KC - 1:KC],
                                             cols[:, r:r + 1], ALU.mult, ALU.add))
                        for k in range(KC - 1):
                            l = v.scalar_tensor_tensor(cv[q][:, c, :], xpad[q][:, c, k:k + S], convw[:, c, k:k + 1],
                                                       cv[q][:, c, :], ALU.mult, ALU.add)
                            if k < KC - 2:
                                link(l)
                        l.then_inc(cv_ready, 1)

                def ssm_proj(q):
                    dve.wait_ge(ssm_done[q], pr + 1)
                    link(v.tensor_copy(ssm[q][:].rearrange("p t n -> p (t n)"), (ps_x, ps_s[1])[q][:, 0:T * NX]))
                    x0, neg, u, w, ln, d, z, dl = ssm[q][:, :, 0], *(sp_x[q][:, i, :] for i in (0, 2, 3, 4, 5, 6, 7))
                    link(v.tensor_scalar(neg, x0, -1.0, None, ALU.mult))
                    v.tensor_tensor(sp_x[q][:, 1, :], x0, neg, ALU.min).then_inc(abs_ready[q], 1)
                    dve.wait_ge(u_ready[q], pr + 1)
                    v.tensor_scalar(w, u, 1.0, None, ALU.add).then_inc(w_ready[q], 1)
                    dve.wait_ge(w_ready[q], pr + 1)
                    link(v.tensor_scalar(d, w, -1.0, None, ALU.add))
                    link(v.tensor_scalar(z, d, 0.0, None, ALU.is_equal))
                    link(v.tensor_tensor(d, d, z, ALU.add))
                    link(v.reciprocal(neg, d))
                    link(v.tensor_tensor(neg, neg, u, ALU.mult))
                    link(v.tensor_tensor(z, z, u, ALU.mult))
                    dve.wait_ge(l_ready[q], pr + 1)
                    link(v.tensor_tensor(ln, ln, neg, ALU.mult))
                    link(v.tensor_tensor(ln, ln, z, ALU.add))
                    link(v.scalar_tensor_tensor(dl, x0, 0.0, ln, ALU.max, ALU.add))
                    link(v.tensor_scalar(dl, dl, 1.0 / S, None, ALU.mult))
                    v.tensor_tensor(dB[q][:], ssm[q][:, :, 1:1 + NS], over(dl, NS), ALU.mult).then_inc(db_ready[q], 1)

                def ssm_out(q):
                    for c in range(IC):
                        dve.wait_ge(yt_done[q], at(pr, q, IC, c + 1))
                        r = R_DS + c
                        link(v.scalar_tensor_tensor(yT[q][:, c, :], xc[q][:, c, :], cols[:, r:r + 1], ps_o[c][:],
                                                    ALU.mult, ALU.add))
                        v.tensor_tensor(yT[q][:, c, :], yT[q][:, c, :], sz[q][:, c, :], ALU.mult).then_inc(yt_ready[q], 1)

                def ssm_down(q):
                    dve.wait_ge(y_done[q], at(pr, q, N_Y, Y_SSM + 1))
                    link(v.tensor_tensor(xr[q][:], tiles(y_bank[q]), xr[q][:], ALU.add))
                    moments(q, xr[q])
                    normalize(q, xh[q], xr[q], 6).then_inc(ln_ready[q], 1)

                def kept(q):
                    dve.wait_ge(x_kept[q], pr + 1)
                for q in range(2):
                    ln_in(q)
                for q in range(2):
                    attention(q)
                for q in range(2):
                    ffn(q)
                for q in range(2):
                    cross_scores(q, 0)
                for q in range(2):
                    cross_probs(q, 0)
                for q in range(2):
                    cross_values(q, 0)
                for q in range(2):
                    router(q)
                for q in range(2):
                    router_weights(q)
                for q in range(2):
                    experts(q)
                for q in range(2):
                    ssm_conv(q)
                for q in range(2):
                    ssm_proj(q)
                for q in range(2):
                    ssm_out(q)
                for q in range(2):
                    ssm_down(q)
                for q in range(2):
                    cross_scores(q, 1)
                for q in range(2):
                    cross_probs(q, 1)
                for q in range(2):
                    cross_values(q, 1)
                for q in range(2):
                    kept(q)
                assert n[0] == VEC_STEPS, n

        ph.close()
        NG = T
        NT = B * T
        TG = B
        CAP = -(-2 * (B * S // NG) // E1)
        CS = CAP + CAP % 2
        RS = P // 2
        NK = E1 // 2
        EQ = 8
        NQ = E1 // EQ
        WS = E1 * CS
        NF = 7
        assert CS <= RS and EQ * CS <= 512 and NG % 2 == 0

        hd = sb("hd", [P, 2 * NK * FF])
        disp = sb("disp", [P, 2, TG, E1 * RS])
        dT = sb("dT", [P, NK, TG * P])
        xT = sb("xT", [P, E1, 2, RS])
        ht = sb("ht", [P, 2, TG, FF])
        iw = sb("iw", [P, WS])
        cT24 = sb("cT24", [E1, 2, TG * P])
        b124 = sb("b124", [E1, FF])
        b224 = sb("b224", [E1, D])
        lnw = sb("lnw", [P, D])
        lnb = sb("lnb", [P, D])
        wg24 = sb("wg24", [P, E1])
        comb24 = sb("comb24", [P, NT, E1])
        combp = sb("combp", [P, TG, 2, E1])
        sl = sb("sl", [P, NT, 2])
        slp = sb("slp", [P, TG, 2, 2])
        ft = sb("ft", [P, NT, NF], BF16)
        ftp = sb("ftp", [P, TG, 2, NF], BF16)
        lwp = sb("lwp", [P, 2 * FC])
        lbp = sb("lbp", [P, 2 * FC])
        ecol = sb("ecol", [P, NK])
        gf = sb("gf", [P, 2, NK, NF])
        gs = sb("gs", [P, 2, NK])
        gt = sb("gt", [P, 2, NK])
        gate = sb("gate", [P, 2, NK])
        tri = sb("tri", [P, P], BF16)
        one = sb("one", [P, P], BF16)
        st6 = sb("st6", [P, TG, 6])
        mv6 = sb("mv6", [P, TG, 2])
        ve6 = sb("ve6", [P, TG])
        rs6 = sb("rs6", [P, TG])
        ob = sb("ob", [P, 2, TG, D])
        sv = sb("sv", [P, 16, NT])

        hd2 = hd[:].rearrange("p (g k f) -> p g k f", g=2, k=NK)
        d2T = hd[:].rearrange("p (c e g s) -> p c e g s", c=FC, e=E1, g=2)
        xT_f = xT[:].rearrange("p e g s -> p (e g s)")
        hn = xT_f[:, 0:2 * FF].rearrange("p (n f) -> p n f", n=2)
        yv = xT_f.rearrange("p (g k d) -> p g k d", g=2, k=NK)
        assert NK * D == E1 * RS
        ug_parts = [dT[:].rearrange("p k t -> p (k t)")[:, i * TG * 2 * D:(i + 1) * TG * 2 * D]
                    .rearrange("p (b g d) -> p b g d", b=TG, g=2) for i in range(2)]
        ht_parts = [ht[:], dT[:, 0:2 * TG, :].rearrange("p (i b) f -> p i b f", i=2)]
        NR_HD = 2
        hd_parts = sb("hd_parts", [P, NR_HD, 2, FF])
        dT_last = hd[:, 0:NK * TG * P].rearrange("p (k t) -> p k t", k=NK)
        dTs = (dT[:], dT[:], dT[:], dT_last)
        uT = hd[:, 0:NT * P]
        TW = NT * E1
        tmp = [hd[:, NT * P + i * TW:NT * P + (i + 1) * TW].rearrange("p (t e) -> p t e", e=E1) for i in range(6)]
        h0 = NT * P + 6 * TW
        i24 = hd[:, h0:h0 + TW].rearrange("p (t e) -> p t e", e=E1)
        i24i = hd[:, h0 + TW:h0 + 2 * TW].bitcast(I32).rearrange("p (t e) -> p t e", e=E1)
        eci = hd[:, h0 + 2 * TW:h0 + 2 * TW + NK].bitcast(I32)
        h1 = h0 + 3 * TW + WS
        oh1b, oh2b = (hd[:, h1 + i * TW:h1 + i * TW + TW // 2].bitcast(BF16).rearrange("p (t e) -> p t e", e=E1)
                      for i in range(2))
        iwi = hd[:, h0 + 3 * TW:h0 + 3 * TW + WS].bitcast(I32)

        def slots(gi, b):
            return disp[:, gi, b, :].rearrange("p (e s) -> p e s", s=RS)[:, :, 0:CS]

        names = ("w2_in k2 uT_done uT_act uT_dve lg2_done lgd_ready lge_ready oh_ready loc_done pair_act pair_dve "
                 "disp_ready cT_done cT_act cT_dve pA evA_act evA_dve gt_done gate_ready dt_done dt_act dt_dve "
                 "c1_done hv_ready hr_ready ht_ready pads_ready w_used o_ready r2_ready vec2 hi_ready lo_ready hd_used "
                 "xpads_ready hn_ready hh_ready yg_ready ug_ready").split()
        (w2_in, k2, uT_done, uT_act, uT_dve, lg2_done, lgd_ready, lge_ready, oh_ready, loc_done, pair_act, pair_dve,
         disp_ready, cT_done, cT_act, cT_dve, pA, evA_act, evA_dve, gt_done, gate_ready, dt_done, dt_act, dt_dve,
         c1_done, hv_ready, hr_ready, ht_ready, pads_ready, w_used, o_ready, r2_ready, vec2, hi_ready, lo_ready,
         hd_used, xpads_ready, hn_ready, hh_ready, yg_ready, ug_ready) = [
             sem(x) for x in names]
        NP2 = NG // 2
        assert NP2 == 2
        U_DISP, U_UP = 0, 2 * NQ
        U_D2 = U_UP + E1
        U_DOWN = U_D2 + 2 * FC * NQ
        U_ALL = U_DOWN + E1 // 4
        VEC2_PRE, VEC2_STEPS = 55, 54
        N_C1 = 2 * TG + 2
        assert U_UP % 2 == 0 and U_D2 % 2 == 0 and U_DOWN % 2 == 0 and U_ALL % 2 == 0
        bg = lambda x: x.rearrange("p (b g) d -> p b g d", g=NG)

        block2 = ctx.enter_context(nc.Block())

        @block2.sync
        def _(sp):
            for dst, src in ((b124[:], a["L1_ffn_b1"]), (b224[:], a["L1_ffn_b2"]), (wg24[:], a["L1_ffn_Wg"]),
                             (lnw[:], a["L1_ffn_ln_out_w"].rearrange("(o d) -> o d", o=1).to_broadcast([P, D])),
                             (lnb[:], a["L1_ffn_ln_out_b"].rearrange("(o d) -> o d", o=1).to_broadcast([P, D]))):
                sp.dma_start(dst, src).then_inc(w2_in, 16)
            NC = E1 // NR
            w_dram = (a["L1_ffn_W1"].rearrange("e d f -> d e f"),
                      a["L1_ffn_W2"].rearrange("e (c p) d -> p e c d", p=P))

            def load(kind, e, k):
                if kind == 0:
                    src, dst = w_dram[0][:, bass.ds(e, 1), :], ring[:, k:k + 1, :]
                else:
                    src = w_dram[1][:, bass.ds(e, 1), :, :].rearrange("p e c d -> p (e c) d")
                    dst = ring[:, k, :].rearrange("p (c d) -> p c d", c=FC)
                sp.dma_start(dst, src).then_inc(slot_in[k], 16)

            for pair in range(NP2):
                for kind in range(2):
                    used, base = ((pA, pair * U_DOWN + U_UP), (w_used, pair * E1))[kind]
                    if pair or kind:
                        before, last = ((w_used, pair * E1), (pA, pair * U_DOWN + U_UP + E1))[kind]
                        for k in range(NR):
                            sp.wait_ge(before, last - NR + k + 1)
                            load(kind, k, k)
                    with sp.Fori(1, NC) as c:
                        for k in range(NR):
                            sp.wait_ge(used, c * NR + (base - NR + k + 1))
                            load(kind, c * NR + k, k)

        @block2.gpsimd
        def _(pool):
            g_ = nc.gpsimd
            g_.iota(iwi, pattern=[[1, WS]], base=0, channel_multiplier=0)
            g_.iota(eci[0:RS], pattern=[[2, NK]], base=0, channel_multiplier=0).then_inc(k2, 1)
            pool.wait_ge(k2, 1)
            g_.iota(eci[RS:P], pattern=[[2, NK]], base=1, channel_multiplier=0).then_inc(k2, 1)
            pool.wait_ge(k2, 2)
            g_.iota(i24i, pattern=[[0, NT], [1, E1]], base=0, channel_multiplier=0)
            g_.memset(one[:], 1.0)
            g_.memset(tri[:], 1.0).then_inc(k2, 1)
            pool.wait_ge(k2, 3)
            g_.affine_select(out=tri[:], in_=tri[:], compare_op=ALU.is_gt, fill=0.0, base=0, pattern=[[1, P]],
                             channel_multiplier=-1)
            for gi in range(2):
                for b in range(TG):
                    l = g_.memset(disp[:, gi, b, :].rearrange("p (e s) -> p e s", s=RS)[:, :, CS:RS], 0.0)
            l.then_inc(k2, 1)
            with pool.Fori(0, NP2) as pg:
                g_.memset(xT[:, :, :, CS:RS], 0.0).then_inc(xpads_ready, 1)
                for m in range(2 * TG):
                    pool.wait_ge(hv_ready, pg * (2 * TG + 2) + (m + 1))
                    g_.tensor_tensor(rs6[:, 0:1], ve6[:, 0:1], half[:, 0:1], ALU.pow).then_inc(hr_ready, 1)
                pool.wait_ge(c1_done, pg * N_C1 + 2 * TG)
                g_.tensor_tensor(tick[:, 1:2], half[:, 0:1], half[:, 0:1], ALU.add)
                g_.memset(d2T[:, :, :, :, CS:RS].rearrange("p c e g s -> p (c e g) s"), 0.0).then_inc(pads_ready, 1)
                for q in range(E1 // 4):
                    pool.wait_ge((evA_act, evA_dve)[q % 2], pg * (U_ALL // 2) + (U_DOWN + q) // 2 + 1)
                    y = yv[:, :, 2 * q:2 * q + 2, :]
                    g_.tensor_tensor(y, y, gate[:, :, 2 * q:2 * q + 2].unsqueeze(3).to_broadcast([P, 2, 2, D]),
                                     ALU.mult).then_inc(yg_ready, 1)
                for m in range(2):
                    pool.wait_ge(hv_ready, pg * (2 * TG + 2) + (2 * TG + m + 1))
                    g_.tensor_tensor(rs6[:], ve6[:], half[:, 0:TG], ALU.pow).then_inc(hr_ready, 1)

        @block2.tensor
        def _(pe):
            mm, tr = nc.tensor.matmul, nc.tensor.transpose
            for i in range(NT // 4):
                for j in range(4):
                    l = tr(bank[i][:, j * P:(j + 1) * P], u_all[:, 4 * i + j, :], ident[:])
                l.then_inc(uT_done, 1)
            pe.wait_ge(w2_in, 16 * 5)
            pe.wait_ge(uT_act, 2)
            pe.wait_ge(uT_dve, 2)
            for t in range(NT):
                l = mm(bank[4][:, t * E1:(t + 1) * E1], uT[:, t * P:(t + 1) * P], wg24[:], start=True, stop=True)
            l.then_inc(lg2_done, 1)
            pe.wait_ge(oh_ready, 1)
            pe.wait_ge(k2, 4)
            W = NG * E1
            flat = [x.rearrange("p t e -> p (t e)") for x in (oh1b, oh2b)]
            for which in range(2):
                for t in range(TG):
                    terms = [(tri, which, t)] + [(one, which, p) for p in range(t)]
                    terms += [(one, 0, p) for p in range(TG)] if which else []
                    for i, (m, c, p) in enumerate(terms):
                        l = mm(bank[5 + which][:, t * W:(t + 1) * W], m[:], flat[c][:, p * W:(p + 1) * W],
                               start=(i == 0), stop=(i == len(terms) - 1))
            l.then_inc(loc_done, 1)
            pe.wait_ge(r2_ready, 1)

            with pe.Fori(0, NP2) as pg:
                def bank_a(u):
                    if u >= 4:
                        pe.wait_ge((evA_act, evA_dve)[u % 2], pg * (U_ALL // 2) + (u - 4) // 2 + 1)
                    return bank[u % 4]

                pe.wait_ge(pair_act, pg + 1)
                pe.wait_ge(pair_dve, pg + 1)
                for gi in range(2):
                    for b in range(TG):
                        l = tr(bank[4 + gi][0:E1, b * P:(b + 1) * P], combp[:, b, gi, :], ident[:])
                    l.then_inc(cT_done, 1)
                pe.wait_ge(ug_ready, pg + 1)
                for gi in range(2):
                    pe.wait_ge(disp_ready, pg * 2 + gi + 1)
                    for q in range(NQ):
                        ps = bank_a(U_DISP + gi * NQ + q)
                        for b in range(TG):
                            for i in range(2):
                                l = mm(ps[:, 0:EQ * CS], ug_parts[i][:, b, gi, :].bitcast(F32R),
                                       slots(gi, b)[:, q * EQ:(q + 1) * EQ, :].bitcast(F32R),
                                       start=(b == 0 and i == 0), stop=(b == TG - 1 and i == 1))
                        l.then_inc(pA, 1)
                for gi in range(2):
                    for k in range(NK):
                        for b in range(TG):
                            hot = disp[:, gi, b, :].bitcast(BF16).rearrange("p (s h) -> p s h", h=2)[:, :, 1]
                            l = mm(bank[6 + gi][:, k * NF:(k + 1) * NF], hot[:, k * P:(k + 1) * P], ftp[:, b, gi, :],
                                   start=(b == 0), stop=(b == TG - 1))
                    l.then_inc(gt_done, 1)

                def slots_to_rows(i, gi, k):
                    m = i * NK + k
                    if m < 2:
                        pe.wait_ge((cT_act, cT_dve)[k], pg + 1)
                    else:
                        pe.wait_ge((dt_act, dt_dve)[k % 2], pg * 2 * NK + (m - 2) // 2 + 1)
                    for b in range(TG):
                        l = tr(bank[4 + k % 2][:, b * P:(b + 1) * P], disp[:, gi, b, k * P:(k + 1) * P], ident[:])
                    l.then_inc(dt_done, 1)

                pe.wait_ge(evA_act, pg * (U_ALL // 2) + U_UP // 2)
                pe.wait_ge(evA_dve, pg * (U_ALL // 2) + U_UP // 2)
                pe.wait_ge(xpads_ready, pg + 1)
                for e in range(E1):
                    ps = bank_a(U_UP + e)
                    pe.wait_ge(slot_in[e % NR], (pg * (2 * E1 // NR) + (e // NR + 1)) * 16)
                    mm(ps[:], xT[:, e, :, :], ring[:, e % NR, :], start=True, stop=True).then_inc(pA, 1)
                    if e % 2:
                        slots_to_rows(0, 0, e // 2)

                for gi in range(2):
                    acc = bank[4 * gi:4 * gi + 4]
                    if gi == 0:
                        pe.wait_ge(evA_act, pg * (U_ALL // 2) + U_D2 // 2)
                        pe.wait_ge(evA_dve, pg * (U_ALL // 2) + U_D2 // 2)
                        pe.wait_ge(gate_ready, pg + 1)
                    else:
                        pe.wait_ge(dt_act, pg * 2 * NK + NK)
                        pe.wait_ge(dt_dve, pg * 2 * NK + NK)
                    for b in range(TG):
                        mm(acc[b][:], cT24[:, gi, b * P:(b + 1) * P], b124[:], start=True, stop=False)
                    for k in range(NK):
                        m = gi * NK + k
                        pe.wait_ge((dt_act, dt_dve)[k % 2], pg * 2 * NK + m // 2 + 1)
                        pe.wait_ge(hi_ready, pg * 2 * NK + m + 1)
                        pe.wait_ge(lo_ready, pg * 2 * NK + m + 1)
                        for b in range(TG):
                            for i in range(2):
                                l = mm(acc[b][:], dT[:, k, b * P:(b + 1) * P].bitcast(F32R),
                                       hd_parts[:, m % NR_HD, i, :].bitcast(F32R),
                                       start=False, stop=(k == NK - 1 and i == 1))
                            if k == NK - 1:
                                l.then_inc(c1_done, 1)
                        if k < NK - 1:
                            l.then_inc(hd_used, 1)
                        if gi == 0 and k:
                            slots_to_rows(1, 1, k - 1)
                    if gi == 0:
                        slots_to_rows(1, 1, NK - 1)
                for gi in range(2):
                    pe.wait_ge(ht_ready, pg * 2 * TG + (gi + 1) * TG)
                    for c in range(FC):
                        for q in range(NQ):
                            ps = bank_a(U_D2 + (gi * FC + c) * NQ + q)
                            for b in range(TG):
                                for i in range(2):
                                    l = mm(ps[:, 0:EQ * CS], ht_parts[gi][:, i, b, c * P:(c + 1) * P].bitcast(F32R),
                                           slots(gi, b)[:, q * EQ:(q + 1) * EQ, :].bitcast(F32R),
                                           start=(b == 0 and i == 0), stop=(b == TG - 1 and i == 1))
                            l.then_inc(pA, 1)
                pe.wait_ge(evA_act, pg * (U_ALL // 2) + U_DOWN // 2)
                pe.wait_ge(evA_dve, pg * (U_ALL // 2) + U_DOWN // 2)
                pe.wait_ge(pads_ready, pg + 1)
                for e in range(E1):
                    if e % 4 == 0:
                        ps = bank_a(U_DOWN + e // 4)
                    pe.wait_ge(slot_in[e % NR], (pg * (2 * E1 // NR) + (E1 // NR + e // NR + 1)) * 16)
                    for c in range(FC):
                        l = mm(ps[:, (e % 4) * P:(e % 4 + 1) * P], d2T[:, c, e, :, :],
                               ring[:, e % NR, c * P:(c + 1) * P], start=(c == 0), stop=(c == FC - 1))
                    l.then_inc(w_used, 1)
                    if e % 2:
                        slots_to_rows(2, 0, e // 2)
                pe.wait_ge(yg_ready, pg * (E1 // 4) + E1 // 4)
                for gi in range(2):
                    pe.wait_ge(dt_act, pg * 2 * NK + (3 + gi) * NK // 2)
                    pe.wait_ge(dt_dve, pg * 2 * NK + (3 + gi) * NK // 2)
                    ps = bank[6 + gi]
                    for b in range(TG):
                        o = ps[:, b * P:(b + 1) * P]
                        mm(o, cT24[:, gi, b * P:(b + 1) * P], b224[:], start=True, stop=False)
                        for k in range(NK):
                            l = mm(o, dTs[2 + gi][:, k, b * P:(b + 1) * P], yv[:, gi, k, :], start=False,
                                   stop=(k == NK - 1))
                        if b == TG - 1:
                            l.then_inc(c1_done, 1)
                        if gi == 0:
                            for k in range(b * NK // TG, (b + 1) * NK // TG):
                                slots_to_rows(3, 1, k)

        @block2.scalar
        def _(act):
            af = nc.scalar.activation
            for i in (0, 2):
                act.wait_ge(uT_done, i + 1)
                af(uT[:, i * 512:(i + 1) * 512], bank[i][:], ACT.Copy).then_inc(uT_act, 1)
            act.wait_ge(lgd_ready, 1)
            af(tmp[4], tmp[4], ACT.Exp).then_inc(out_done, 1)
            af(sv[:, 4, :], sv[:, 4, :], ACT.Exp).then_inc(lge_ready, 1)

            with act.Fori(0, NP2) as pg:
                two = bass.ds(pg * 2, 2)

                def taken(u):
                    act.wait_ge(pA, pg * U_DOWN + u + 1)
                    return bank[u % 4]

                act.wait_ge(r2_ready, 1)
                af(ug_parts[0].bitcast(F32R), bg(u_all[:])[:, :, two, :], ACT.Copy).then_inc(pair_act, 1)
                act.wait_ge(cT_done, pg * 2 + 1)
                af(cT24[:, 0, :], bank[4][0:E1, :], ACT.Copy).then_inc(cT_act, 1)
                for n in range(0, 2 * NQ, 2):
                    gi, q = n // NQ, n % NQ
                    af(xT[:, q * EQ:(q + 1) * EQ, gi, 0:CS],
                       taken(U_DISP + n)[:, 0:EQ * CS].rearrange("p (e s) -> p e s", s=CS), ACT.Copy).then_inc(evA_act, 1)

                def rows(i, gi, k):
                    act.wait_ge(dt_done, pg * 4 * NK + (i * NK + k + 1))
                    dst = dTs[i][:, k, :]
                    af(dst.bitcast(F32R) if i < 3 else dst, bank[4][:], ACT.Copy).then_inc(dt_act, 1)

                for e in range(0, E1, 2):
                    ps = taken(U_UP + e)
                    af(hd2[0:RS, 0, e // 2, :], ps[0:RS, :], ACT.Copy)
                    af(hd2[0:RS, 1, e // 2, :], ps[RS:P, :], ACT.Copy).then_inc(evA_act, 1)
                    if e % 4 == 0:
                        rows(0, 0, e // 2)

                def split(gi, k):
                    m = gi * NK + k
                    if m >= NR_HD:
                        g, kk = divmod(m - NR_HD, NK)
                        if kk == NK - 1:
                            act.wait_ge(c1_done, pg * N_C1 + TG)
                        else:
                            act.wait_ge(hd_used, pg * 2 * (NK - 1) + (g * (NK - 1) + kk + 1))
                    af(hd_parts[:, m % NR_HD, 0, :].bitcast(F32R), hd2[:, gi, k, :], ACT.Copy,
                       scale=gate[:, gi, k:k + 1]).then_inc(hi_ready, 1)

                def hidden_part(m):
                    gi, b = m // TG, m % TG
                    act.wait_ge(hn_ready, pg * 2 * TG + m + 1)
                    af(ht_parts[gi][:, 0, b, :].bitcast(F32R), hn[:, m % 2, :], ACT.Copy).then_inc(hh_ready, 1)

                act.wait_ge(out_done, pg * 32 + 1)
                act.wait_ge(gate_ready, pg + 1)
                act.wait_ge(evA_dve, pg * (U_ALL // 2) + U_D2 // 2)
                for k in range(NK):
                    split(0, k)
                    if k >= 2 and k % 2 == 0:
                        rows(1, 1, k - 2)
                rows(1, 1, NK - 2)
                for k in range(NK):
                    split(1, k)
                    if k % 2 == 0 and 2 <= k < 2 + 2 * TG:
                        hidden_part((k - 2) // 2)
                act.wait_ge(c1_done, pg * N_C1 + 2 * TG)
                for n in range(0, 2 * FC * NQ, 2):
                    gi, c, q = n // (FC * NQ), n // NQ % FC, n % NQ
                    r = gi * FC + c
                    af(d2T[:, c, q * EQ:(q + 1) * EQ, gi, 0:CS],
                       taken(U_D2 + n)[:, 0:EQ * CS].rearrange("p (e s) -> p e s", s=CS), ACT.Relu,
                       scale=lwp[:, r:r + 1], bias=lbp[:, r:r + 1]).then_inc(evA_act, 1)
                    if n < 2 * TG:
                        hidden_part(TG + n // 2)

                def outputs_of_experts(q):
                    act.wait_ge(w_used, pg * E1 + 4 * q + 4)
                    ps = bank[(U_DOWN + q) % 4][:].rearrange("p (k two d) -> p k two d", two=2, d=D)
                    for gi in range(2):
                        for par in range(2):
                            l = af(yv[par * RS:(par + 1) * RS, gi, 2 * q:2 * q + 2, :],
                                   ps[gi * RS:(gi + 1) * RS, :, par, :], ACT.Copy)
                    l.then_inc(evA_act, 1)

                for q in range(E1 // 4):
                    rows(2, 0, 2 * q)
                    if q % 2 == 0:
                        outputs_of_experts(q)
                for k in range(0, NK, 2):
                    rows(3, 1, k)
                for gi in range(2):
                    act.wait_ge(o_ready, pg * 2 + gi + 1)
                    dst = out.rearrange("b (g p) d -> p b g d", p=P)[:, :, bass.ds(pg * 2 + gi, 1), :]\
                        .rearrange("p b g d -> p (b g) d")
                    act.dma_start(dst, ob[:, gi, :, :]).then_inc(out_done, 16)
            act.wait_ge(out_done, 16 * NG + 1)

        @block2.vector
        def _(dve):
            v = nc.vector
            n = [0]

            def link0(ins):
                n[0] += 1
                ins.then_inc(vec2, 1)
                dve.wait_ge(vec2, n[0])

            def wide(col, w=E1):
                return col.unsqueeze(2).to_broadcast([P, NT, w])

            for i in (1, 3):
                dve.wait_ge(uT_done, i + 1)
                v.tensor_copy(uT[:, i * 512:(i + 1) * 512], bank[i][:]).then_inc(uT_dve, 1)
            lgs, key, oh1, oh2, ex, l2 = tmp
            m1, m2, n1, n2, e21, ssum, p1, p2, pos1, pos2, k1, k2_, den, t0, t1, t2 = (sv[:, i, :] for i in range(16))
            dve.wait_ge(k2, 4)
            v.tensor_copy(iw[:], iwi)
            v.tensor_copy(ecol[:], eci)
            link0(v.tensor_copy(i24, i24i))
            dve.wait_ge(lg2_done, 1)
            link0(v.tensor_copy(lgs, bank[4][:, 0:NT * E1].rearrange("p (t e) -> p t e", e=E1)))

            def argmax(src, top, idx, onehot):
                link0(v.tensor_reduce(top, src, AX.X, ALU.max))
                link0(v.tensor_tensor(key, src, wide(top), ALU.is_equal))
                link0(v.scalar_tensor_tensor(key, key, -64.0, i24, ALU.mult, ALU.add))
                link0(v.tensor_reduce(idx, key, AX.X, ALU.min))
                link0(v.tensor_tensor(onehot, key, wide(idx), ALU.is_equal))

            argmax(lgs, m1, n1, oh1)
            link0(v.scalar_tensor_tensor(l2, oh1, -BIG, lgs, ALU.mult, ALU.add))
            argmax(l2, m2, n2, oh2)
            v.tensor_copy(oh1b, oh1)
            v.tensor_copy(oh2b, oh2).then_inc(oh_ready, 1)
            v.tensor_tensor(ex, lgs, wide(m1), ALU.subtract)
            v.tensor_tensor(e21, m2, m1, ALU.subtract).then_inc(lgd_ready, 1)
            dve.wait_ge(lge_ready, 1)
            link0(v.tensor_reduce(ssum, ex, AX.X, ALU.add))
            link0(v.reciprocal(p1, ssum))
            link0(v.tensor_tensor(p2, p1, e21, ALU.mult))
            dve.wait_ge(loc_done, 1)
            for i, (oh, pos, kp, pr, idx) in enumerate(((oh1, pos1, k1, p1, n1), (oh2, pos2, k2_, p2, n2))):
                loc = bank[5 + i][:, 0:NT * E1].rearrange("p (t e) -> p t e", e=E1)
                link0(v.tensor_tensor(key, loc, oh, ALU.mult))
                link0(v.tensor_reduce(pos, key, AX.X, ALU.add))
                link0(v.tensor_scalar(kp, pos, float(CAP), None, ALU.is_lt))
                link0(v.scalar_tensor_tensor(t0, idx, float(CS), pos, ALU.mult, ALU.add))
                link0(v.tensor_scalar(t0, t0, float(64 * CS + 1), None, ALU.add))
                link0(v.tensor_tensor(t0, t0, kp, ALU.mult))
                v.tensor_scalar(sl[:, :, i], t0, -1.0, None, ALU.add)
                link0(v.tensor_tensor(pr, pr, kp, ALU.mult))
            link0(v.tensor_tensor(den, p1, p2, ALU.add))
            link0(v.tensor_scalar(den, den, 1e-9, None, ALU.max))
            link0(v.reciprocal(t0, den))
            v.tensor_tensor(p1, p1, t0, ALU.mult)
            link0(v.tensor_tensor(p2, p2, t0, ALU.mult))
            v.tensor_tensor(comb24[:], oh1, wide(p1), ALU.mult)
            link0(v.tensor_tensor(key, oh2, wide(p2), ALU.mult))
            v.tensor_tensor(comb24[:], comb24[:], key, ALU.add)
            link0(v.tensor_scalar(ft[:, :, 6], n1, 64.0, None, ALU.add))
            for i, g in enumerate((p1, p2)):
                link0(v.tensor_copy(ft[:, :, 3 * i], g))
                link0(v.tensor_tensor(t1, g, ft[:, :, 3 * i], ALU.subtract))
                link0(v.tensor_copy(ft[:, :, 3 * i + 1], t1))
                link0(v.tensor_tensor(t2, t1, ft[:, :, 3 * i + 1], ALU.subtract))
                link0(v.tensor_copy(ft[:, :, 3 * i + 2], t2))
            v.tensor_copy(t1, t2).then_inc(r2_ready, 1)
            dve.wait_ge(r2_ready, 1)

            def one_hot(gi, b, link):
                hot, ids = slots(gi, b).bitcast(F32R), iw[:].rearrange("p (e s) -> p e s", s=CS)
                link(v.tensor_scalar(hot, ids, slp[:, b, gi, 0:1], None, ALU.is_equal))
                return v.scalar_tensor_tensor(hot, ids, slp[:, b, gi, 1:2], slots(gi, b), ALU.is_equal, ALU.add)

            link0(v.tensor_copy(slp[:], bg(sl[:])[:, :, 0:2, :]))
            for gi in range(2):
                for b in range(TG):
                    l = one_hot(gi, b, link0)
                l.then_inc(disp_ready, 1)
            assert n[0] == VEC2_PRE, n
            n[0] = 0

            with dve.Fori(0, NP2) as pg:
                two = bass.ds(pg * 2, 2)

                def link(ins):
                    n[0] += 1
                    ins.then_inc(vec2, 1)
                    dve.wait_ge(vec2, pg * VEC2_STEPS + VEC2_PRE + n[0])

                def taken(u):
                    dve.wait_ge(pA, pg * U_DOWN + u + 1)
                    return bank[u % 4]

                def over(col, w):
                    return col.unsqueeze(2).to_broadcast([P, TG, w])

                def rows(i, gi, k):
                    dve.wait_ge(dt_done, pg * 4 * NK + (i * NK + k + 1))
                    dst = dTs[i][:, k, :]
                    v.tensor_copy(dst.bitcast(F32R) if i < 3 else dst, bank[5][:]).then_inc(dt_dve, 1)

                v.tensor_copy(ftp[:], bg(ft[:])[:, :, two, :])
                v.tensor_copy(lwp[:], cols[:, R_LW:R_LW + NG * FC].rearrange("p (g c) -> p g c", c=FC)[:, two, :]
                              .rearrange("p g c -> p (g c)"))
                v.tensor_copy(lbp[:], cols[:, R_LB:R_LB + NG * FC].rearrange("p (g c) -> p g c", c=FC)[:, two, :]
                              .rearrange("p g c -> p (g c)"))
                v.tensor_copy(combp[:], bg(comb24[:])[:, :, two, :]).then_inc(pair_dve, 1)
                dve.wait_ge(pair_dve, pg + 1)
                dve.wait_ge(pair_act, pg + 1)
                v.tensor_tensor(ug_parts[1].bitcast(F32R), bg(u_all[:])[:, :, two, :], ug_parts[0], ALU.subtract)\
                    .then_inc(ug_ready, 1)
                dve.wait_ge(cT_done, pg * 2 + 2)
                v.tensor_copy(cT24[:, 1, :], bank[5][0:E1, :]).then_inc(cT_dve, 1)
                for m in range(1, 2 * NQ, 2):
                    gi, q = m // NQ, m % NQ
                    v.tensor_copy(xT[:, q * EQ:(q + 1) * EQ, gi, 0:CS],
                                  taken(U_DISP + m)[:, 0:EQ * CS].rearrange("p (e s) -> p e s", s=CS))\
                        .then_inc(evA_dve, 1)
                dve.wait_ge(gt_done, pg * 2 + 2)
                for gi in range(2):
                    l = v.tensor_copy(gf[:, gi].rearrange("p k f -> p (k f)"), bank[6 + gi][:, 0:NK * NF])
                link(l)
                for gi in range(2):
                    v.tensor_tensor(gt[:, gi, :], gf[:, gi, :, 6], ecol[:], ALU.is_equal)
                    v.tensor_reduce(gate[:, gi, :], gf[:, gi, :, 0:3], AX.X, ALU.add)
                    l = v.tensor_reduce(gs[:, gi, :], gf[:, gi, :, 3:6], AX.X, ALU.add)
                link(l)
                link(v.tensor_tensor(gate[:], gate[:], gt[:], ALU.mult))
                link(v.tensor_tensor(gt[:], gs[:], gt[:], ALU.mult))
                link(v.tensor_tensor(gs[:], gs[:], gt[:], ALU.subtract))
                v.tensor_tensor(gate[:], gate[:], gs[:], ALU.add).then_inc(gate_ready, 1)
                for e in range(1, E1, 2):
                    ps = taken(U_UP + e)
                    v.tensor_copy(hd2[RS:P, 0, e // 2, :], ps[0:RS, :])
                    v.tensor_copy(hd2[RS:P, 1, e // 2, :], ps[RS:P, :]).then_inc(evA_dve, 1)
                    if e % 4 == 3:
                        rows(0, 0, e // 2)

                def moments(src, m):
                    for b, x in enumerate(src):
                        l = v.bn_stats(st6[:, b, :], x)
                    link(l)
                    v.tensor_copy(tick[:, 0:1], half[:, 0:1])
                    for b in range(len(src)):
                        l = v.bn_aggr(mv6[:, b, :], st6[:, b, :])
                    link(l)
                    k = len(src)
                    v.tensor_scalar(ve6[:, 0:k], mv6[:, 0:k, 1], 1e-6, None, ALU.add).then_inc(hv_ready, 1)
                    dve.wait_ge(hr_ready, pg * N_C1 + m + 1)

                def split(gi, k):
                    m = gi * NK + k
                    dve.wait_ge(hi_ready, pg * 2 * NK + m + 1)
                    v.scalar_tensor_tensor(hd_parts[:, m % NR_HD, 1, :].bitcast(F32R), hd2[:, gi, k, :],
                                           gate[:, gi, k:k + 1], hd_parts[:, m % NR_HD, 0, :],
                                           ALU.mult, ALU.subtract).then_inc(lo_ready, 1)

                def hidden_norm(m):
                    gi, b = m // TG, m % TG
                    dve.wait_ge(c1_done, pg * N_C1 + m + 1)
                    moments([bank[m][:]], m)
                    v.tensor_scalar(hn[:, m % 2, :], bank[m][:], mv6[:, 0, 0:1], rs6[:, 0:1], ALU.subtract, ALU.mult)\
                        .then_inc(hn_ready, 1)
                    dve.wait_ge(hh_ready, pg * 2 * TG + m + 1)
                    v.tensor_tensor(ht_parts[gi][:, 1, b, :].bitcast(F32R), hn[:, m % 2, :], ht_parts[gi][:, 0, b, :],
                                    ALU.subtract).then_inc(ht_ready, 1)

                dve.wait_ge(evA_act, pg * (U_ALL // 2) + U_D2 // 2)
                for k in range(NK):
                    split(0, k)
                    if k >= 3 and k % 2:
                        rows(1, 1, k - 2)
                rows(1, 1, NK - 1)
                for k in range(NK):
                    split(1, k)
                    if k % 2 == 0 and 2 <= k < 2 + 2 * TG:
                        hidden_norm((k - 2) // 2)
                for m in range(1, 2 * FC * NQ, 2):
                    gi, c, q = m // (FC * NQ), m // NQ % FC, m % NQ
                    r = gi * FC + c
                    o = d2T[:, c, q * EQ:(q + 1) * EQ, gi, 0:CS]
                    link(v.tensor_scalar(o, taken(U_D2 + m)[:, 0:EQ * CS].rearrange("p (e s) -> p e s", s=CS),
                                         lwp[:, r:r + 1], lbp[:, r:r + 1], ALU.mult, ALU.add))
                    v.tensor_scalar(o, o, 0.0, None, ALU.max).then_inc(evA_dve, 1)
                    if m < 2 * TG:
                        hidden_norm(TG + m // 2)
                for q in range(E1 // 4):
                    rows(2, 0, 2 * q + 1)
                    if q % 2 == 0:
                        continue
                    dve.wait_ge(w_used, pg * E1 + 4 * q + 4)
                    ps = bank[(U_DOWN + q) % 4][:].rearrange("p (k two d) -> p k two d", two=2, d=D)
                    for gi in range(2):
                        for par in range(2):
                            l = v.tensor_copy(yv[par * RS:(par + 1) * RS, gi, 2 * q:2 * q + 2, :],
                                              ps[gi * RS:(gi + 1) * RS, :, par, :])
                    l.then_inc(evA_dve, 1)
                link(v.tensor_copy(slp[:], bg(sl[:])[:, :, bass.ds(pg * (-2) + 2, 2), :]))
                for k in range(1, NK, 2):
                    rows(3, 1, k)
                    if k // 2 < TG:
                        l = one_hot(0, k // 2, link)
                    if k // 2 == TG - 1:
                        l.then_inc(disp_ready, 1)
                for gi in range(2):
                    if gi:
                        for b in range(TG):
                            l = one_hot(1, b, link)
                        l.then_inc(disp_ready, 1)
                    dve.wait_ge(c1_done, pg * N_C1 + 2 * TG + gi + 1)
                    zb = ob[:, gi]
                    link(v.tensor_tensor(zb, bank[6 + gi][:].rearrange("p (b d) -> p b d", b=TG), bg(u_all[:])[:, :, bass.ds(pg * 2 + gi, 1), :]
                                         .rearrange("p b g d -> p (b g) d"),
                                         ALU.add))
                    moments([zb[:, b, :] for b in range(TG)], 2 * TG + gi)
                    for b in range(TG):
                        l = v.tensor_scalar(zb[:, b, :], zb[:, b, :], mv6[:, b, 0:1], rs6[:, b:b + 1],
                                            ALU.subtract, ALU.mult)
                    link(l)
                    link(v.tensor_tensor(zb, zb, lnw[:].unsqueeze(1).to_broadcast([P, TG, D]), ALU.mult))
                    link(v.tensor_tensor(zb, zb, lnb[:].unsqueeze(1).to_broadcast([P, TG, D]), ALU.add))
                    v.tensor_tensor(ob[:, gi, :, :], zb, bg(x_all[:])[:, :, bass.ds(pg * 2 + gi, 1), :]
                                    .rearrange("p b g d -> p (b g) d"), ALU.add).then_inc(o_ready, 1)
                assert n[0] == VEC2_STEPS, n


def kernel(**inputs):
    import numpy as _np
    import concourse.bacc as _bacc
    from concourse import mybir as _mybir
    from concourse.bass_utils import run_bass_kernel_spmd as _run

    nc = _bacc.Bacc("TRN2", target_bir_lowering=False, num_devices=1)
    arrays, args = {}, {}
    for name, value in inputs.items():
        v = _np.ascontiguousarray(value)
        arrays[f"in_{name}_dram"] = v
        args[name] = nc.dram_tensor(f"in_{name}_dram", v.shape, _mybir.dt.from_np(v.dtype), kind="ExternalInput").ap()
    x = inputs["x"]
    out = nc.dram_tensor("out_0_dram", x.shape, _mybir.dt.from_np(_np.dtype("float32")), kind="ExternalOutput").ap()
    decoder(nc, args, out)
    r = _run(nc, [arrays], core_ids=[0])
    return r.results[0]["out_0_dram"]
```
